# Optimizing a Trainium2 kernel written in Bass

```python
import numpy as np
import jax
import jax.numpy as jnp

def _softmax(x, axis=-1):
    return jax.nn.softmax(x, axis=axis)

def _gelu(x):
    return jax.nn.gelu(x, approximate=True)

def _silu(x):
    return jax.nn.silu(x)

def _sigmoid(x):
    return jax.nn.sigmoid(x)

def _layernorm(x, axis=-1, eps=1e-05):
    m = jnp.mean(x, axis=axis, keepdims=True)
    v = jnp.var(x, axis=axis, keepdims=True)
    return (x - m) / jnp.sqrt(v + eps)

def _scatter_add(tgt, idx, src, axis=0):
    return tgt.at[idx].add(src)

def _segment_sum(src, seg, n):
    return jax.ops.segment_sum(src, seg, n)
kernel_name = 'mk_adj_ffn_d2_adj_r2_9bbc05'

def setup_inputs(seed: int=0):
    np.random.seed(seed)
    _w = jnp.asarray

    def _rec_inputs():
        import jax
        import jax.numpy as jnp
        _gk = jax.random.key(seed)
        x = -0.0005207 + 1.001 * jax.random.normal(jax.random.fold_in(_gk, 1), (4096, 128), jnp.float32)
        _a = jax.random.bernoulli(jax.random.fold_in(_gk, 2), 0.000488281, (4096, 4096))
        _a = jnp.logical_or(_a, jnp.eye(4096, dtype=bool))
        _af = _a.astype(jnp.float32)
        _af = _af * jax.random.uniform(jax.random.fold_in(_gk, 3), (4096, 4096), jnp.float32, 0.05, 1)
        adj = _af
        return (x, adj)
    x, adj = _rec_inputs()

    def _L0_gnn_setup():
        import jax, jax.numpy as jnp
        import numpy as np
        N = 4096
        F_IN = 128
        F_OUT = 128
        key = jax.random.key(seed)
        k1, k2, k3 = jax.random.split(key, 3)
        H = jax.random.normal(k1, (N, F_IN), dtype=jnp.float32)
        A_tilde = jax.random.uniform(k2, (N, N), dtype=jnp.float32)
        limit = np.sqrt(6.0 / (F_IN + F_OUT)).astype(np.float32)
        W = jax.random.uniform(k3, (F_IN, F_OUT), dtype=jnp.float32, minval=-limit, maxval=limit)
        return {'H': H, 'A_tilde': A_tilde, 'W': W}
    _L0_gnn_all = _L0_gnn_setup()
    _L0_gnn_in = {k: v for k, v in _L0_gnn_all.items() if k in ('W',)}
    del _L0_gnn_all

    def _L0_ffn_setup():
        import jax, jax.numpy as jnp
        import numpy as np
        H, P, G, NS, K = (8, 64, 64, 64, 3)
        D_INNER = H * P
        CONV_DIM = D_INNER + 2 * NS
        D_IN_PROJ = 2 * D_INNER + 2 * NS + 2 * H

        def _hydra(u, in_w, conv_w, conv_b, dt_bias, A_log, Dp, fcD_w, norm_w, out_w):
            Bt, L, _ = u.shape
            zxbcdt = u @ in_w.T
            z = zxbcdt[..., :D_INNER]
            xBC = zxbcdt[..., D_INNER:D_INNER + CONV_DIM]
            dt = zxbcdt[..., -2 * H:]
            dt = jnp.concatenate([dt[..., :H], jnp.flip(dt[..., H:], axis=1)], axis=0)
            dt = jax.nn.softplus(dt + dt_bias)
            xp = jnp.pad(xBC, ((0, 0), (K - 1, 0), (0, 0)))
            xBC = sum((xp[:, k:k + L, :] * conv_w[:, k] for k in range(K))) + conv_b
            xBC = jax.nn.silu(xBC)
            x = xBC[..., :D_INNER]
            Bm = xBC[..., D_INNER:D_INNER + NS]
            Cm = xBC[..., D_INNER + NS:]
            x_og = x
            x2 = jnp.concatenate([x, jnp.flip(x, 1)], 0).reshape(2 * Bt, L, H, P)
            B2 = jnp.concatenate([Bm, jnp.flip(Bm, 1)], 0)
            C2 = jnp.concatenate([Cm, jnp.flip(Cm, 1)], 0)
            dA = jnp.exp(dt * -jnp.exp(A_log))
            dBx = jnp.einsum('blh,bln,blhp->blhpn', dt, B2, x2)

            def step(h, inp):
                dA_t, dBx_t, C_t = inp
                h = h * dA_t[:, :, None, None] + dBx_t
                return (h, jnp.einsum('bhpn,bn->bhp', h, C_t))
            h0 = jnp.zeros((2 * Bt, H, P, NS), u.dtype)
            _, ys = jax.lax.scan(step, h0, (dA.transpose(1, 0, 2), dBx.transpose(1, 0, 2, 3, 4), C2.transpose(1, 0, 2)))
            y = ys.transpose(1, 0, 2, 3).reshape(2 * Bt, L, D_INNER)
            y_fw, y_bw = (y[:Bt], jnp.flip(y[Bt:], 1))
            y = jnp.pad(y_fw[:, :-1], ((0, 0), (1, 0), (0, 0))) + jnp.pad(y_bw[:, 1:], ((0, 0), (0, 1), (0, 0)))
            y = y + x_og * jnp.repeat(x_og @ fcD_w.T + Dp, P, axis=-1)
            yg = y * jax.nn.silu(z)
            yg = yg * jax.lax.rsqrt(jnp.mean(jnp.square(yg), -1, keepdims=True) + 1e-05) * norm_w
            return yg @ out_w.T
        key = jax.random.key(seed)
        ks = jax.random.split(key, 10)
        dim, Bsz, N = (128, 4, 4096)
        s = 0.02
        return {'x': jax.random.normal(ks[0], (Bsz, N, dim), jnp.float32), 'W_fx': jax.random.normal(ks[1], (D_INNER, dim), jnp.float32) * s, 'b_fx': jnp.zeros((D_INNER,), jnp.float32), 'W_x': jax.random.normal(ks[2], (D_INNER, dim), jnp.float32) * s, 'b_x': jnp.zeros((D_INNER,), jnp.float32), 'W_slice': jax.random.normal(ks[3], (G, P), jnp.float32) * s, 'b_slice': jnp.zeros((G,), jnp.float32), 'temperature': jnp.full((1, H, 1, 1), 0.5, jnp.float32), 'hy_in_w': jax.random.normal(ks[4], (D_IN_PROJ, D_INNER), jnp.float32) * s, 'hy_conv_w': jax.random.normal(ks[5], (CONV_DIM, K), jnp.float32) * s, 'hy_conv_b': jnp.zeros((CONV_DIM,), jnp.float32), 'hy_dt_bias': jnp.log(jnp.expm1(jnp.full((H,), 0.01, jnp.float32))), 'hy_A_log': jnp.log(jnp.linspace(1.0, 16.0, H)).astype(jnp.float32), 'hy_D': jnp.ones((H,), jnp.float32), 'hy_fcD_w': jax.random.normal(ks[6], (H, D_INNER), jnp.float32) * s, 'hy_norm_w': jnp.ones((D_INNER,), jnp.float32), 'hy_out_w': jax.random.normal(ks[7], (D_INNER, D_INNER), jnp.float32) * s, 'out_w': jax.random.normal(ks[8], (dim, D_INNER), jnp.float32) * s, 'out_b': jnp.zeros((dim,), jnp.float32)}
    _L0_ffn_all = _L0_ffn_setup()
    _L0_ffn_in = {k: v for k, v in _L0_ffn_all.items() if k in ('W_fx', 'b_fx', 'W_x', 'b_x', 'W_slice', 'b_slice', 'temperature', 'hy_in_w', 'hy_conv_w', 'hy_conv_b', 'hy_dt_bias', 'hy_A_log', 'hy_D', 'hy_fcD_w', 'hy_norm_w', 'hy_out_w', 'out_w', 'out_b')}
    del _L0_ffn_all

    def _L1_gnn_setup():
        import jax, jax.numpy as jnp
        import numpy as np
        N = 4096
        F = 128
        NEG_INF = -9000000000000000.0
        ALPHA = 0.2
        THRESH = 1e-06
        key = jax.random.key(seed)
        k1, k2, k3, k4 = jax.random.split(key, 4)
        x = jax.random.normal(k1, (N, F), jnp.float32)
        h0 = jax.random.normal(k2, (N, F), jnp.float32)
        limit = float(np.sqrt(6.0 / (2 * F + 1)) * 1.414)
        a = jax.random.uniform(k3, (2 * F, 1), jnp.float32, -limit, limit)
        temp = jnp.zeros((5,), jnp.float32)
        adj = jax.random.bernoulli(k4, 0.005, (N, N)).astype(jnp.float32)
        adj = jnp.maximum(adj, jnp.eye(N, dtype=jnp.float32))
        return {'x': x, 'h0': h0, 'a': a, 'temp': temp, 'adj': adj, 'l': 1}
    _L1_gnn_all = _L1_gnn_setup()
    _L1_gnn_in = {k: v for k, v in _L1_gnn_all.items() if k in ('h0', 'a', 'temp')}
    del _L1_gnn_all

    def _L1_ffn_setup():
        import jax, jax.numpy as jnp
        import numpy as np
        B, T, IN_DIM = (64, 128, 128)
        HID, OUT_DIM = (256, 128)
        N_LAYERS, N_EXPERTS, N_SHARED = (2, 16, 1)
        key = jax.random.key(seed)
        ks = jax.random.split(key, 10)
        s = 0.02
        x = jax.random.normal(ks[0], (B, T, IN_DIM), dtype=jnp.float32)
        route_id = jax.random.randint(ks[1], (B,), 0, N_EXPERTS)
        Wi = jax.random.normal(ks[2], (HID, IN_DIM), dtype=jnp.float32) * s
        bi = jnp.zeros((HID,), dtype=jnp.float32)
        Wr = jax.random.normal(ks[3], (N_LAYERS, N_EXPERTS, HID, HID), dtype=jnp.float32) * s
        br = jax.random.normal(ks[4], (N_LAYERS, N_EXPERTS, HID), dtype=jnp.float32) * s
        Ws = jax.random.normal(ks[5], (N_LAYERS, N_SHARED, HID, HID), dtype=jnp.float32) * s
        bs = jax.random.normal(ks[6], (N_LAYERS, N_SHARED, HID), dtype=jnp.float32) * s
        Wo = jax.random.normal(ks[7], (OUT_DIM, HID), dtype=jnp.float32) * s
        bo = jnp.zeros((OUT_DIM,), dtype=jnp.float32)
        return {'x': x, 'route_id': route_id, 'Wi': Wi, 'bi': bi, 'Wr': Wr, 'br': br, 'Ws': Ws, 'bs': bs, 'Wo': Wo, 'bo': bo}
    _L1_ffn_all = _L1_ffn_setup()
    _L1_ffn_in = {k: v for k, v in _L1_ffn_all.items() if k in ('route_id', 'Wi', 'bi', 'Wr', 'br', 'Ws', 'bs', 'Wo', 'bo')}
    del _L1_ffn_all
    return {'x': x, 'adj': adj, 'L0_gnn_W': _L0_gnn_in['W'], 'L0_ffn_W_fx': _L0_ffn_in['W_fx'], 'L0_ffn_b_fx': _L0_ffn_in['b_fx'], 'L0_ffn_W_x': _L0_ffn_in['W_x'], 'L0_ffn_b_x': _L0_ffn_in['b_x'], 'L0_ffn_W_slice': _L0_ffn_in['W_slice'], 'L0_ffn_b_slice': _L0_ffn_in['b_slice'], 'L0_ffn_temperature': _L0_ffn_in['temperature'], 'L0_ffn_hy_in_w': _L0_ffn_in['hy_in_w'], 'L0_ffn_hy_conv_w': _L0_ffn_in['hy_conv_w'], 'L0_ffn_hy_conv_b': _L0_ffn_in['hy_conv_b'], 'L0_ffn_hy_dt_bias': _L0_ffn_in['hy_dt_bias'], 'L0_ffn_hy_A_log': _L0_ffn_in['hy_A_log'], 'L0_ffn_hy_D': _L0_ffn_in['hy_D'], 'L0_ffn_hy_fcD_w': _L0_ffn_in['hy_fcD_w'], 'L0_ffn_hy_norm_w': _L0_ffn_in['hy_norm_w'], 'L0_ffn_hy_out_w': _L0_ffn_in['hy_out_w'], 'L0_ffn_out_w': _L0_ffn_in['out_w'], 'L0_ffn_out_b': _L0_ffn_in['out_b'], 'L1_gnn_h0': _L1_gnn_in['h0'], 'L1_gnn_a': _L1_gnn_in['a'], 'L1_gnn_temp': _L1_gnn_in['temp'], 'L1_ffn_route_id': _L1_ffn_in['route_id'], 'L1_ffn_Wi': _L1_ffn_in['Wi'], 'L1_ffn_bi': _L1_ffn_in['bi'], 'L1_ffn_Wr': _L1_ffn_in['Wr'], 'L1_ffn_br': _L1_ffn_in['br'], 'L1_ffn_Ws': _L1_ffn_in['Ws'], 'L1_ffn_bs': _L1_ffn_in['bs'], 'L1_ffn_Wo': _L1_ffn_in['Wo'], 'L1_ffn_bo': _L1_ffn_in['bo']}

def reference(x, adj, L0_gnn_W, L0_ffn_W_fx, L0_ffn_b_fx, L0_ffn_W_x, L0_ffn_b_x, L0_ffn_W_slice, L0_ffn_b_slice, L0_ffn_temperature, L0_ffn_hy_in_w, L0_ffn_hy_conv_w, L0_ffn_hy_conv_b, L0_ffn_hy_dt_bias, L0_ffn_hy_A_log, L0_ffn_hy_D, L0_ffn_hy_fcD_w, L0_ffn_hy_norm_w, L0_ffn_hy_out_w, L0_ffn_out_w, L0_ffn_out_b, L1_gnn_h0, L1_gnn_a, L1_gnn_temp, L1_ffn_route_id, L1_ffn_Wi, L1_ffn_bi, L1_ffn_Wr, L1_ffn_br, L1_ffn_Ws, L1_ffn_bs, L1_ffn_Wo, L1_ffn_bo):
    import jax
    import jax.numpy as jnp

    def _L0_gnn_ref(H, A_tilde, W):
        import jax, jax.numpy as jnp
        import numpy as np
        N = 4096
        F_IN = 128
        F_OUT = 128
        d_inv_sqrt = jnp.sum(A_tilde, axis=1) ** (-0.5)
        A_norm = d_inv_sqrt[:, None] * A_tilde * d_inv_sqrt[None, :]
        H_next = A_norm @ H @ W
        return jax.nn.relu(H_next)

    def _L0_ffn_ref(x, W_fx, b_fx, W_x, b_x, W_slice, b_slice, temperature, hy_in_w, hy_conv_w, hy_conv_b, hy_dt_bias, hy_A_log, hy_D, hy_fcD_w, hy_norm_w, hy_out_w, out_w, out_b):
        import jax, jax.numpy as jnp
        import numpy as np
        H, P, G, NS, K = (8, 64, 64, 64, 3)
        D_INNER = H * P
        CONV_DIM = D_INNER + 2 * NS
        D_IN_PROJ = 2 * D_INNER + 2 * NS + 2 * H

        def _hydra(u, in_w, conv_w, conv_b, dt_bias, A_log, Dp, fcD_w, norm_w, out_w):
            Bt, L, _ = u.shape
            zxbcdt = u @ in_w.T
            z = zxbcdt[..., :D_INNER]
            xBC = zxbcdt[..., D_INNER:D_INNER + CONV_DIM]
            dt = zxbcdt[..., -2 * H:]
            dt = jnp.concatenate([dt[..., :H], jnp.flip(dt[..., H:], axis=1)], axis=0)
            dt = jax.nn.softplus(dt + dt_bias)
            xp = jnp.pad(xBC, ((0, 0), (K - 1, 0), (0, 0)))
            xBC = sum((xp[:, k:k + L, :] * conv_w[:, k] for k in range(K))) + conv_b
            xBC = jax.nn.silu(xBC)
            x = xBC[..., :D_INNER]
            Bm = xBC[..., D_INNER:D_INNER + NS]
            Cm = xBC[..., D_INNER + NS:]
            x_og = x
            x2 = jnp.concatenate([x, jnp.flip(x, 1)], 0).reshape(2 * Bt, L, H, P)
            B2 = jnp.concatenate([Bm, jnp.flip(Bm, 1)], 0)
            C2 = jnp.concatenate([Cm, jnp.flip(Cm, 1)], 0)
            dA = jnp.exp(dt * -jnp.exp(A_log))
            dBx = jnp.einsum('blh,bln,blhp->blhpn', dt, B2, x2)

            def step(h, inp):
                dA_t, dBx_t, C_t = inp
                h = h * dA_t[:, :, None, None] + dBx_t
                return (h, jnp.einsum('bhpn,bn->bhp', h, C_t))
            h0 = jnp.zeros((2 * Bt, H, P, NS), u.dtype)
            _, ys = jax.lax.scan(step, h0, (dA.transpose(1, 0, 2), dBx.transpose(1, 0, 2, 3, 4), C2.transpose(1, 0, 2)))
            y = ys.transpose(1, 0, 2, 3).reshape(2 * Bt, L, D_INNER)
            y_fw, y_bw = (y[:Bt], jnp.flip(y[Bt:], 1))
            y = jnp.pad(y_fw[:, :-1], ((0, 0), (1, 0), (0, 0))) + jnp.pad(y_bw[:, 1:], ((0, 0), (0, 1), (0, 0)))
            y = y + x_og * jnp.repeat(x_og @ fcD_w.T + Dp, P, axis=-1)
            yg = y * jax.nn.silu(z)
            yg = yg * jax.lax.rsqrt(jnp.mean(jnp.square(yg), -1, keepdims=True) + 1e-05) * norm_w
            return yg @ out_w.T
        B, N, _ = x.shape
        fx = (x @ W_fx.T + b_fx).reshape(B, N, H, P).transpose(0, 2, 1, 3)
        xm = (x @ W_x.T + b_x).reshape(B, N, H, P).transpose(0, 2, 1, 3)
        temp = jnp.maximum(temperature, 1e-06)
        sw = jax.nn.softmax((xm @ W_slice.T + b_slice) / temp, axis=-1)
        snorm = sw.sum(2)
        st = jnp.einsum('bhnc,bhng->bhgc', fx, sw) / (snorm + 1e-05)[..., None]
        st = st.transpose(0, 2, 1, 3).reshape(B, G, D_INNER)
        ot = _hydra(st, hy_in_w, hy_conv_w, hy_conv_b, hy_dt_bias, hy_A_log, hy_D, hy_fcD_w, hy_norm_w, hy_out_w)
        ot = ot.reshape(B, G, H, P).transpose(0, 2, 1, 3)
        out = jnp.einsum('bhgc,bhng->bhnc', ot, sw).transpose(0, 2, 1, 3).reshape(B, N, D_INNER)
        return out @ out_w.T + out_b

    def _L1_gnn_ref(x, h0, a, temp, adj, l):
        import jax, jax.numpy as jnp
        import numpy as np
        N = 4096
        F = 128
        NEG_INF = -9000000000000000.0
        ALPHA = 0.2
        THRESH = 1e-06
        Fdim = x.shape[1]
        feat_1 = x @ a[:Fdim]
        feat_2 = x @ a[Fdim:]
        e = jax.nn.leaky_relu(feat_1 + feat_2.T, ALPHA)
        att = jnp.where(adj > 0, e, NEG_INF)
        U = jax.nn.softmax(att, axis=1)
        P = 0.5 * U
        prop_u = U @ x
        rowsum = jnp.sum(U * P, axis=1)
        coe = jax.nn.sigmoid(temp)
        xi = x * rowsum[:, None]
        feat_odd = prop_u - xi
        feat_even = x + prop_u - xi
        feat = coe[2] * feat_odd + (1.0 - coe[2]) * feat_even
        sgn = jnp.sign(feat)
        mod = jnp.abs(feat)
        mod = jnp.where(mod > THRESH, mod - THRESH, 0.0)
        feat = mod * sgn
        pu = U @ feat
        feat_odd2 = feat - coe[3] * pu
        feat_even2 = pu + feat_odd2 * rowsum[:, None]
        feat_odd2 = coe[0] * feat_odd2 + (1.0 - coe[0]) * h0
        out = coe[1] * feat_even2 + (1.0 - coe[1]) * feat_odd2
        return out

    def _L1_ffn_ref(x, route_id, Wi, bi, Wr, br, Ws, bs, Wo, bo):
        import jax, jax.numpy as jnp
        import numpy as np
        B, T, IN_DIM = (64, 128, 128)
        HID, OUT_DIM = (256, 128)
        N_LAYERS, N_EXPERTS, N_SHARED = (2, 16, 1)
        flat = x.reshape(-1, x.shape[-1])
        n_tok = flat.shape[0]
        route = jnp.repeat(route_id, n_tok // route_id.shape[0])
        h = jax.nn.relu(flat @ Wi.T + bi)
        n_layers, n_experts = (Wr.shape[0], Wr.shape[1])
        for l in range(n_layers):
            shared = (jnp.einsum('nd,shd->snh', h, Ws[l]) + bs[l][:, None, :]).mean(axis=0)
            routed = jnp.zeros_like(h)
            for e in range(n_experts):
                ye = h @ Wr[l, e].T + br[l, e]
                routed = routed + jnp.where((route == e)[:, None], ye, 0.0)
            h = jax.nn.relu(shared + routed + h)
        out = h @ Wo.T + bo
        return out.reshape(*x.shape[:-1], out.shape[-1])
    x = x + _L0_gnn_ref(_layernorm(x, axis=-1), adj, L0_gnn_W)
    x = x + _L0_ffn_ref(_layernorm(x, axis=-1)[None], L0_ffn_W_fx, L0_ffn_b_fx, L0_ffn_W_x, L0_ffn_b_x, L0_ffn_W_slice, L0_ffn_b_slice, L0_ffn_temperature, L0_ffn_hy_in_w, L0_ffn_hy_conv_w, L0_ffn_hy_conv_b, L0_ffn_hy_dt_bias, L0_ffn_hy_A_log, L0_ffn_hy_D, L0_ffn_hy_fcD_w, L0_ffn_hy_norm_w, L0_ffn_hy_out_w, L0_ffn_out_w, L0_ffn_out_b)[0]
    x = x + _L1_gnn_ref(_layernorm(x, axis=-1), L1_gnn_h0, L1_gnn_a, L1_gnn_temp, adj, 1)
    x = x + _L1_ffn_ref(_layernorm(x, axis=-1)[None], L1_ffn_route_id, L1_ffn_Wi, L1_ffn_bi, L1_ffn_Wr, L1_ffn_br, L1_ffn_Ws, L1_ffn_bs, L1_ffn_Wo, L1_ffn_bo)[0]
    return x

_drawn_inputs = setup_inputs


def setup_inputs(seed=0):
    import zlib

    import numpy as np

    out = dict(_drawn_inputs(seed))
    spreads = {'L0_ffn_b_fx': (0.0, 0.1),
     'L0_ffn_b_x': (0.0, 0.8),
     'L0_ffn_b_slice': (0.0, 0.8),
     'L0_ffn_temperature': (0.5, 0.6),
     'L0_ffn_hy_conv_b': (0.0, 0.1),
     'L0_ffn_hy_dt_bias': (-4.600166320800781, 0.6),
     'L0_ffn_hy_D': (1.0, 0.6),
     'L0_ffn_hy_norm_w': (1.0, 0.6),
     'L0_ffn_out_b': (0.0, 0.1),
     'L1_gnn_temp': (0.0, 0.8),
     'L1_ffn_bi': (0.0, 0.673),
     'L1_ffn_bo': (0.0, 0.1)}
    factors = {'L0_ffn_W_fx': 8.0,
     'L0_ffn_W_x': 8.0,
     'L0_ffn_W_slice': 8.0,
     'L0_ffn_hy_conv_w': 8.0,
     'L0_ffn_hy_A_log': 64.0,
     'L0_ffn_hy_fcD_w': 24.266,
     'L1_ffn_Wr': 4.847,
     'L1_ffn_br': 8.0,
     'L1_ffn_Ws': 5.059,
     'L1_ffn_bs': 8.0}
    for name, (base, spread) in spreads.items():
        noise = np.random.default_rng([zlib.crc32(name.encode()), seed]).standard_normal(out[name].shape)
        drawn = base * np.exp(spread * noise) if base else spread * noise
        out[name] = jnp.asarray(drawn.astype(out[name].dtype))
    for name, factor in factors.items():
        out[name] = (out[name] * factor).astype(out[name].dtype)
    return out
```

```python
from contextlib import ExitStack

import numpy as np

import concourse.bass as bass
from concourse import mybir

F32 = mybir.dt.float32
BF16 = mybir.dt.bfloat16
U8 = mybir.dt.uint8
I32 = mybir.dt.int32
ALU = mybir.AluOpType
ACT = mybir.ActivationFunctionType
AX = mybir.AxisListType
RMAX = bass.bass_isa.ReduceOp.max

P = 128
N = 4096
F = 128
NT = N // P
BANK = 512
NB = N // BANK
HALF = N // 2
EPS = 1e-5
H = 8
G = 64
HG = H * G
DI = 512
NS = 64
NPROJ = 2 * DI + 2 * NS + 2 * H
CH = 6
NE = 16
HID = 256
KH = HID // P
THRESH = 1e-6
SLOPE = 0.2
A_LOG_CAP = 69.0


class Chain:

    def __init__(self, eng, sem):
        self.eng, self.sem, self.n, self.turn, self.start = eng, sem, 0, 0, 0

    def __call__(self, ins):
        self.n += 1
        ins.then_inc(self.sem, 1)
        self.eng.wait_ge(self.sem, self.turn + self.n)

    def enter(self, i, per):
        self.start, self.per, self.turn = self.n, per, i * per

    def leave(self, turns):
        assert self.n - self.start == self.per, (self.n - self.start, self.per)
        self.n, self.turn = self.start + self.per * turns, 0


class Core:

    def __init__(self, nc, args, out):
        self.nc, self.args, self.out = nc, args, out

    def stage(self, name):
        return Stage(self, name)


class Stage:

    def __init__(self, core, name):
        self.core, self.nc, self.name, self.ctx = core, core.nc, name, ExitStack()

    def __enter__(self):
        return self

    def __exit__(self, *a):
        return self.ctx.__exit__(*a)

    def sb(self, name, shape, dt=F32):
        return self.ctx.enter_context(self.nc.sbuf_tensor(f"{self.name}_{name}", shape, dt))

    def ps(self, name, shape, dt=F32):
        return self.ctx.enter_context(self.nc.psum_tensor(f"{self.name}_{name}", shape, dt))

    def sem(self, name):
        return self.core.ctx.enter_context(self.nc.semaphore(f"{self.name}_{name}"))

    def block(self):
        return self.nc.Block()


def natural(ap):
    return ap.rearrange("(t p) f -> p t f", p=P)


def bcast_mid(ap, n):
    return ap.unsqueeze(2).to_broadcast([ap.shape[0], ap.shape[1], n])


def bcast_row(ap, n):
    return ap.unsqueeze(1).to_broadcast([ap.shape[0], n, ap.shape[1]])


def column(ap, t):
    return ap[:, bass.ds(t, 1), :].rearrange("p a f -> p (a f)")


def token_statistics(nc, dve, own, x, stats, mean, var_eps):
    with dve.Fori(0, NT // 4) as i:
        own.enter(i, 1)
        for b in range(4):
            t = 4 * i + b
            last = nc.vector.bn_stats(stats[:, bass.ds(t, 1), :], x[:, bass.ds(t, 1), :])
        own(last)
        own.leave(NT // 4)
    mean_e, m2_e, mean_o, m2_o = (stats[:, :, k] for k in (1, 2, 4, 5))
    own(nc.vector.tensor_tensor(mean[:, :], mean_e, mean_o, ALU.add))
    nc.vector.tensor_tensor(mean_o, mean_e, mean_o, ALU.subtract)
    own(nc.vector.tensor_tensor(m2_e, m2_e, m2_o, ALU.add))
    nc.vector.tensor_scalar(mean[:, :], mean[:, :], 0.5, None, ALU.mult)
    own(nc.vector.scalar_tensor_tensor(out=m2_o, in0=mean_o, scalar=F / 4, in1=mean_o, op0=ALU.mult, op1=ALU.mult))
    own(nc.vector.tensor_tensor(m2_e, m2_e, m2_o, ALU.add))
    own(nc.vector.tensor_scalar(var_eps[:, :], m2_e, 1.0 / F, EPS, ALU.mult, ALU.add))


def constants(core):
    nc = core.nc
    with core.stage("const") as st:
        made = st.sem("made")
        x_in = st.sem("x_in")
        with st.block() as block:
            @block.gpsimd
            def _(pool):
                nc.gpsimd.memset(core.ident[:, :], 0.0).then_inc(made, 1)
                pool.wait_ge(made, 1)
                nc.gpsimd.affine_select(out=core.ident[:, :], in_=core.ident[:, :], compare_op=ALU.not_equal,
                                        fill=1.0, base=0, pattern=[[-1, P]], channel_multiplier=1).then_inc(made, 1)
                nc.gpsimd.memset(core.select[:, :], 1.0).then_inc(made, 1)
                pool.wait_ge(made, 3)
                nc.gpsimd.affine_select(out=core.select[:, :], in_=core.select[:, :], compare_op=ALU.is_ge,
                                        fill=0.0, base=0, pattern=[[-3, 4]], channel_multiplier=1).then_inc(made, 1)
                pool.wait_ge(made, 4)
                nc.gpsimd.affine_select(out=core.select[:, :], in_=core.select[:, :], compare_op=ALU.is_ge,
                                        fill=0.0, base=2, pattern=[[3, 4]], channel_multiplier=-1).then_inc(made, 1)

            @block.vector
            def _(dve):
                nc.vector.memset(core.ones[:, :], 1.0)
                nc.vector.memset(core.ones_b[:, :], 1.0)
                nc.vector.memset(core.zeros_b[:, :], 0.0)

            @block.sync
            def _(sp):
                sp.dma_start(core.x[:, :, :], natural(core.args["x"])).then_inc(x_in, 16)
                sp.wait_ge(x_in, 16)


def gcn_propagate(core, st):
    nc = core.nc
    adj_rows = core.args["adj"].rearrange("(t p) (h c) -> t h p c", p=P, h=2)
    adj_cols = core.args["adjT"].rearrange("(t p) (h c) -> t h p c", p=P, h=2)
    rows = st.sb("rows", [P, 2, HALF])
    cols = core.gcn_cols
    half_sum = st.sb("half_sum", [P, 2, 2])
    stats = st.sb("stats", [P, NT, 6])
    mean = st.sb("mean", [P, NT])
    var_eps = st.sb("var_eps", [P, NT])
    total = st.sb("total", [P, 2])
    var_sum = st.sb("var_sum", [P, 2])
    root = st.sb("root", [P, 2])
    scale = st.sb("scale", [P, 2])
    y = st.sb("y", [P, 2, F])
    rows_in = [st.sem(f"rows_in{h}") for h in range(2)]
    cols_in = [st.sem(f"cols_in{h}") for h in range(4)]
    rows_summed = st.sem("rows_summed")
    cols_masked = st.sem("cols_masked")
    cols_used = st.sem("cols_used")
    var_ready = st.sem("var_ready")
    root_ready = st.sem("root_ready")
    y_ready = st.sem("y_ready")
    dve_own = st.sem("dve_own")
    pe_own = st.sem("pe_own")

    with st.block() as block:
        @block.sync
        def _(sp):
            with sp.Fori(0, NT // 2) as i:
                for b in range(2):
                    t = 2 * i + b
                    for h in range(2):
                        sp.wait_ge(rows_summed, 2 * t + h + 1)
                        sp.dma_start(rows[:, h, :], adj_rows[t, h]).then_inc(rows_in[h], 16)
                    for h in range(2):
                        sp.wait_ge(cols_masked, 2 * t + h + 1)
                        sp.wait_ge(cols_used, 2 * t + h + 1)
                        sp.dma_start(cols[:, 2 * b + h, :], adj_cols[t, h]).then_inc(cols_in[2 * b + h], 16)

        @block.scalar
        def _(act):
            act.sem_inc(rows_summed, 2)
            with act.Fori(0, NT // 2) as i:
                for b in range(2):
                    t = 2 * i + b
                    for h in range(2):
                        act.wait_ge(rows_in[h], 16 * (t + 1))
                        nc.scalar.activation(rows[:, h, :], rows[:, h, :], ACT.Copy,
                                             accum_out=half_sum[:, b, h:h + 1]).then_inc(rows_summed, 1)
                    act.wait_ge(var_ready, t + 1)
                    nc.scalar.activation(root[:, b:b + 1], var_sum[:, b:b + 1], ACT.Sqrt).then_inc(root_ready, 1)

        @block.vector
        def _(dve):
            own = Chain(dve, dve_own)
            dve.sem_inc(cols_masked, 4)
            token_statistics(nc, dve, own, core.x, stats, mean, var_eps)
            with dve.Fori(0, NT // 2) as i:
                own.enter(i, 4)
                for b in range(2):
                    t = 2 * i + b
                    dve.wait_ge(rows_summed, 2 * t + 4)
                    own(nc.vector.tensor_tensor(total[:, b:b + 1], half_sum[:, b, 0:1], half_sum[:, b, 1:2], ALU.add))
                    nc.vector.tensor_copy(core.rowsum[:, bass.ds(t, 1)], total[:, b:b + 1])
                    nc.vector.tensor_tensor(var_sum[:, b:b + 1], var_eps[:, bass.ds(t, 1)], total[:, b:b + 1],
                                            ALU.mult).then_inc(var_ready, 1)
                    dve.wait_ge(root_ready, t + 1)
                    own(nc.vector.reciprocal(scale[:, b:b + 1], root[:, b:b + 1]))
                    dve.wait_ge(cols_used, 2 * t + 2)
                    nc.vector.tensor_scalar(y[:, b, :], column(core.x, t), mean[:, bass.ds(t, 1)],
                                            scale[:, b:b + 1], ALU.subtract, ALU.mult).then_inc(y_ready, 1)
                    for h in range(2):
                        dve.wait_ge(cols_in[2 * b + h], 16 * (i + 1))
                        nc.vector.tensor_scalar(core.mask[:, bass.ds(t, 1), h * HALF:(h + 1) * HALF].rearrange("p a f -> p (a f)"),
                                                cols[:, 2 * b + h, :], 0.0, None, ALU.is_gt).then_inc(cols_masked, 1)
                own.leave(NT // 2)

        @block.tensor
        def _(pe):
            acc = core.acc
            pe.sem_inc(cols_used, 4)
            for c in range(NB):
                nc.tensor.matmul(acc[:, c, :], core.zeros_b[:, 0:P], core.zeros_b[:, :], start=True, stop=False)
            with pe.Fori(0, NT // 2) as i:
                for b in range(2):
                    t = 2 * i + b
                    pe.wait_ge(y_ready, t + 1)
                    for h in range(2):
                        pe.wait_ge(cols_in[2 * b + h], 16 * (i + 1))
                        for c in range(NB // 2):
                            last = nc.tensor.matmul(acc[:, h * (NB // 2) + c, :], y[:, b, :],
                                                    cols[:, 2 * b + h, c * BANK:(c + 1) * BANK], start=False, stop=False)
                        last.then_inc(cols_used, 1)
            for c in range(NB):
                last = nc.tensor.matmul(acc[:, c, :], core.zeros_b[:, 0:P], core.zeros_b[:, :], start=False, stop=True)
            last.then_inc(pe_own, 1)
            pe.wait_ge(pe_own, 1)


def gcn_finish(core, st):
    nc = core.nc
    evac = st.sb("evac", [P, 2, BANK])
    act_out = st.sb("act_out", [P, 2, BANK])
    w = st.sb("w", [F, F])
    d_root = st.sb("d_root", [P, NT])
    d = st.sb("d", [P, NT])
    w_in = st.sem("w_in")
    rooted = st.sem("rooted")
    d_ready = st.sem("d_ready")
    evacuated = st.sem("evacuated")
    projected = st.sem("projected")
    dve_own = st.sem("dve_own2")
    xg = core.x[:, :, :].rearrange("p (g q) f -> p g (q f)", q=4)

    with st.block() as block:
        @block.sync
        def _(sp):
            sp.dma_start(w[:, :], core.args["L0_gnn_W"]).then_inc(w_in, 16)

        @block.scalar
        def _(act):
            nc.scalar.activation(d_root[:, :], core.rowsum[:, :], ACT.Sqrt).then_inc(rooted, 1)
            with act.Fori(0, NB // 2) as i:
                for b in range(2):
                    k = 2 * i + b
                    act.wait_ge(projected, k + 1)
                    nc.scalar.activation(evac[:, b, :], core.acc[:, bass.ds(k, 1), :].rearrange("p a f -> p (a f)"),
                                         ACT.Copy).then_inc(evacuated, 1)

        @block.tensor
        def _(pe):
            pe.sem_inc(projected, 2)
            pe.wait_ge(w_in, 16)
            with pe.Fori(0, NB // 2) as i:
                for b in range(2):
                    k = 2 * i + b
                    pe.wait_ge(evacuated, k + 1)
                    for q in range(4):
                        last = nc.tensor.matmul(core.acc[:, bass.ds(k, 1), q * P:(q + 1) * P].rearrange("p a f -> p (a f)"),
                                                evac[:, b, q * P:(q + 1) * P], w[:, :], start=True, stop=True)
                    last.then_inc(projected, 1)

        @block.vector
        def _(dve):
            own = Chain(dve, dve_own)
            dve.wait_ge(rooted, 1)
            own(nc.vector.reciprocal(d[:, :], d_root[:, :]))
            with dve.Fori(0, NB // 2) as i:
                own.enter(i, 4)
                for b in range(2):
                    k = 2 * i + b
                    dve.wait_ge(projected, k + 3)
                    for q in range(4):
                        ins = nc.vector.tensor_scalar(act_out[:, b, q * P:(q + 1) * P],
                                                      core.acc[:, bass.ds(k, 1), q * P:(q + 1) * P].rearrange("p a f -> p (a f)"),
                                                      d[:, bass.ds(4 * k + q, 1)], 0.0, ALU.mult, ALU.max)
                    own(ins)
                    xk = xg[:, bass.ds(k, 1), :].rearrange("p a f -> p (a f)")
                    own(nc.vector.tensor_tensor(xk, xk, act_out[:, b, :], ALU.add))
                own.leave(NB // 2)


def split3(nc, own, parts, src, rest):
    own(nc.vector.tensor_copy(parts[0], src))
    own(nc.vector.tensor_tensor(rest, src, parts[0], ALU.subtract))
    own(nc.vector.tensor_copy(parts[1], rest))
    own(nc.vector.tensor_tensor(rest, rest, parts[1], ALU.subtract))
    own(nc.vector.tensor_copy(parts[2], rest))


def slice_weights(core, st):
    nc, a = core.nc, core.args
    w_x = st.sb("w_x", [G, H, F])
    w_sliceT = st.sb("w_sliceT", [G, G])
    b_xT = st.sb("b_xT", [G, H])
    b_slice = st.sb("b_slice", [1, G])
    temp = st.sb("temp", [P, H])
    r_temp = st.sb("r_temp", [P, H])
    row = st.sb("row", [1, HG + 2 * F])
    parts = st.sb("parts", [1, 3, HG + 2 * F], BF16)
    rest = st.sb("rest", [1, HG + 2 * F])
    wc_ps = st.ps("wc_ps", [P, BANK])
    bc_ps = st.ps("bc_ps", [P, BANK])
    loaded = st.sem("loaded")
    multiplied = st.sem("multiplied")
    split = st.sem("split")
    moved = st.sem("moved")
    dve_own = st.sem("dve_own")

    with st.block() as block:
        @block.sync
        def _(sp):
            sp.dma_start(w_x[:, :, :], a["L0_ffn_W_x"].rearrange("(h p) f -> p h f", p=G)).then_inc(loaded, 16)
            sp.dma_start(w_sliceT[:, :], a["L0_ffn_W_sliceT"]).then_inc(loaded, 16)
            sp.dma_start(b_xT[:, :], a["L0_ffn_b_xT"]).then_inc(loaded, 16)
            sp.dma_start(b_slice[:, :], a["L0_ffn_b_slice"].unsqueeze(0)).then_inc(loaded, 16)
            sp.dma_start(temp[:, :], a["L0_ffn_temperature"].partition_broadcast(P)).then_inc(loaded, 16)
            sp.dma_start(row[:, HG:HG + F], a["L0_ffn_out_b"].unsqueeze(0)).then_inc(loaded, 16)
            sp.dma_start(row[:, HG + F:HG + 2 * F], a["L1_ffn_bo"].unsqueeze(0)).then_inc(loaded, 16)
            sp.wait_ge(split, 1)
            for k in range(3):
                sp.dma_start(core.bias3[k:k + 1, :], parts[:, k, :]).then_inc(moved, 16)
            sp.wait_ge(moved, 48)

        @block.tensor
        def _(pe):
            pe.wait_ge(loaded, 16 * 7)
            for h in range(H):
                nc.tensor.matmul(wc_ps[:, h * G:(h + 1) * G], w_x[:, h, :], w_sliceT[:, :], start=True, stop=True)
            for h in range(H):
                last = nc.tensor.matmul(bc_ps[0:1, h * G:(h + 1) * G], b_xT[:, h:h + 1], w_sliceT[:, :], start=True, stop=True)
            last.then_inc(multiplied, 1)

        @block.vector
        def _(dve):
            own = Chain(dve, dve_own)
            own(nc.vector.memset(core.bias3[:, :], 0.0))
            dve.wait_ge(loaded, 16 * 7)
            own(nc.vector.tensor_scalar(temp[:, :], temp[:, :], 1e-6, None, ALU.max))
            own(nc.vector.reciprocal(r_temp[:, :], temp[:, :]))
            dve.wait_ge(multiplied, 1)
            nc.vector.tensor_tensor(core.wc[:, :].rearrange("p (h g) -> p h g", h=H),
                                    wc_ps[:, :].rearrange("p (h g) -> p h g", h=H), bcast_mid(r_temp[:, :], G), ALU.mult)
            bc = row[:, 0:HG].rearrange("p (h g) -> p h g", h=H)
            own(nc.vector.tensor_tensor(bc, bc_ps[0:1, :].rearrange("p (h g) -> p h g", h=H),
                                        bcast_row(b_slice[:, :], H), ALU.add))
            own(nc.vector.tensor_tensor(bc, bc, bcast_mid(r_temp[0:1, :], G), ALU.mult))
            split3(nc, own, [parts[:, k, :] for k in range(3)], row[:, :], rest[:, :])
            dve.sem_inc(split, 1)


Q = 4


def slice_gather(core, st):
    nc = core.nc
    stats = st.sb("stats", [P, NT, 6])
    mean = st.sb("mean", [P, NT])
    var_eps = st.sb("var_eps", [P, NT])
    root = st.sb("root", [P, NT])
    rstd = st.sb("rstd", [P, NT])
    xn = st.sb("xn", [P, Q, F + 2])
    xnT = st.sb("xnT", [P, Q, P])
    e = st.sb("e", [P, Q, HG])
    sw = st.sb("sw", [P, Q, HG])
    top = st.sb("top", [P, Q * H])
    rsum = st.sb("rsum", [P, Q * H])
    xnT_ps = st.ps("xnT_ps", [P, Q, P])
    logits = st.ps("logits", [P, Q, HG])
    gath = st.ps("gath", [P, 2, BANK])
    rooted = st.sem("rooted")
    normed = st.sem("normed")
    xnT_done = st.sem("xnT_done")
    xnT_copied = st.sem("xnT_copied")
    logits_done = st.sem("logits_done")
    shifted = st.sem("shifted")
    exped = st.sem("exped")
    sw_ready = st.sem("sw_ready")
    sw_used = st.sem("sw_used")
    sw_stored = st.sem("sw_stored")
    gath_done = st.sem("gath_done")
    x_stored = st.sem("x_stored")
    dve_own = st.sem("dve_own")
    turns = NT // Q
    PAIRS = Q // 2
    PH = 2 * H

    def region(g):
        return gath[:, g // 2, (g % 2) * 256:(g % 2) * 256 + F + 2]

    with st.block() as block:
        @block.sync
        def _(sp):
            sp.sem_inc(sw_stored, 16)
            with sp.Fori(0, turns) as i:
                for c in range(PAIRS):
                    sp.wait_ge(sw_ready, PAIRS * i + c + 1)
                    sp.dma_start(core.sw_dram[bass.ds(PAIRS * i + c, 1), :, :].rearrange("a p f -> p (a f)"),
                                 sw[:, 2 * c:2 * c + 2, :].rearrange("p a f -> p (a f)")).then_inc(sw_stored, 16)
            sp.wait_ge(gath_done, 1)
            sp.dma_start(natural(core.x_dram), core.x[:, :, :]).then_inc(x_stored, 16)
            sp.wait_ge(sw_stored, 16 * (PAIRS * turns + 1))
            sp.wait_ge(x_stored, 16)

        @block.scalar
        def _(act):
            act.wait_ge(rooted, 1)
            nc.scalar.activation(root[:, :], var_eps[:, :], ACT.Sqrt).then_inc(rooted, 1)
            with act.Fori(0, turns) as i:
                act.wait_ge(xnT_done, i + 1)
                nc.scalar.activation(xnT[:, :, :], xnT_ps[:, :, :], ACT.Copy).then_inc(xnT_copied, 1)
                for c in range(PAIRS):
                    act.wait_ge(shifted, PAIRS * i + c + 1)
                    nc.scalar.activation(e[:, 2 * c:2 * c + 2, :], e[:, 2 * c:2 * c + 2, :], ACT.Exp).then_inc(exped, 1)

        @block.vector
        def _(dve):
            own = Chain(dve, dve_own)
            token_statistics(nc, dve, own, core.x, stats, mean, var_eps)
            dve.sem_inc(rooted, 1)
            dve.wait_ge(rooted, 2)
            own(nc.vector.reciprocal(rstd[:, :], root[:, :]))
            own(nc.vector.memset(xn[:, :, F:F + 2], 1.0))
            with dve.Fori(0, turns) as i:
                own.enter(i, 2 * PAIRS + PAIRS * 2)
                dve.wait_ge(sw_used, PAIRS * i + 1)
                for q in range(Q):
                    t = Q * i + q
                    last = nc.vector.tensor_scalar(xn[:, q, 0:F], column(core.x, t), mean[:, bass.ds(t, 1)],
                                                   rstd[:, bass.ds(t, 1)], ALU.subtract, ALU.mult)
                last.then_inc(normed, 1)
                for c in range(PAIRS):
                    dve.wait_ge(logits_done, PAIRS * i + c + 1)
                    lg = logits[:, 2 * c:2 * c + 2, :].rearrange("p a (h g) -> p (a h) g", g=G)
                    ev = e[:, 2 * c:2 * c + 2, :].rearrange("p a (h g) -> p (a h) g", g=G)
                    tp = top[:, c * PH:(c + 1) * PH]
                    own(nc.vector.tensor_reduce(tp, lg, AX.X, ALU.max))
                    nc.vector.tensor_tensor(ev, lg, bcast_mid(tp, G), ALU.subtract).then_inc(shifted, 1)
                for c in range(PAIRS):
                    dve.wait_ge(exped, PAIRS * i + c + 1)
                    ev = e[:, 2 * c:2 * c + 2, :].rearrange("p a (h g) -> p (a h) g", g=G)
                    sv = sw[:, 2 * c:2 * c + 2, :].rearrange("p a (h g) -> p (a h) g", g=G)
                    rs = rsum[:, c * PH:(c + 1) * PH]
                    own(nc.vector.tensor_reduce(rs, ev, AX.X, ALU.add))
                    own(nc.vector.reciprocal(rs, rs))
                    dve.wait_ge(sw_stored, 16 * (PAIRS * i + 1))
                    own(nc.vector.tensor_tensor(sv, ev, bcast_mid(rs, G), ALU.mult))
                    dve.sem_inc(sw_ready, 1)
                own.leave(turns)
            dve.wait_ge(gath_done, 1)
            for g in range(4):
                ins = nc.vector.tensor_copy(core.gathered[:, g, :], region(g)[:, 0:F + 1])
            own(ins)

        @block.tensor
        def _(pe):
            pe.sem_inc(sw_used, 1)
            for k in range(2):
                nc.tensor.matmul(gath[:, k, :], core.zeros_b[:, 0:P], core.zeros_b[:, :], start=True, stop=False)
            with pe.Fori(0, turns) as i:
                pe.wait_ge(normed, i + 1)
                for q in range(Q):
                    last = nc.tensor.transpose(xnT_ps[:, q, :], xn[:, q, 0:F], core.ident[:, :])
                last.then_inc(xnT_done, 1)
                pe.wait_ge(xnT_copied, i + 1)
                for q in range(Q):
                    nc.tensor.matmul(logits[:, q, :], xnT[:, q, :], core.wc[:, :], start=True, stop=False)
                    last = nc.tensor.matmul(logits[:, q, :], core.ones_b[:, :], core.bias3[:, 0:HG], start=False, stop=True)
                    if q % 2:
                        last.then_inc(logits_done, 1)
                for c in range(PAIRS):
                    pe.wait_ge(sw_ready, PAIRS * i + c + 1)
                    for q in (2 * c, 2 * c + 1):
                        for g in range(4):
                            last = nc.tensor.matmul(region(g), sw[:, q, g * P:(g + 1) * P], xn[:, q, :], start=False, stop=False)
                    last.then_inc(sw_used, 1)
            for k in range(2):
                last = nc.tensor.matmul(gath[:, k, :], core.zeros_b[:, 0:P], core.zeros_b[:, :], start=False, stop=True)
            last.then_inc(gath_done, 1)


def mixer(core, st):
    nc, a = core.nc, core.args
    in_wT = st.sb("in_wT", [P, 4, NPROJ])
    spare = core.x[:, :, :].rearrange("p t f -> p (t f)")
    hy_outT = spare[:, 0:4 * DI].rearrange("p (k n) -> p k n", k=4)
    w_fxT = spare[:, 4 * DI:5 * DI]
    steps = spare[0:G, 5 * DI:7 * DI].rearrange("p (d h t) -> p d h t", d=2, h=H)
    y = spare[0:G, 7 * DI:8 * DI]
    b_fx = st.sb("b_fx", [1, DI])
    conv_w = st.sb("conv_w", [P, CH, 3])
    conv_b = st.sb("conv_b", [P, CH])
    dt_bias = st.sb("dt_bias", [G, 2, H])
    a_neg = st.sb("a_neg", [G, H])
    d_skip = st.sb("d_skip", [G, H])
    fcdT = st.sb("fcdT", [P, 4, H])
    norm_w = st.sb("norm_w", [G, DI])
    out_wT = st.sb("out_wT", [P, 4, F])
    gT = st.sb("gT", [P, 4, P])
    ratio_row = st.sb("ratio_row", [1, 4, P])
    inv = st.sb("inv", [P, 4])
    scaled = st.sb("scaled", [P, 4, F + 1])
    stT = st.sb("stT", [P, 4, G])
    xpad = st.sb("xpad", [P, CH, G + 2])
    tap = st.sb("tap", [P, CH, G])
    conv = st.sb("conv", [P, CH, G])
    act_e = tap
    xc = st.sb("xc", [P, CH, G])
    c_pad = st.sb("c_pad", [G, G + 2])
    x_nat = st.sb("x_nat", [G, DI])
    z = st.sb("z", [G, DI])
    z_e = st.sb("z_e", [G, DI])
    dt_raw = st.sb("dt_raw", [G, 2 * H])
    dt_u = st.sb("dt_u", [G, 2 * H])
    dt_l = st.sb("dt_l", [G, 2 * H])
    dt_p = st.sb("dt_p", [G, 2 * H])
    dt = st.sb("dt", [G, 2 * H])
    gt = st.sb("gt", [G, G])
    lt = st.sb("lt", [G, G])
    decay = st.sb("decay", [G, 2, H, G])
    cb = st.sb("cb", [G, 2, G])
    mix = st.sb("mix", [G, H, G])
    gate = st.sb("gate", [G, H])
    sq = st.sb("sq", [G, 2])
    ygT = st.sb("ygT", [P, 4, G])
    blocks = gT
    ps = [st.ps(f"ps{k}", [P, BANK]) for k in range(8)]
    loaded = st.sem("loaded")
    masks = st.sem("masks")
    to_pe = st.sem("to_pe")
    from_pe = st.sem("from_pe")
    to_act = st.sem("to_act")
    from_act = st.sem("from_act")
    dve_own = st.sem("dve_own")
    NLOADS = 13

    with st.block() as block:
        @block.sync
        def _(sp):
            for dst, src in ((w_fxT[:, :], a["L0_ffn_W_fxT"]), (b_fx[:, :], a["L0_ffn_b_fx"].unsqueeze(0)),
                             (in_wT[:, :, :], a["L0_ffn_hy_in_wT"].rearrange("(k p) n -> p k n", p=P)),
                             (conv_w[:, :, :], a["conv_w"]), (conv_b[:, :], a["conv_b"]),
                             (dt_bias[:, 0, :], a["L0_ffn_hy_dt_bias"].partition_broadcast(G)),
                             (dt_bias[:, 1, :], a["L0_ffn_hy_dt_bias"].partition_broadcast(G)),
                             (a_neg[:, :], a["L0_ffn_hy_A_log"].partition_broadcast(G)),
                             (d_skip[:, :], a["L0_ffn_hy_D"].partition_broadcast(G)),
                             (fcdT[:, :, :], a["L0_ffn_hy_fcD_wT"]),
                             (norm_w[:, :], a["L0_ffn_hy_norm_w"].partition_broadcast(G)),
                             (hy_outT[:, :, :], a["L0_ffn_hy_out_wT"].rearrange("(k p) n -> p k n", p=P)),
                             (out_wT[:, :, :], a["L0_ffn_out_wT"].rearrange("(k p) n -> p k n", p=P))):
                sp.dma_start(dst, src).then_inc(loaded, 16)

        @block.gpsimd
        def _(pool):
            nc.gpsimd.memset(gt[:, :], 0.0)
            nc.gpsimd.memset(lt[:, :], 0.0).then_inc(masks, 1)
            pool.wait_ge(masks, 1)
            nc.gpsimd.affine_select(out=gt[:, :], in_=gt[:, :], compare_op=ALU.is_ge, fill=1.0,
                                    base=0, pattern=[[1, G]], channel_multiplier=-1)
            nc.gpsimd.affine_select(out=lt[:, :], in_=lt[:, :], compare_op=ALU.is_ge, fill=1.0,
                                    base=0, pattern=[[-1, G]], channel_multiplier=1).then_inc(masks, 1)

        @block.vector
        def _(dve):
            own = Chain(dve, dve_own)
            own(nc.vector.memset(xpad[:, :, :], 0.0))
            own(nc.vector.memset(c_pad[:, :], 0.0))
            own(nc.vector.memset(conv[:, :, :], 0.0))
            snorm = core.gathered[:, :, F]
            own(nc.vector.tensor_scalar(inv[:, :], snorm, EPS, None, ALU.add))
            own(nc.vector.reciprocal(inv[:, :], inv[:, :]))
            own(nc.vector.tensor_tensor(scaled[:, :, :], core.gathered[:, :, :], bcast_mid(inv[:, :], F + 1), ALU.mult))
            dve.sem_inc(to_pe, 1)
            dve.wait_ge(from_pe, 1)
            nc.vector.tensor_copy(gT[:, :, :], ps[0][:, :].rearrange("p (k g) -> p k g", k=4))
            own(nc.vector.tensor_copy(ratio_row[:, :, :], ps[1][0:1, :].rearrange("p (k g) -> p k g", k=4)))
            dve.sem_inc(to_pe, 1)
            dve.wait_ge(from_pe, 2)
            own(nc.vector.memset(blocks[:, :, :], 0.0))
            v = ps[2][:, :].rearrange("p (k g) -> p k g", k=4)
            nc.vector.tensor_copy(stT[0:G, :, :], v[0:G, :, 0:G])
            own(nc.vector.tensor_copy(stT[G:P, :, :], v[G:P, :, G:P]))
            dve.sem_inc(to_pe, 1)
            dve.wait_ge(loaded, 16 * NLOADS)
            dve.wait_ge(from_pe, 3)
            nc.vector.tensor_copy(z[:, :], ps[3][0:G, :])
            nc.vector.tensor_tensor(dt_raw[:, :], ps[4][0:G, 0:2 * H], dt_bias[:, :, :].rearrange("p a h -> p (a h)"), ALU.add)
            pre = ps[5][:, 0:CH * G].rearrange("p (c t) -> p c t", c=CH)
            nc.vector.tensor_scalar(a_neg[:, :], a_neg[:, :], A_LOG_CAP, None, ALU.min)
            nc.vector.tensor_copy(xpad[:, 0:4, 2:G + 2], pre[:, 0:4, :])
            own(nc.vector.tensor_copy(xpad[0:G, 4:6, 2:G + 2], pre[0:G, 4:6, :]))
            own(nc.vector.tensor_scalar(dt_u[:, :], dt_raw[:, :], -1.0, None, ALU.mult))
            own(nc.vector.tensor_tensor(dt_u[:, :], dt_u[:, :], dt_raw[:, :], ALU.min))
            dve.sem_inc(to_act, 1)
            for k in range(3):
                own(nc.vector.tensor_tensor(tap[:, :, :], xpad[:, :, k:k + G], bcast_mid(conv_w[:, :, k], G), ALU.mult))
                own(nc.vector.tensor_tensor(conv[:, :, :], conv[:, :, :], tap[:, :, :], ALU.add))
            own(nc.vector.tensor_tensor(conv[:, :, :], conv[:, :, :], bcast_mid(conv_b[:, :], G), ALU.add))
            dve.sem_inc(to_act, 1)
            dve.wait_ge(from_act, 1)
            own(nc.vector.tensor_scalar(dt_p[:, :], dt_u[:, :], 1.0, None, ALU.add))
            dve.sem_inc(to_act, 1)
            dve.wait_ge(from_act, 2)
            own(nc.vector.tensor_scalar(act_e[:, :, :], act_e[:, :, :], 1.0, None, ALU.add))
            own(nc.vector.reciprocal(act_e[:, :, :], act_e[:, :, :]))
            own(nc.vector.tensor_tensor(xc[:, :, :], conv[:, :, :], act_e[:, :, :], ALU.mult))
            own(nc.vector.tensor_copy(c_pad[:, 1:G + 1], xc[0:G, 5, :]))
            dve.sem_inc(to_pe, 1)
            dve.wait_ge(from_act, 3)
            own(nc.vector.tensor_scalar(dt[:, :], dt_p[:, :], -1.0, 1e-30, ALU.add, ALU.max))
            own(nc.vector.reciprocal(dt[:, :], dt[:, :]))
            own(nc.vector.tensor_tensor(dt_l[:, :], dt_l[:, :], dt[:, :], ALU.mult))
            own(nc.vector.tensor_scalar(dt[:, :], dt_p[:, :], 1.0, None, ALU.is_equal))
            own(nc.vector.tensor_tensor(dt_l[:, :], dt_l[:, :], dt[:, :], ALU.add))
            own(nc.vector.tensor_tensor(dt_l[:, :], dt_l[:, :], dt_u[:, :], ALU.mult))
            own(nc.vector.scalar_tensor_tensor(out=dt[:, :], in0=dt_raw[:, :], scalar=0.0, in1=dt_l[:, :],
                                               op0=ALU.max, op1=ALU.add))
            dve.wait_ge(masks, 2)
            for d, m in ((0, lt), (1, gt)):
                own(nc.vector.tensor_tensor(steps[:, d, :, :], bcast_row(m[:, :], H),
                                            bcast_mid(dt[:, d * H:(d + 1) * H], G), ALU.mult))
            dve.sem_inc(to_pe, 1)
            dve.wait_ge(from_pe, 4)
            own(nc.vector.tensor_copy(x_nat[:, :], ps[6][0:G, :]))
            own(nc.vector.tensor_tensor(cb[:, 0, :], ps[7][0:G, 0:G], lt[:, :], ALU.mult))
            own(nc.vector.tensor_tensor(cb[:, 1, :], ps[7][0:G, G:2 * G], gt[:, :], ALU.mult))
            own(nc.vector.tensor_tensor(gate[:, :], ps[7][0:G, 2 * G:2 * G + H], d_skip[:, :], ALU.add))
            dve.wait_ge(from_pe, 5)
            for d in range(2):
                own(nc.vector.tensor_tensor(decay[:, d, :, :], ps[d][0:G, :].rearrange("p (h t) -> p h t", h=H),
                                            bcast_mid(a_neg[:, :], G), ALU.mult))
            dve.sem_inc(to_act, 1)
            dve.wait_ge(from_act, 4)
            for d in range(2):
                own(nc.vector.tensor_tensor(decay[:, d, :, :], decay[:, d, :, :], bcast_row(cb[:, d, :], H), ALU.mult))
                own(nc.vector.tensor_tensor(decay[:, d, :, :], decay[:, d, :, :],
                                            bcast_mid(dt[:, d * H:(d + 1) * H], G), ALU.mult))
            own(nc.vector.tensor_tensor(mix[:, :, :], decay[:, 0, :, :], decay[:, 1, :, :], ALU.add))
            dve.sem_inc(to_pe, 1)
            own(nc.vector.tensor_scalar(z_e[:, :], z_e[:, :], 1.0, None, ALU.add))
            own(nc.vector.reciprocal(z_e[:, :], z_e[:, :]))
            own(nc.vector.tensor_tensor(z[:, :], z[:, :], z_e[:, :], ALU.mult))
            own(nc.vector.tensor_tensor(y[:, :].rearrange("p (h c) -> p h c", h=H),
                                        x_nat[:, :].rearrange("p (h c) -> p h c", h=H), bcast_mid(gate[:, :], G), ALU.mult))
            dve.wait_ge(from_pe, 6)
            own(nc.vector.tensor_tensor(y[:, :], y[:, :], ps[2][0:G, :], ALU.add))
            own(nc.vector.tensor_tensor(y[:, :], y[:, :], z[:, :], ALU.mult))
            dve.sem_inc(to_act, 1)
            dve.wait_ge(from_act, 5)
            own(nc.vector.tensor_scalar(sq[:, 0:1], sq[:, 0:1], 1.0 / DI, EPS, ALU.mult, ALU.add))
            dve.sem_inc(to_act, 1)
            dve.wait_ge(from_act, 6)
            own(nc.vector.reciprocal(sq[:, 0:1], sq[:, 1:2]))
            own(nc.vector.scalar_tensor_tensor(out=y[:, :], in0=y[:, :], scalar=sq[:, 0:1], in1=norm_w[:, :],
                                               op0=ALU.mult, op1=ALU.mult))
            dve.sem_inc(to_pe, 1)
            dve.wait_ge(from_pe, 7)
            own(nc.vector.tensor_copy(ygT[:, :, :], ps[3][:, 0:4 * G].rearrange("p (k t) -> p k t", k=4)))
            dve.sem_inc(to_pe, 1)
            dve.wait_ge(from_pe, 8)
            v = ps[4][:, 0:4 * G].rearrange("p (k t) -> p k t", k=4)
            nc.vector.tensor_copy(blocks[0:G, :, 0:G], v[0:G, :, :])
            own(nc.vector.tensor_copy(blocks[G:P, :, G:P], v[G:P, :, :]))
            dve.sem_inc(to_pe, 1)
            dve.wait_ge(from_pe, 9)
            own(nc.vector.tensor_copy(core.way_back[:, :, :], ps[5][:, :].rearrange("p (k f) -> p k f", k=4)))

        @block.scalar
        def _(act):
            act.wait_ge(to_act, 1)
            nc.scalar.activation(a_neg[:, :], a_neg[:, :], ACT.Exp)
            nc.scalar.activation(z_e[:, :], z[:, :], ACT.Exp, scale=-1.0)
            nc.scalar.activation(dt_u[:, :], dt_u[:, :], ACT.Exp).then_inc(from_act, 1)
            act.wait_ge(from_act, 1)
            nc.scalar.mul(a_neg[:, :], a_neg[:, :], -1.0)
            act.wait_ge(to_act, 2)
            nc.scalar.activation(act_e[:, :, :], conv[:, :, :], ACT.Exp, scale=-1.0).then_inc(from_act, 1)
            act.wait_ge(to_act, 3)
            nc.scalar.activation(dt_l[:, :], dt_p[:, :], ACT.Ln).then_inc(from_act, 1)
            act.wait_ge(to_act, 4)
            nc.scalar.activation(decay[:, :, :, :], decay[:, :, :, :], ACT.Exp).then_inc(from_act, 1)
            act.wait_ge(to_act, 5)
            nc.scalar.activation(z_e[:, :], y[:, :], ACT.Square, accum_out=sq[:, 0:1]).then_inc(from_act, 1)
            act.wait_ge(to_act, 6)
            nc.scalar.activation(sq[:, 1:2], sq[:, 0:1], ACT.Sqrt).then_inc(from_act, 1)

        @block.tensor
        def _(pe):
            mm, tr = nc.tensor.matmul, nc.tensor.transpose
            pe.wait_ge(to_pe, 1)
            for k in range(4):
                tr(ps[0][:, k * P:(k + 1) * P], scaled[:, k, 0:F], core.ident[:, :])
                last = tr(ps[1][0:1, k * P:(k + 1) * P], scaled[:, k, F:F + 1], core.ident[:, :])
            last.then_inc(from_pe, 1)
            pe.wait_ge(loaded, 16 * NLOADS)
            pe.wait_ge(to_pe, 2)
            for k in range(4):
                mm(ps[2][:, k * P:(k + 1) * P], w_fxT[:, k * P:(k + 1) * P], gT[:, k, :], start=True, stop=False)
                last = mm(ps[2][:, k * P:(k + 1) * P], b_fx[:, k * P:(k + 1) * P], ratio_row[:, k, :], start=False, stop=True)
            last.then_inc(from_pe, 1)
            pe.wait_ge(to_pe, 3)
            for k in range(4):
                mm(ps[3][0:G, :], stT[:, k, :], in_wT[:, k, 0:DI], start=k == 0, stop=k == 3)
            for k in range(4):
                mm(ps[4][0:G, 0:2 * H], stT[:, k, :], in_wT[:, k, 2 * DI + 2 * NS:NPROJ], start=k == 0, stop=k == 3)
            for c in range(CH):
                lo = DI + c * P if c < 4 else 2 * DI + (c - 4) * NS
                m = P if c < 4 else NS
                for k in range(4):
                    last = mm(ps[5][0:m, c * G:(c + 1) * G], in_wT[:, k, lo:lo + m], stT[:, k, :], start=k == 0, stop=k == 3)
            last.then_inc(from_pe, 1)
            pe.wait_ge(to_pe, 4)
            for k in range(4):
                tr(ps[6][0:G, k * P:(k + 1) * P], xc[:, k, :], core.ident[:, :])
            for d in range(2):
                mm(ps[7][0:G, d * G:(d + 1) * G], xc[0:G, 4, :], c_pad[:, 2 * d:2 * d + G], start=True, stop=True)
            for k in range(4):
                last = mm(ps[7][0:G, 2 * G:2 * G + H], xc[:, k, :], fcdT[:, k, :], start=k == 0, stop=k == 3)
            last.then_inc(from_pe, 1)
            pe.wait_ge(to_pe, 5)
            for d, m in ((0, gt), (1, lt)):
                last = mm(ps[d][0:G, :], m[:, :], steps[:, d, :, :].rearrange("p h t -> p (h t)"), start=True, stop=True)
            last.then_inc(from_pe, 1)
            pe.wait_ge(to_pe, 6)
            for h in range(H):
                last = mm(ps[2][0:G, h * G:(h + 1) * G], mix[:, h, :], x_nat[:, h * G:(h + 1) * G], start=True, stop=True)
            last.then_inc(from_pe, 1)
            pe.wait_ge(to_pe, 7)
            for k in range(4):
                last = tr(ps[3][:, k * G:(k + 1) * G], y[:, k * P:(k + 1) * P], core.ident[0:G, 0:G])
            last.then_inc(from_pe, 1)
            pe.wait_ge(to_pe, 8)
            for m in range(4):
                for k in range(4):
                    last = mm(ps[4][:, m * G:(m + 1) * G], hy_outT[:, k, m * P:(m + 1) * P], ygT[:, k, :], start=k == 0, stop=k == 3)
            last.then_inc(from_pe, 1)
            pe.wait_ge(to_pe, 9)
            for k in range(4):
                last = mm(ps[5][:, k * P:(k + 1) * P], blocks[:, k, :], out_wT[:, k, :], start=True, stop=True)
            last.then_inc(from_pe, 1)


def slice_scatter(core, st):
    nc = core.nc
    sw = st.sb("sw", [P, 2, Q, HG])
    swT = st.sb("swT", [P, Q, 4, P])
    swT_ps = st.ps("swT_ps", [P, Q, 4, P])
    out_ps = st.ps("out_ps", [P, 2, Q, P])
    sw_in = [st.sem(f"sw_in{k}") for k in range(2)]
    turned = st.sem("turned")
    swT_ready = st.sem("swT_ready")
    scattered = st.sem("scattered")
    added = st.sem("added")
    x_back = st.sem("x_back")
    turns = NT // Q // 2
    xg = core.x[:, :, :].rearrange("p (g q) f -> p g (q f)", q=Q)

    with st.block() as block:
        @block.sync
        def _(sp):
            sp.dma_start(core.x[:, :, :], natural(core.x_dram)).then_inc(x_back, 16)
            with sp.Fori(0, turns) as i:
                for b in range(2):
                    g = 2 * i + b
                    sp.wait_ge(turned, 2 * g + 2)
                    for c in range(2):
                        sp.dma_start(sw[:, b, 2 * c:2 * c + 2, :].rearrange("p a f -> p (a f)"),
                                     core.sw_dram[bass.ds(2 * g + c, 1), :, :].rearrange("a p f -> p (a f)")).then_inc(sw_in[b], 16)

        @block.tensor
        def _(pe):
            pe.sem_inc(turned, 4)
            pe.sem_inc(scattered, 1)
            with pe.Fori(0, turns) as i:
                for b in range(2):
                    g = 2 * i + b
                    pe.wait_ge(sw_in[b], 32 * (i + 1))
                    for c in range(2):
                        pe.wait_ge(swT_ready, 2 * g + c + 1)
                        for q in (2 * c, 2 * c + 1):
                            for k in range(4):
                                last = nc.tensor.transpose(swT_ps[:, q, k, :], sw[:, b, q, k * P:(k + 1) * P], core.ident[:, :])
                        last.then_inc(turned, 1)
                    pe.wait_ge(added, g + 1)
                    for c in range(2):
                        pe.wait_ge(swT_ready, 2 * g + c + 3)
                        for q in (2 * c, 2 * c + 1):
                            for k in range(4):
                                nc.tensor.matmul(out_ps[:, b, q, :], swT[:, q, k, :], core.way_back[:, k, :], start=k == 0, stop=False)
                            last = nc.tensor.matmul(out_ps[:, b, q, :], core.ones_b[:, :], core.bias3[:, HG:HG + F], start=False, stop=True)
                    last.then_inc(scattered, 1)

        @block.scalar
        def _(act):
            act.sem_inc(swT_ready, 2)
            with act.Fori(0, turns) as i:
                for b in range(2):
                    g = 2 * i + b
                    act.wait_ge(scattered, g + 1)
                    for c in range(2):
                        act.wait_ge(turned, 2 * g + c + 5)
                        nc.scalar.activation(swT[:, 2 * c:2 * c + 2, :, :], swT_ps[:, 2 * c:2 * c + 2, :, :], ACT.Copy).then_inc(swT_ready, 1)

        @block.vector
        def _(dve):
            dve.sem_inc(added, 2)
            dve.wait_ge(x_back, 16)
            with dve.Fori(0, turns) as i:
                for b in range(2):
                    g = 2 * i + b
                    dve.wait_ge(scattered, g + 2)
                    nc.vector.tensor_tensor(column(xg, g), out_ps[:, b, :, :].rearrange("p q f -> p (q f)"), column(xg, g),
                                            ALU.add).then_inc(added, 1)


def slice_attention(core):
    with core.stage("slice") as st:
        core.wc = st.sb("wc", [P, HG])
        core.gathered = st.sb("gathered", [P, 4, F + 1])
        core.way_back = st.sb("way_back", [P, 4, F])
        with core.stage("sliw") as s:
            slice_weights(core, s)
        with core.stage("slig") as s:
            slice_gather(core, s)
        with core.stage("mix") as s:
            mixer(core, s)
        with core.stage("slis") as s:
            slice_scatter(core, s)


def attention_factors(core, st):
    nc, a = core.nc, core.args
    stats = st.sb("stats", [P, NT, 6])
    mean = st.sb("mean", [P, NT])
    var_eps = st.sb("var_eps", [P, NT])
    root = st.sb("root", [P, NT])
    rstd = st.sb("rstd", [P, NT])
    avec = st.sb("avec", [P, 2, F])
    product = core.r_rows[:, :].rearrange("p (t f) -> p t f", f=F)
    feats = st.sb("feats", [P, 2, NT])
    top = st.sb("top", [P, 1])
    top_all = st.sb("top_all", [P, 1])
    expo = st.sb("expo", [P, 4, NT])
    fours = st.sb("fours", [P, 4, NT])
    parts = st.sb("parts", [P, 3, 4, NT], BF16)
    rest = st.sb("rest", [P, 4, NT])
    diag = st.sb("diag", [P, 2, 4, P])
    rows_ps = st.ps("rows_ps", [P, 2, BANK])
    x_stored = st.sem("x_stored")
    loaded = st.sem("loaded")
    rooted = st.sem("rooted")
    stats_done = st.sem("stats_done")
    top_ready = st.sem("top_ready")
    expo_ready = st.sem("expo_ready")
    exped = st.sem("exped")
    diag_ready = st.sem("diag_ready")
    rows_done = st.sem("rows_done")
    rows_copied = st.sem("rows_copied")
    product_used = st.sem("product_used")
    dve_own = st.sem("dve_own")

    with st.block() as block:
        @block.sync
        def _(sp):
            for k in range(2):
                sp.dma_start(avec[:, k, :], a["L1_gnn_a"][k * F:(k + 1) * F].partition_broadcast(P)).then_inc(loaded, 16)
            sp.dma_start(core.coef[:, :], a["L1_gnn_temp"].partition_broadcast(P)).then_inc(loaded, 16)
            sp.dma_start(natural(core.x_dram), core.x[:, :, :]).then_inc(x_stored, 16)
            sp.wait_ge(x_stored, 16)

        @block.gpsimd
        def _(pool):
            pool.wait_ge(top_ready, 1)
            nc.gpsimd.partition_all_reduce(top_all[:, :], top[:, :], P, RMAX).then_inc(top_ready, 1)

        @block.scalar
        def _(act):
            act.wait_ge(stats_done, 1)
            nc.scalar.activation(root[:, :], var_eps[:, :], ACT.Sqrt).then_inc(rooted, 1)
            act.wait_ge(expo_ready, 1)
            nc.scalar.activation(core.coef[:, :], core.coef[:, :], ACT.Exp, scale=-1.0)
            nc.scalar.activation(expo[:, 0:3, :], expo[:, 0:3, :], ACT.Exp).then_inc(exped, 1)
            act.sem_inc(rows_copied, 1)
            with act.Fori(0, NB // 2) as i:
                for b in range(2):
                    g = 2 * i + b
                    act.wait_ge(rows_done, g + 1)
                    nc.scalar.activation(core.r_rows[:, bass.ds(g * BANK, BANK)], rows_ps[:, b, :], ACT.Copy).then_inc(rows_copied, 1)

        @block.vector
        def _(dve):
            own = Chain(dve, dve_own)
            token_statistics(nc, dve, own, core.x, stats, mean, var_eps)
            dve.sem_inc(stats_done, 1)
            dve.wait_ge(rooted, 1)
            own(nc.vector.reciprocal(rstd[:, :], root[:, :]))
            dve.wait_ge(x_stored, 16)
            with dve.Fori(0, NT // 4) as i:
                own.enter(i, 1)
                for b in range(4):
                    t = 4 * i + b
                    last = nc.vector.tensor_scalar(column(core.x, t), column(core.x, t), mean[:, bass.ds(t, 1)],
                                                   rstd[:, bass.ds(t, 1)], ALU.subtract, ALU.mult)
                own(last)
                own.leave(NT // 4)
            dve.wait_ge(loaded, 48)
            for k in range(2):
                own(nc.vector.tensor_tensor(product, core.x[:, :, :], bcast_row(avec[:, k, :], NT), ALU.mult))
                own(nc.vector.tensor_reduce(feats[:, k, :], product, AX.X, ALU.add))
            own(nc.vector.tensor_reduce(top[:, :], feats[:, 1, :], AX.X, ALU.max))
            dve.sem_inc(top_ready, 1)
            dve.wait_ge(top_ready, 2)
            own(nc.vector.tensor_scalar(expo[:, 0, :], feats[:, 1, :], top_all[:, :], None, ALU.subtract))
            nc.vector.tensor_scalar(expo[:, 1, :], expo[:, 0, :], SLOPE, None, ALU.mult)
            own(nc.vector.tensor_scalar(expo[:, 2, :], feats[:, 0, :], top_all[:, :], 0.0, ALU.add, ALU.max))
            own(nc.vector.tensor_scalar(expo[:, 2, :], expo[:, 2, :], SLOPE - 1.0, None, ALU.mult))
            dve.sem_inc(expo_ready, 1)
            dve.wait_ge(exped, 1)
            high, low, r = (expo[:, k, :] for k in range(3))
            nc.vector.tensor_copy(core.r[:, :], r)
            nc.vector.tensor_copy(core.token[:, :, HIGH], high)
            nc.vector.tensor_copy(core.token[:, :, LOW], low)
            nc.vector.tensor_scalar(core.token[:, :, NEG_HIGH], high, -1.0, None, ALU.mult)
            own(nc.vector.tensor_scalar(core.coef[:, :], core.coef[:, :], 1.0, None, ALU.add))
            own(nc.vector.reciprocal(core.coef[:, :], core.coef[:, :]))
            own(nc.vector.tensor_scalar(core.coef_rest[:, :], core.coef[:, :], -1.0, 1.0, ALU.mult, ALU.add))
            with dve.Fori(0, NB // 2) as i:
                for b in range(2):
                    g = 2 * i + b
                    dve.wait_ge(rows_copied, g + 1)
                    nc.vector.tensor_tensor(diag[:, b, :, :], bcast_row(core.ident[:, :], 4),
                                            bcast_mid(core.r[:, bass.ds(4 * g, 4)], P), ALU.mult).then_inc(diag_ready, 1)
            own(nc.vector.tensor_copy(fours[:, 0, :], high))
            own(nc.vector.tensor_tensor(fours[:, 1, :], high, high, ALU.mult))
            own(nc.vector.tensor_copy(fours[:, 2, :], low))
            own(nc.vector.tensor_tensor(fours[:, 3, :], low, low, ALU.mult))
            split3(nc, own, [parts[:, k, :, :] for k in range(3)], fours[:, :, :], rest[:, :, :])
            own(nc.vector.memset(core.weigh[:, :, :], 0.0))
            for k in range(3):
                nc.vector.tensor_copy(core.weigh[:, :, k:6:3].rearrange("p t q -> p q t"), parts[:, k, 0:2, :])
                nc.vector.tensor_scalar(core.weigh[:, :, WK + k:WK + 6:3].rearrange("p t q -> p q t"), parts[:, k, 0:2, :], -1.0, None, ALU.mult)
                own(nc.vector.tensor_copy(core.weigh[:, :, WK + 6 + k:WK + 12:3].rearrange("p t q -> p q t"), parts[:, k, 2:4, :]))

        @block.tensor
        def _(pe):
            with pe.Fori(0, NB // 2) as i:
                for b in range(2):
                    g = 2 * i + b
                    pe.wait_ge(diag_ready, g + 1)
                    nc.tensor.matmul(rows_ps[:, b, :], core.ones[:, :], diag[:, b, :, :].rearrange("p q f -> p (q f)"),
                                     start=True, stop=True).then_inc(rows_done, 1)


WK = 12
CHUNK = 1024
HIGH, LOW, NEG_HIGH = range(3)


def propagate_first(core, st, half):
    nc = core.nc
    above = st.sb("above", [P, 2, CHUNK])
    mask_b = st.sb("mask_b", [P, 2, CHUNK], BF16)
    z = st.sb("z", [P, 2, CHUNK])
    lower = st.sb("lower", [P, 2, CHUNK], BF16)
    tokj = st.sb("tokj", [P, 2, 3])
    xj = st.sb("xj", [P, 2, F])
    wj = st.sb("wj", [P, 2, 2 * WK], BF16)
    above_ready = st.sem("above_ready")
    mask_ready = st.sem("mask_ready")
    weighed = st.sem("weighed")
    used = st.sem("used")
    picked = st.sem("picked")
    ended = st.sem("ended")
    acc, sums = core.acc, core.sums
    base = half * HALF

    with st.block() as block:
        @block.gpsimd
        def _(pool):
            with pool.Fori(0, NT // 2) as i:
                for b in range(2):
                    j = 2 * i + b
                    pool.wait_ge(used, 2 * j + 2)
                    nc.gpsimd.tensor_copy(xj[:, b, :], column(core.x, j))
                    nc.gpsimd.tensor_copy(tokj[:, b, :], column(core.token, j))
                    nc.gpsimd.tensor_copy(wj[:, b, :], column(core.weigh, j)).then_inc(picked, 1)

        @block.scalar
        def _(act):
            with act.Fori(0, NT // 2) as i:
                for b in range(2):
                    j = 2 * i + b
                    act.wait_ge(picked, j + 1)
                    for c in range(2):
                        n = 2 * j + c
                        lo = base + c * CHUNK
                        act.wait_ge(weighed, n + 1)
                        nc.scalar.activation(above[:, c, :], core.r_rows[:, lo:lo + CHUNK], ACT.Relu,
                                             scale=tokj[:, b, LOW:LOW + 1], bias=tokj[:, b, NEG_HIGH:NEG_HIGH + 1]).then_inc(above_ready, 1)
                        act.wait_ge(used, n + 3)
                        nc.scalar.activation(mask_b[:, c, :], column(core.mask[:, :, lo:lo + CHUNK], j), ACT.Copy).then_inc(mask_ready, 1)

        @block.vector
        def _(dve):
            dve.sem_inc(weighed, 2)
            with dve.Fori(0, NT // 2) as i:
                for b in range(2):
                    j = 2 * i + b
                    for c in range(2):
                        n = 2 * j + c
                        lo = base + c * CHUNK
                        dve.wait_ge(above_ready, n + 1)
                        dve.wait_ge(used, n + 3)
                        nc.vector.scalar_tensor_tensor(out=lower[:, c, :], in0=above[:, c, :], scalar=0.0,
                                                       in1=column(core.mask[:, :, lo:lo + CHUNK], j), op0=ALU.is_gt, op1=ALU.mult)
                        nc.vector.scalar_tensor_tensor(out=z[:, c, :], in0=above[:, c, :], scalar=tokj[:, b, HIGH:HIGH + 1],
                                                       in1=column(core.mask[:, :, lo:lo + CHUNK], j), op0=ALU.add, op1=ALU.mult).then_inc(weighed, 1)

        @block.tensor
        def _(pe):
            pe.sem_inc(used, 4)
            for k in range(4):
                nc.tensor.matmul(acc[:, k, :], core.zeros_b[:, 0:P], core.zeros_b[:, :], start=True, stop=False)
                nc.tensor.matmul(sums[0:WK, k, :], core.zeros_b[:, 0:WK], core.zeros_b[:, :], start=True, stop=False)
            with pe.Fori(0, NT // 2) as i:
                for b in range(2):
                    j = 2 * i + b
                    pe.wait_ge(picked, j + 1)
                    for c in range(2):
                        n = 2 * j + c
                        pe.wait_ge(mask_ready, n + 1)
                        pe.wait_ge(weighed, n + 3)
                        for k in range(2):
                            nc.tensor.matmul(sums[0:WK, 2 * c + k, :], wj[:, b, 0:WK], mask_b[:, c, k * BANK:(k + 1) * BANK],
                                             start=False, stop=False)
                            nc.tensor.matmul(sums[0:WK, 2 * c + k, :], wj[:, b, WK:2 * WK], lower[:, c, k * BANK:(k + 1) * BANK],
                                             start=False, stop=False)
                        for k in range(2):
                            last = nc.tensor.matmul(acc[:, 2 * c + k, :], xj[:, b, :], z[:, c, k * BANK:(k + 1) * BANK],
                                                    start=False, stop=False)
                        last.then_inc(used, 1)
            for k in range(4):
                nc.tensor.matmul(sums[0:WK, k, :], core.zeros_b[:, 0:WK], core.zeros_b[:, :], start=False, stop=True)
                last = nc.tensor.matmul(acc[:, k, :], core.zeros_b[:, 0:P], core.zeros_b[:, :], start=False, stop=True)
            last.then_inc(ended, 1)
            pe.wait_ge(ended, 1)


def features(core, st, half):
    nc = core.nc
    TH = NT // 2
    accS = st.sb("accS", [P, HALF])
    sumS = st.sb("sumS", [WK, HALF])
    four = st.sb("four", [P, TH, 4])
    tok = st.sb("tok", [P, 4, TH])
    feat = st.sb("feat", [P, TH, F])
    evacuated = st.sem("evacuated")
    turned = st.sem("turned")
    ready = st.sem("ready")
    stored = st.sem("stored")
    dve_own = st.sem("dve_own")
    lo = half * TH
    acc, sums = core.acc, core.sums

    with st.block() as block:
        @block.scalar
        def _(act):
            nc.scalar.activation(accS[:, :], acc[:, :, :].rearrange("p k c -> p (k c)"), ACT.Copy).then_inc(evacuated, 1)

        @block.tensor
        def _(pe):
            pe.wait_ge(evacuated, 2)
            for t in range(TH):
                nc.tensor.matmul(sums[:, 0, 4 * t:4 * t + 4], sumS[:, t * P:(t + 1) * P], core.select[:, :], start=True, stop=True)
            for t in range(TH):
                last = nc.tensor.transpose(acc[:, t // 4, (t % 4) * P:(t % 4 + 1) * P], accS[:, t * P:(t + 1) * P], core.ident[:, :])
            last.then_inc(turned, 1)

        @block.vector
        def _(dve):
            own = Chain(dve, dve_own)
            own(nc.vector.tensor_copy(sumS[:, :], sums[0:WK, :, :].rearrange("p k c -> p (k c)")))
            dve.sem_inc(evacuated, 1)
            x = core.x[:, lo:lo + TH, :]
            r, inv, rowsum = core.r[:, lo:lo + TH], core.inv_z[:, lo:lo + TH], core.half_u2[:, lo:lo + TH]
            dve.wait_ge(turned, 1)
            own(nc.vector.tensor_copy(four[:, :, :].rearrange("p t k -> p (t k)"), sums[:, 0, 0:4 * TH]))
            own(nc.vector.tensor_tensor(tok[:, 0, :], four[:, :, 2], r, ALU.mult))
            own(nc.vector.tensor_tensor(tok[:, 0, :], tok[:, 0, :], four[:, :, 0], ALU.add))
            own(nc.vector.reciprocal(inv, tok[:, 0, :]))
            own(nc.vector.tensor_tensor(tok[:, 1, :], four[:, :, 3], r, ALU.mult))
            own(nc.vector.tensor_tensor(tok[:, 1, :], tok[:, 1, :], r, ALU.mult))
            own(nc.vector.tensor_tensor(tok[:, 1, :], tok[:, 1, :], four[:, :, 1], ALU.add))
            own(nc.vector.tensor_tensor(tok[:, 1, :], tok[:, 1, :], inv, ALU.mult))
            own(nc.vector.scalar_tensor_tensor(out=rowsum, in0=tok[:, 1, :], scalar=0.5, in1=inv, op0=ALU.mult, op1=ALU.mult))
            own(nc.vector.tensor_scalar(tok[:, 3, :], rowsum, -1.0, core.coef_rest[:, 2:3], ALU.mult, ALU.add))
            own(nc.vector.tensor_tensor(feat[:, :, :], acc[:, :, :].rearrange("p k (q f) -> p (k q) f", f=F), bcast_mid(inv, F), ALU.mult))
            u = accS[:, :].rearrange("p (t f) -> p t f", f=F)
            own(nc.vector.tensor_tensor(u, x, bcast_mid(tok[:, 3, :], F), ALU.mult))
            own(nc.vector.tensor_tensor(feat[:, :, :], feat[:, :, :], u, ALU.add))
            own(nc.vector.tensor_scalar(u, feat[:, :, :], THRESH, -THRESH, ALU.min, ALU.max))
            own(nc.vector.tensor_tensor(feat[:, :, :], feat[:, :, :], u, ALU.subtract))
            dve.sem_inc(ready, 1)

        @block.sync
        def _(sp):
            sp.wait_ge(ready, 1)
            sp.dma_start(natural(core.feat_dram)[:, lo:lo + TH, :], feat[:, :, :]).then_inc(stored, 16)
            sp.wait_ge(stored, 16)


def propagate_second(core, st):
    nc = core.nc
    above = st.sb("above", [P, 2, CHUNK])
    z = st.sb("z", [P, 2, CHUNK])
    fj = st.sb("fj", [P, 2, F])
    tokj = st.sb("tokj", [P, 2, 3])
    feat_in = st.sem("feat_in")
    above_ready = st.sem("above_ready")
    weighed = st.sem("weighed")
    used = st.sem("used")
    picked = st.sem("picked")
    ended = st.sem("ended")
    acc = core.acc2
    NC = N // CHUNK

    with st.block() as block:
        @block.sync
        def _(sp):
            sp.dma_start(core.x[:, :, :], natural(core.feat_dram)).then_inc(feat_in, 16)

        @block.gpsimd
        def _(pool):
            pool.wait_ge(feat_in, 16)
            with pool.Fori(0, NT // 2) as i:
                for b in range(2):
                    j = 2 * i + b
                    pool.wait_ge(used, NC * j + 1)
                    nc.gpsimd.tensor_copy(fj[:, b, :], column(core.x, j))
                    nc.gpsimd.tensor_copy(tokj[:, b, :], column(core.token, j)).then_inc(picked, 1)

        @block.scalar
        def _(act):
            with act.Fori(0, NT // 2) as i:
                for b in range(2):
                    j = 2 * i + b
                    act.wait_ge(picked, j + 1)
                    for c in range(NC):
                        act.wait_ge(weighed, NC * j + c + 1)
                        nc.scalar.activation(above[:, c % 2, :], core.r_rows[:, c * CHUNK:(c + 1) * CHUNK], ACT.Relu,
                                             scale=tokj[:, b, LOW:LOW + 1], bias=tokj[:, b, NEG_HIGH:NEG_HIGH + 1]).then_inc(above_ready, 1)

        @block.vector
        def _(dve):
            dve.sem_inc(weighed, 2)
            with dve.Fori(0, NT // 2) as i:
                for b in range(2):
                    j = 2 * i + b
                    for c in range(NC):
                        n = NC * j + c
                        dve.wait_ge(above_ready, n + 1)
                        dve.wait_ge(used, n + 4)
                        nc.vector.scalar_tensor_tensor(out=z[:, c % 2, :], in0=above[:, c % 2, :], scalar=tokj[:, b, HIGH:HIGH + 1],
                                                       in1=column(core.mask[:, :, c * CHUNK:(c + 1) * CHUNK], j),
                                                       op0=ALU.add, op1=ALU.mult).then_inc(weighed, 1)

        @block.tensor
        def _(pe):
            pe.sem_inc(used, 5)
            for k in range(NB):
                nc.tensor.matmul(acc[:, k, :], core.zeros_b[:, 0:P], core.zeros_b[:, :], start=True, stop=False)
            with pe.Fori(0, NT // 2) as i:
                for b in range(2):
                    j = 2 * i + b
                    pe.wait_ge(picked, j + 1)
                    for c in range(NC):
                        pe.wait_ge(weighed, NC * j + c + 3)
                        for k in range(2):
                            last = nc.tensor.matmul(acc[:, 2 * c + k, :], fj[:, b, :], z[:, c % 2, k * BANK:(k + 1) * BANK],
                                                    start=False, stop=False)
                        last.then_inc(used, 1)
            for k in range(NB):
                last = nc.tensor.matmul(acc[:, k, :], core.zeros_b[:, 0:P], core.zeros_b[:, :], start=False, stop=True)
            last.then_inc(ended, 1)
            pe.wait_ge(ended, 1)


def attention_finish(core, st):
    nc, a = core.nc, core.args
    x2 = st.sb("x2", [P, NT, F])
    h0 = st.sb("h0", [P, NT, F])
    evac = st.sb("evac", [P, 2, BANK])
    gamma = st.sb("gamma", [P, NT])
    mu = st.sb("mu", [P, NT])
    k0 = st.sb("k0", [P, 2])
    part = st.sb("part", [P, 2, BANK])
    loaded = st.sem("loaded")
    evacuated = st.sem("evacuated")
    turned = st.sem("turned")
    read = st.sem("read")
    dve_own = st.sem("dve_own")
    acc = core.acc2
    coef, rest = core.coef, core.coef_rest

    def four(ap, g):
        return ap[:, bass.ds(4 * g, 4), :]

    with st.block() as block:
        @block.sync
        def _(sp):
            sp.dma_start(x2[:, :, :], natural(core.x_dram)).then_inc(loaded, 16)
            sp.dma_start(h0[:, :, :], natural(a["L1_gnn_h0"])).then_inc(loaded, 16)
            load_expert_weights(core, sp)

        @block.scalar
        def _(act):
            with act.Fori(0, NB // 2) as i:
                for b in range(2):
                    g = 2 * i + b
                    act.wait_ge(turned, g + 1)
                    nc.scalar.activation(evac[:, b, :], column(acc, g), ACT.Copy).then_inc(evacuated, 1)

        @block.tensor
        def _(pe):
            pe.sem_inc(turned, 2)
            for g in range(NB):
                pe.wait_ge(evacuated, g + 1)
                for q in range(4):
                    last = nc.tensor.transpose(acc[:, g, q * P:(q + 1) * P], evac[:, g % 2, q * P:(q + 1) * P], core.ident[:, :])
                last.then_inc(turned, 1)

        @block.vector
        def _(dve):
            own = Chain(dve, dve_own)
            own(nc.vector.tensor_tensor(k0[:, 0:1], rest[:, 1:2], coef[:, 0:1], ALU.mult))
            own(nc.vector.tensor_tensor(k0[:, 1:2], rest[:, 1:2], rest[:, 0:1], ALU.mult))
            own(nc.vector.tensor_scalar(gamma[:, :], core.half_u2[:, :], coef[:, 1:2], k0[:, 0:1], ALU.mult, ALU.add))
            own(nc.vector.tensor_scalar(mu[:, :], gamma[:, :], coef[:, 3:4], None, ALU.mult))
            own(nc.vector.tensor_scalar(mu[:, :], mu[:, :], -1.0, coef[:, 1:2], ALU.mult, ALU.add))
            own(nc.vector.tensor_tensor(mu[:, :], mu[:, :], core.inv_z[:, :], ALU.mult))
            dve.wait_ge(loaded, 32)
            with dve.Fori(0, NB // 2) as i:
                own.enter(i, 10)
                for b in range(2):
                    g = 2 * i + b
                    pt = part[:, b, :].rearrange("p (q f) -> p q f", q=4)
                    own(nc.vector.scalar_tensor_tensor(out=four(x2, g), in0=four(h0, g), scalar=k0[:, 1:2], in1=four(x2, g),
                                                       op0=ALU.mult, op1=ALU.add))
                    own(nc.vector.tensor_tensor(pt, four(core.x, g), bcast_mid(gamma[:, bass.ds(4 * g, 4)], F), ALU.mult))
                    own(nc.vector.tensor_tensor(four(x2, g), four(x2, g), pt, ALU.add))
                    dve.wait_ge(turned, g + 3)
                    own(nc.vector.tensor_tensor(pt, column(acc, g).rearrange("p (q f) -> p q f", q=4),
                                                bcast_mid(mu[:, bass.ds(4 * g, 4)], F), ALU.mult))
                    own(nc.vector.tensor_tensor(four(core.x, g), four(x2, g), pt, ALU.add))
                own.leave(NB // 2)


def graph_attention(core):
    nc = core.nc
    with core.stage("attn") as st:
        core.r_rows = st.sb("r_rows", [P, N])
        core.weigh = st.sb("weigh", [P, NT, 2 * WK], BF16)
        core.token = st.sb("token", [P, NT, 3])
        core.r = st.sb("r", [P, NT])
        with core.stage("attf") as s:
            attention_factors(core, s)
        with core.stage("att1") as outer:
            core.acc = outer.ps("acc", [P, 4, BANK])
            core.sums = outer.ps("sums", [P, 4, BANK])
            for half in range(2):
                with core.stage(f"att1p{half}") as s:
                    propagate_first(core, s, half)
                with core.stage(f"att1f{half}") as s:
                    features(core, s, half)
        core.late_psum = core.stage("late")
        core.acc2 = core.late_psum.ps("acc2", [P, NB, BANK])
        with core.stage("att2") as s:
            propagate_second(core, s)


def from_stage_two(core, upto):
    slice_attention(core)
    if upto > 3:
        graph_attention(core)
        expert_weights(core)
        with core.stage("attd") as s:
            attention_finish(core, s)


TOK = N // 64
U = 4


def expert_weights(core):
    words = core.mask[:, 0:24, :].rearrange("p t n -> p (t n)").bitcast(F32)
    size = KH * NE * (HID + 1)
    core.w_routed = words[:, 0:2 * size].rearrange("p (l k e h) -> p l k e h", l=2, k=KH, e=NE)
    at = 2 * size
    core.w_shared = words[:, at:at + 2 * KH * (HID + 1)].rearrange("p (l k h) -> p l k h", l=2, k=KH)
    at += 2 * KH * (HID + 1)
    core.w_in = words[:, at:at + HID]
    at += HID
    core.w_out = words[:, at:at + KH * F].rearrange("p (k f) -> p k f", k=KH)
    at += KH * F
    core.b_in = words[:, at:at + KH]
    core.route = core.late.sb("route", [1, N // TOK], I32)
    core.small_in = core.late.sem("small_in")
    core.weights_in = [core.late.sem(f"weights_in{l}") for l in range(2)]


def load_expert_weights(core, sp):
    nc, a = core.nc, core.args
    for dst, src in ((core.w_in, a["L1_ffn_WiT"]), (core.b_in, a["L1_ffn_bi"]),
                     (core.w_out, a["L1_ffn_WoT"].rearrange("(k p) f -> p k f", p=P)),
                     (core.route[:, :], a["L1_ffn_route_id"].unsqueeze(0)),
                     (core.w_shared, a["L1_ffn_WsT"])):
        sp.dma_start(dst, src).then_inc(core.small_in, 16)
    for l in range(2):
        sp.dma_start(core.w_routed[:, l].rearrange("p k e h -> p (k e h)"), a["L1_ffn_WrT"][:, l]).then_inc(core.weights_in[l], 16)


def routed_mlp(core, st):
    nc = core.nc
    stats = st.sb("stats", [P, NT, 6])
    mean = st.sb("mean", [P, NT])
    var_eps = st.sb("var_eps", [P, NT])
    root = st.sb("root", [P, NT])
    rstd = st.sb("rstd", [P, NT])
    w_sum = st.sb("w_sum", [P, 2, U, 2, KH, HID + 1])
    xn = st.sb("xn", [P, U, F])
    xnT = st.sb("xnT", [P, U, P])
    hT = [st.sb(f"hT{l}", [P, U, KH, P]) for l in range(3)]
    res = st.sb("res", [P, U, F])
    turn_ps = st.ps("turn_ps", [P, U, P])
    first_ps = st.ps("first_ps", [P, U, KH, P])
    layer_ps = st.ps("layer_ps", [P, U, BANK // P, P])
    out_ps = st.ps("out_ps", [P, U, F])
    stats_done = st.sem("stats_done")
    rooted = st.sem("rooted")
    w_shared_ready = st.sem("w_shared_ready")
    normed = st.sem("normed")
    turned = st.sem("turned")
    xnT_ready = st.sem("xnT_ready")
    w_ready = [st.sem(f"w_ready{l}") for l in range(2)]
    h_done = [st.sem(f"h_done{l}") for l in range(3)]
    h_ready = [st.sem(f"h_ready{l}") for l in range(3)]
    out_done = st.sem("out_done")
    res_ready = st.sem("res_ready")
    stored = st.sem("stored")
    dve_own = st.sem("dve_own")
    groups = NT // U
    PAIRS = U // 2
    SMALL = 16 * 5
    x_out = core.out.rearrange("(i q p) f -> i p q f", p=P, q=U)
    xg = core.x[:, :, :].rearrange("p (g q) f -> p g (q f)", q=U)

    def sum_weights(eng, g, l, ahead):
        expert = [eng.value_load(core.route[0:1, bass.ds(2 * U * g + u, 1)], min_val=0, max_val=NE - 1) for u in range(2 * U)]
        if not ahead:
            eng.wait_ge(core.weights_in[l], 16)
        for q in range(U):
            if ahead:
                eng.wait_ge(h_ready[l + 1], U * g - U + q + 1)
            for s in range(2):
                picked = core.w_routed[:, l, :, bass.ds(expert[2 * q + s], 1), :].rearrange("p k a h -> p k (a h)")
                ins = eng.tensor_tensor(w_sum[:, l, q, s, :, :], picked, core.w_shared[:, l, :, :], ALU.add)
            ins.then_inc(w_ready[l], 1)

    with st.block() as block:
        @block.gpsimd
        def _(pool):
            pool.wait_ge(w_shared_ready, 1)
            sum_weights(pool, 0, 1, False)
            with pool.Fori(0, groups - 1) as i:
                sum_weights(pool, i + 1, 1, True)

        @block.sync
        def _(sp):
            sp.sem_inc(stored, 16)
            with sp.Fori(0, groups) as i:
                sp.wait_ge(res_ready, i + 2)
                sp.dma_start(x_out[i], res[:, :, :]).then_inc(stored, 16)
            sp.wait_ge(stored, 16 * (groups + 1))

        @block.scalar
        def _(act):
            def copy_turned(g):
                act.wait_ge(turned, g + 2)
                nc.scalar.activation(xnT[:, :, :], turn_ps[:, :, :], ACT.Copy).then_inc(xnT_ready, 1)

            def first(g):
                for c in range(PAIRS):
                    act.wait_ge(h_done[0], PAIRS * g + c + 1)
                    for k in range(KH):
                        ins = nc.scalar.activation(hT[0][:, 2 * c:2 * c + 2, k, :], first_ps[:, 2 * c:2 * c + 2, k, :], ACT.Relu,
                                                   bias=core.b_in[:, k:k + 1])
                    ins.then_inc(h_ready[0], 1)

            def layer(g, l):
                for q in range(U):
                    act.wait_ge(h_done[l + 1], U * g + q + 1)
                    for s in range(2):
                        for k in range(KH):
                            part = slice(s * TOK, (s + 1) * TOK)
                            ins = nc.scalar.activation(hT[l + 1][:, q, k, part], layer_ps[:, q, k, part], ACT.Relu,
                                                       bias=w_sum[:, l, q, s, k, HID:HID + 1])
                    ins.then_inc(h_ready[l + 1], 1)

            act.wait_ge(stats_done, 1)
            nc.scalar.activation(root[:, :], var_eps[:, :], ACT.Sqrt).then_inc(rooted, 1)
            act.wait_ge(core.small_in, SMALL)
            copy_turned(0)
            first(0)
            with act.Fori(0, groups - 1) as i:
                layer(i, 0)
                copy_turned(i + 1)
                layer(i, 1)
                first(i + 1)
            layer(groups - 1, 0)
            layer(groups - 1, 1)

        @block.vector
        def _(dve):
            own = Chain(dve, dve_own)

            def normalise(g):
                dve.wait_ge(turned, g + 1)
                for q in range(U):
                    t = U * g + q
                    ins = nc.vector.tensor_scalar(xn[:, q, :], column(core.x, t), mean[:, bass.ds(t, 1)], rstd[:, bass.ds(t, 1)],
                                                  ALU.subtract, ALU.mult)
                ins.then_inc(normed, 1)

            def finish(g):
                dve.wait_ge(out_done, g + 1)
                dve.wait_ge(stored, 16 * (g + 1))
                nc.vector.tensor_tensor(res[:, :, :].rearrange("p q f -> p (q f)"), out_ps[:, :, :].rearrange("p q f -> p (q f)"),
                                        column(xg, g), ALU.add).then_inc(res_ready, 1)

            token_statistics(nc, dve, own, core.x, stats, mean, var_eps)
            dve.sem_inc(stats_done, 1)
            dve.sem_inc(res_ready, 1)
            dve.wait_ge(core.small_in, SMALL)
            for l in range(2):
                for k in range(KH):
                    part = core.w_shared[:, l, k, k * P:(k + 1) * P]
                    ins = nc.vector.tensor_tensor(part, part, core.ident[:, :], ALU.add)
            own(ins)
            dve.wait_ge(rooted, 1)
            own(nc.vector.reciprocal(rstd[:, :], root[:, :]))
            normalise(0)
            dve.sem_inc(w_shared_ready, 1)
            sum_weights(dve, 0, 0, False)
            with dve.Fori(0, groups - 1) as i:
                normalise(i + 1)
                sum_weights(dve, i + 1, 0, True)
                finish(i)
            finish(groups - 1)

        @block.tensor
        def _(pe):
            mm, tr = nc.tensor.matmul, nc.tensor.transpose

            def turn(g):
                pe.wait_ge(normed, g + 1)
                for q in range(U):
                    ins = tr(turn_ps[:, q, :], xn[:, q, :], core.ident[:, :])
                ins.then_inc(turned, 1)

            def first(g):
                pe.wait_ge(xnT_ready, g + 1)
                for q in range(U):
                    for k in range(KH):
                        ins = mm(first_ps[:, q, k, :], core.w_in[:, k * P:(k + 1) * P], xnT[:, q, :], start=True, stop=True)
                    if q % 2:
                        ins.then_inc(h_done[0], 1)

            def layer(g, l):
                for q in range(U):
                    pe.wait_ge(w_ready[l], U * g + q + 1)
                    pe.wait_ge(h_ready[l], U * g + q + 1 if l else PAIRS * g + q // 2 + 1)
                    for s in range(2):
                        part = slice(s * TOK, (s + 1) * TOK)
                        for m in range(KH):
                            for k in range(KH):
                                ins = mm(layer_ps[:, q, m, part], w_sum[:, l, q, s, k, m * P:(m + 1) * P], hT[l][:, q, k, part],
                                         start=k == 0, stop=k == KH - 1)
                    ins.then_inc(h_done[l + 1], 1)

            def output(g):
                pe.wait_ge(res_ready, g + 1)
                for q in range(U):
                    pe.wait_ge(h_ready[2], U * g + q + 1)
                    for k in range(KH):
                        mm(out_ps[:, q, :], hT[2][:, q, k, :], core.w_out[:, k, :], start=k == 0, stop=False)
                    ins = mm(out_ps[:, q, :], core.ones_b[:, :], core.bias3[:, HG + F:HG + 2 * F], start=False, stop=True)
                ins.then_inc(out_done, 1)

            pe.sem_inc(turned, 1)
            pe.wait_ge(core.small_in, SMALL)
            turn(0)
            first(0)
            with pe.Fori(0, groups - 1) as i:
                layer(i, 0)
                turn(i + 1)
                layer(i, 1)
                first(i + 1)
                output(i)
            layer(groups - 1, 0)
            layer(groups - 1, 1)
            output(groups - 1)


def program(nc, args, out, upto=99):
    core = Core(nc, args, out)
    core.ctx = ExitStack()
    with core.ctx, core.stage("keep") as keep:
        core.ident = keep.sb("ident", [P, P])
        core.ones = keep.sb("ones", [P, P])
        core.ones_b = keep.sb("ones_b", [P, P], BF16)
        core.zeros_b = keep.sb("zeros_b", [P, BANK], BF16)
        core.x = keep.sb("x", [P, NT, F])
        core.bias3 = keep.sb("bias3", [P, HG + 2 * F], BF16)
        core.sw_dram = nc.dram_tensor("sw_scratch", (NT // 2, P, 2 * HG), F32, kind="Internal").ap()
        core.x_dram = nc.dram_tensor("x_scratch", (N, F), F32, kind="Internal").ap()
        core.rowsum = keep.sb("rowsum", [P, NT])
        core.select = keep.sb("select", [WK, 4])
        core.coef = keep.sb("coef", [P, 5])
        core.coef_rest = keep.sb("coef_rest", [P, 5])
        core.inv_z = keep.sb("inv_z", [P, NT])
        core.half_u2 = keep.sb("half_u2", [P, NT])
        core.feat_dram = nc.dram_tensor("feat_scratch", (N, F), F32, kind="Internal").ap()
        constants(core)
        with core.stage("masked") as masked:
            core.mask = masked.sb("mask", [P, NT, N], U8)
            with core.stage("gcn") as st:
                core.gcn_cols = st.sb("cols", [P, 4, HALF])
                core.acc = st.ps("acc", [P, NB, BANK])
                with core.stage("gcnp") as sp:
                    gcn_propagate(core, sp)
                with core.stage("gcnf") as sf:
                    gcn_finish(core, sf)
            with core.stage("late") as core.late:
                if upto > 1:
                    from_stage_two(core, upto)
                if upto > 8:
                    core.late_psum.ctx.close()
                    with core.stage("mlp") as st:
                        routed_mlp(core, st)
        if upto < 9:
            dump(core)


def dump(core):
    nc = core.nc
    with core.stage("dump") as st:
        stored = st.sem("stored")
        with st.block() as block:
            @block.sync
            def _(sp):
                sp.dma_start(natural(core.out), core.x[:, :, :]).then_inc(stored, 16)
                sp.wait_ge(stored, 16)


def channel_chunks(w):
    x, b, c = w[:DI], w[DI:DI + NS], w[DI + NS:]
    return np.concatenate([x.reshape(4, P, -1).transpose(1, 0, 2), np.concatenate([b, b])[:, None],
                           np.concatenate([c, c])[:, None]], axis=1)


def with_bias(w, b):
    wT = w.reshape(w.shape[:3] + (KH, P)).transpose(4, 0, 3, 1, 2)
    bT = b.reshape(b.shape[:2] + (KH, P)).transpose(3, 0, 2, 1)
    return np.concatenate([wT, bT[..., None]], axis=-1)


def layouts(inputs):
    a = {k: np.asarray(v) for k, v in inputs.items()}
    return {
        "x": a["x"],
        "adj": a["adj"],
        "adjT": np.ascontiguousarray(a["adj"].T),
        "L0_gnn_W": a["L0_gnn_W"],
        "L0_ffn_W_x": a["L0_ffn_W_x"],
        "L0_ffn_W_sliceT": a["L0_ffn_W_slice"].T,
        "L0_ffn_b_xT": a["L0_ffn_b_x"].reshape(H, G).T,
        "L0_ffn_b_slice": a["L0_ffn_b_slice"],
        "L0_ffn_temperature": a["L0_ffn_temperature"].reshape(H),
        "L0_ffn_out_b": a["L0_ffn_out_b"],
        "L0_ffn_W_fxT": a["L0_ffn_W_fx"].T,
        "L0_ffn_b_fx": a["L0_ffn_b_fx"],
        "L0_ffn_hy_in_wT": a["L0_ffn_hy_in_w"].T,
        "conv_w": channel_chunks(a["L0_ffn_hy_conv_w"]),
        "conv_b": channel_chunks(a["L0_ffn_hy_conv_b"][:, None])[:, :, 0],
        "L0_ffn_hy_dt_bias": a["L0_ffn_hy_dt_bias"],
        "L0_ffn_hy_A_log": a["L0_ffn_hy_A_log"],
        "L0_ffn_hy_D": a["L0_ffn_hy_D"],
        "L0_ffn_hy_fcD_wT": a["L0_ffn_hy_fcD_w"].reshape(H, 4, P).transpose(2, 1, 0),
        "L0_ffn_hy_norm_w": a["L0_ffn_hy_norm_w"],
        "L0_ffn_hy_out_wT": a["L0_ffn_hy_out_w"].T,
        "L0_ffn_out_wT": a["L0_ffn_out_w"].T,
        "L1_gnn_a": a["L1_gnn_a"].reshape(2 * F),
        "L1_gnn_temp": a["L1_gnn_temp"],
        "L1_gnn_h0": a["L1_gnn_h0"],
        "L1_ffn_bo": a["L1_ffn_bo"],
        "L1_ffn_route_id": a["L1_ffn_route_id"],
        "L1_ffn_WiT": a["L1_ffn_Wi"].T,
        "L1_ffn_bi": a["L1_ffn_bi"].reshape(KH, P).T,
        "L1_ffn_WrT": with_bias(a["L1_ffn_Wr"], a["L1_ffn_br"]).reshape(P, 2, KH * NE * (HID + 1)),
        "L1_ffn_WsT": with_bias(a["L1_ffn_Ws"], a["L1_ffn_bs"])[:, :, :, 0, :],
        "L1_ffn_WoT": a["L1_ffn_Wo"].T,
    }


def kernel(**inputs):
    import concourse.bacc as _bacc
    from concourse import mybir as _mybir
    from concourse.bass_utils import run_bass_kernel_spmd as _run

    nc = _bacc.Bacc("TRN2", target_bir_lowering=False, num_devices=1)
    arrays, args = {}, {}
    for name, a in layouts(inputs).items():
        a = np.ascontiguousarray(a)
        arrays[f"in_{name}"] = a
        args[name] = nc.dram_tensor(f"in_{name}", a.shape, _mybir.dt.from_np(a.dtype), kind="ExternalInput").ap()
    out = nc.dram_tensor("out", (N, F), _mybir.dt.float32, kind="ExternalOutput").ap()
    program(nc, args, out)
    r = _run(nc, [arrays], core_ids=[0])
    return r.results[0]["out"]
```

```python
from contextlib import ExitStack

import numpy as np

import concourse.bass as bass
from concourse import mybir

F32 = mybir.dt.float32
BF16 = mybir.dt.bfloat16
U8 = mybir.dt.uint8
I32 = mybir.dt.int32
ALU = mybir.AluOpType
ACT = mybir.ActivationFunctionType
AX = mybir.AxisListType
RMAX = bass.bass_isa.ReduceOp.max

P = 128
N = 4096
F = 128
NT = N // P
BANK = 512
NB = N // BANK
HALF = N // 2
EPS = 1e-5
H = 8
G = 64
HG = H * G
DI = 512
NS = 64
NPROJ = 2 * DI + 2 * NS + 2 * H
CH = 6
NE = 16
HID = 256
KH = HID // P
THRESH = 1e-6
SLOPE = 0.2
A_LOG_CAP = 69.0


class Chain:

    def __init__(self, eng, sem):
        self.eng, self.sem, self.n, self.turn, self.start = eng, sem, 0, 0, 0

    def __call__(self, ins):
        self.n += 1
        ins.then_inc(self.sem, 1)
        self.eng.wait_ge(self.sem, self.turn + self.n)

    def enter(self, i, per):
        self.start, self.per, self.turn = self.n, per, i * per

    def leave(self, turns):
        assert self.n - self.start == self.per, (self.n - self.start, self.per)
        self.n, self.turn = self.start + self.per * turns, 0


class Core:

    def __init__(self, nc, args, out):
        self.nc, self.args, self.out = nc, args, out

    def stage(self, name):
        return Stage(self, name)


class Stage:

    def __init__(self, core, name):
        self.core, self.nc, self.name, self.ctx = core, core.nc, name, ExitStack()

    def __enter__(self):
        return self

    def __exit__(self, *a):
        return self.ctx.__exit__(*a)

    def sb(self, name, shape, dt=F32):
        return self.ctx.enter_context(self.nc.sbuf_tensor(f"{self.name}_{name}", shape, dt))

    def ps(self, name, shape, dt=F32):
        return self.ctx.enter_context(self.nc.psum_tensor(f"{self.name}_{name}", shape, dt))

    def sem(self, name):
        return self.core.ctx.enter_context(self.nc.semaphore(f"{self.name}_{name}"))

    def block(self):
        return self.nc.Block()


def natural(ap):
    return ap.rearrange("(t p) f -> p t f", p=P)


def bcast_mid(ap, n):
    return ap.unsqueeze(2).to_broadcast([ap.shape[0], ap.shape[1], n])


def bcast_row(ap, n):
    return ap.unsqueeze(1).to_broadcast([ap.shape[0], n, ap.shape[1]])


def column(ap, t):
    return ap[:, bass.ds(t, 1), :].rearrange("p a f -> p (a f)")


def token_statistics(nc, dve, own, stats, mean, var_eps, x=None):
    if x is not None:
        with dve.Fori(0, NT // 4) as i:
            own.enter(i, 1)
            for b in range(4):
                t = 4 * i + b
                last = nc.vector.bn_stats(stats[:, bass.ds(t, 1), :], x[:, bass.ds(t, 1), :])
            own(last)
            own.leave(NT // 4)
    mean_e, m2_e, mean_o, m2_o = (stats[:, :, k] for k in (1, 2, 4, 5))
    own(nc.vector.tensor_tensor(mean[:, :], mean_e, mean_o, ALU.add))
    nc.vector.tensor_tensor(mean_o, mean_e, mean_o, ALU.subtract)
    own(nc.vector.tensor_tensor(m2_e, m2_e, m2_o, ALU.add))
    nc.vector.tensor_scalar(mean[:, :], mean[:, :], 0.5, None, ALU.mult)
    own(nc.vector.scalar_tensor_tensor(out=m2_o, in0=mean_o, scalar=F / 4, in1=mean_o, op0=ALU.mult, op1=ALU.mult))
    own(nc.vector.tensor_tensor(m2_e, m2_e, m2_o, ALU.add))
    own(nc.vector.tensor_scalar(var_eps[:, :], m2_e, 1.0 / F, EPS, ALU.mult, ALU.add))


def constants(core, pool, made):
    nc = core.nc
    nc.gpsimd.memset(core.ident[:, :], 0.0).then_inc(made, 1)
    nc.gpsimd.memset(core.select[:, :, :], 0.0).then_inc(made, 1)
    pool.wait_ge(made, 2)
    nc.gpsimd.affine_select(out=core.ident[:, :], in_=core.ident[:, :], compare_op=ALU.not_equal,
                            fill=1.0, base=0, pattern=[[-1, P]], channel_multiplier=1).then_inc(made, 1)
    for g in range(4):
        part = core.select[32 * g:32 * g + 32, g // 2, :]
        nc.gpsimd.memset(part, 1.0).then_inc(made, 1)
        pool.wait_ge(made, 3 * g + 4)
        nc.gpsimd.affine_select(out=part, in_=part, compare_op=ALU.is_ge,
                                fill=0.0, base=0, pattern=[[-3, 4]], channel_multiplier=1).then_inc(made, 1)
        pool.wait_ge(made, 3 * g + 5)
        nc.gpsimd.affine_select(out=part, in_=part, compare_op=ALU.is_ge,
                                fill=0.0, base=2, pattern=[[3, 4]], channel_multiplier=-1).then_inc(made, 1)
    pool.wait_ge(made, 15)


def split3(nc, own, parts, src, rest):
    own(nc.vector.tensor_copy(parts[0], src))
    own(nc.vector.tensor_tensor(rest, src, parts[0], ALU.subtract))
    own(nc.vector.tensor_copy(parts[1], rest))
    own(nc.vector.tensor_tensor(rest, rest, parts[1], ALU.subtract))
    own(nc.vector.tensor_copy(parts[2], rest))


class SliceWeights:

    def __init__(self, core, st):
        self.core = core
        words = core.mask[:, NT - 4:NT, :].rearrange("p t n -> p (t n)").bitcast(F32)
        at = 0

        def take(rows, n):
            nonlocal at
            at += n
            return words[0:rows, at - n:at]

        width = HG + 2 * F
        self.w_x = take(G, H * F).rearrange("p (h f) -> p h f", h=H)
        self.w_sliceT = take(G, G)
        self.b_xT = take(G, H)
        self.b_slice = take(1, G)
        self.temp = take(P, H)
        self.r_temp = take(P, H)
        self.row = take(1, width)
        self.rest = take(1, width)
        self.parts = take(1, 3 * width // 2).bitcast(BF16).rearrange("p (k n) -> p k n", k=3)
        self.loaded = st.sem("slice_loaded")
        self.multiplied = st.sem("slice_multiplied")
        self.read = st.sem("slice_read")
        self.split = st.sem("slice_split")
        self.moved = st.sem("slice_moved")

    def load(self, sp):
        a = self.core.args
        for dst, src in ((self.w_x, a["L0_ffn_W_x"].rearrange("(h p) f -> p h f", p=G)), (self.w_sliceT, a["L0_ffn_W_sliceT"]),
                         (self.b_xT, a["L0_ffn_b_xT"]), (self.b_slice, a["L0_ffn_b_slice"].unsqueeze(0)),
                         (self.temp, a["L0_ffn_temperature"].partition_broadcast(P)),
                         (self.row[:, HG:HG + F], a["L0_ffn_out_b"].unsqueeze(0)),
                         (self.row[:, HG + F:HG + 2 * F], a["L1_ffn_bo"].unsqueeze(0))):
            sp.dma_start(dst, src).then_inc(self.loaded, 16)

    def move(self, queue):
        queue.wait_ge(self.split, 1)
        for k in range(3):
            queue.dma_start(self.core.bias3[k:k + 1, :], self.parts[:, k, :]).then_inc(self.moved, 16)
        queue.wait_ge(self.moved, 48)

    def multiply(self, pe):
        nc, acc = self.core.nc, self.core.acc
        pe.wait_ge(self.loaded, 16 * 7)
        for h in range(H):
            nc.tensor.matmul(acc[:, 0, h * G:(h + 1) * G], self.w_x[:, h, :], self.w_sliceT, start=True, stop=True)
        for h in range(H):
            last = nc.tensor.matmul(acc[0:1, 1, h * G:(h + 1) * G], self.b_xT[:, h:h + 1], self.w_sliceT, start=True, stop=True)
        last.then_inc(self.multiplied, 1)

    def finish(self, dve, own):
        core, nc, acc, row = self.core, self.core.nc, self.core.acc, self.row
        own(nc.vector.memset(core.bias3[:, :], 0.0))
        dve.wait_ge(self.loaded, 16 * 7)
        own(nc.vector.tensor_scalar(self.temp, self.temp, 1e-6, None, ALU.max))
        own(nc.vector.reciprocal(self.r_temp, self.temp))
        dve.wait_ge(self.multiplied, 1)
        nc.vector.tensor_tensor(core.wc[:, :].rearrange("p (h g) -> p h g", h=H),
                                acc[:, 0, :].rearrange("p (h g) -> p h g", h=H), bcast_mid(self.r_temp, G), ALU.mult)
        bc = row[:, 0:HG].rearrange("p (h g) -> p h g", h=H)
        own(nc.vector.tensor_tensor(bc, acc[0:1, 1, :].rearrange("p (h g) -> p h g", h=H), bcast_row(self.b_slice, H), ALU.add))
        dve.sem_inc(self.read, 1)
        own(nc.vector.tensor_tensor(bc, bc, bcast_mid(self.r_temp[0:1, :], G), ALU.mult))
        split3(nc, own, [self.parts[:, k, :] for k in range(3)], row, self.rest)
        dve.sem_inc(self.split, 1)


def gcn_propagate(core, st):
    nc = core.nc
    adj_rows = core.args["adj"].rearrange("(t p) (h c) -> t h p c", p=P, h=2)
    adj_cols = core.args["adjT"].rearrange("(t p) (h c) -> t h p c", p=P, h=2)
    rows = st.sb("rows", [P, 2, HALF])
    cols = st.sb("cols", [P, 4, HALF])
    slices = SliceWeights(core, st)
    made = st.sem("made")
    zeros_made = st.sem("zeros_made")
    x_in = st.sem("x_in")
    half_sum = st.sb("half_sum", [P, 2, 2])
    mean = st.sb("mean", [P, NT])
    var_eps = st.sb("var_eps", [P, NT])
    total = st.sb("total", [P, 2])
    var_sum = st.sb("var_sum", [P, 2])
    root = st.sb("root", [P, 2])
    scale = st.sb("scale", [P, 2])
    y = st.sb("y", [P, 2, F])
    rows_in = [st.sem(f"rows_in{h}") for h in range(2)]
    cols_in = [st.sem(f"cols_in{h}") for h in range(4)]
    rows_summed = st.sem("rows_summed")
    cols_masked = st.sem("cols_masked")
    cols_used = st.sem("cols_used")
    var_ready = st.sem("var_ready")
    root_ready = st.sem("root_ready")
    y_ready = st.sem("y_ready")
    dve_own = st.sem("dve_own")
    pe_own = st.sem("pe_own")

    with st.block() as block:
        @block.gpsimd
        def _(pool):
            constants(core, pool, made)
            slices.move(pool)

        @block.sync
        def _(sp):
            sp.dma_start(core.x[:, :, :], natural(core.args["x"])).then_inc(x_in, 16)
            slices.load(sp)
            with sp.Fori(0, NT // 2) as i:
                for b in range(2):
                    t = 2 * i + b
                    for h in range(2):
                        sp.wait_ge(rows_summed, 2 * t + h + 1)
                        sp.dma_start(rows[:, h, :], adj_rows[t, h]).then_inc(rows_in[h], 16)
                    for h in range(2):
                        sp.wait_ge(cols_masked, 2 * t + h + 1)
                        sp.wait_ge(cols_used, 2 * t + h + 1)
                        sp.dma_start(cols[:, 2 * b + h, :], adj_cols[t, h]).then_inc(cols_in[2 * b + h], 16)

        @block.scalar
        def _(act):
            act.sem_inc(rows_summed, 2)
            with act.Fori(0, NT // 2) as i:
                for b in range(2):
                    t = 2 * i + b
                    for h in range(2):
                        act.wait_ge(rows_in[h], 16 * (t + 1))
                        nc.scalar.activation(rows[:, h, :], rows[:, h, :], ACT.Copy,
                                             accum_out=half_sum[:, b, h:h + 1]).then_inc(rows_summed, 1)
                    act.wait_ge(var_ready, t + 1)
                    nc.scalar.activation(root[:, b:b + 1], var_sum[:, b:b + 1], ACT.Sqrt).then_inc(root_ready, 1)

        @block.vector
        def _(dve):
            own = Chain(dve, dve_own)
            dve.sem_inc(cols_masked, 4)
            own(nc.vector.memset(core.zeros_b[:, :], 0.0))
            dve.sem_inc(zeros_made, 1)
            own(nc.vector.memset(core.ones_b[:, :], 1.0))
            slices.finish(dve, own)
            dve.wait_ge(x_in, 16)
            token_statistics(nc, dve, own, core.stats, mean, var_eps, core.x)
            dve.wait_ge(slices.moved, 48)
            with dve.Fori(0, NT // 2) as i:
                own.enter(i, 4)
                for b in range(2):
                    t = 2 * i + b
                    dve.wait_ge(rows_summed, 2 * t + 4)
                    own(nc.vector.tensor_tensor(total[:, b:b + 1], half_sum[:, b, 0:1], half_sum[:, b, 1:2], ALU.add))
                    nc.vector.tensor_copy(core.rowsum[:, bass.ds(t, 1)], total[:, b:b + 1])
                    nc.vector.tensor_tensor(var_sum[:, b:b + 1], var_eps[:, bass.ds(t, 1)], total[:, b:b + 1],
                                            ALU.mult).then_inc(var_ready, 1)
                    dve.wait_ge(root_ready, t + 1)
                    own(nc.vector.reciprocal(scale[:, b:b + 1], root[:, b:b + 1]))
                    dve.wait_ge(cols_used, 2 * t + 2)
                    nc.vector.tensor_scalar(y[:, b, :], column(core.x, t), mean[:, bass.ds(t, 1)],
                                            scale[:, b:b + 1], ALU.subtract, ALU.mult).then_inc(y_ready, 1)
                    for h in range(2):
                        dve.wait_ge(cols_in[2 * b + h], 16 * (i + 1))
                        nc.vector.tensor_scalar(core.mask[:, bass.ds(t, 1), h * HALF:(h + 1) * HALF].rearrange("p a f -> p (a f)"),
                                                cols[:, 2 * b + h, :], 0.0, None, ALU.is_gt).then_inc(cols_masked, 1)
                own.leave(NT // 2)

        @block.tensor
        def _(pe):
            acc = core.acc
            pe.sem_inc(cols_used, 4)
            slices.multiply(pe)
            pe.wait_ge(slices.read, 1)
            pe.wait_ge(zeros_made, 1)
            for c in range(NB):
                nc.tensor.matmul(acc[:, c, :], core.zeros_b[:, 0:P], core.zeros_b[:, :], start=True, stop=False)
            with pe.Fori(0, NT // 2) as i:
                for b in range(2):
                    t = 2 * i + b
                    pe.wait_ge(y_ready, t + 1)
                    for h in range(2):
                        pe.wait_ge(cols_in[2 * b + h], 16 * (i + 1))
                        for c in range(NB // 2):
                            last = nc.tensor.matmul(acc[:, h * (NB // 2) + c, :], y[:, b, :],
                                                    cols[:, 2 * b + h, c * BANK:(c + 1) * BANK], start=False, stop=False)
                        last.then_inc(cols_used, 1)
            for c in range(NB):
                last = nc.tensor.matmul(acc[:, c, :], core.zeros_b[:, 0:P], core.zeros_b[:, :], start=False, stop=True)
            last.then_inc(pe_own, 1)
            pe.wait_ge(pe_own, 1)


def gcn_finish(core, st):
    nc = core.nc
    evac = st.sb("evac", [P, 2, BANK])
    act_out = st.sb("act_out", [P, 2, BANK])
    w = st.sb("w", [F, F])
    d_root = st.sb("d_root", [P, NT])
    d = st.sb("d", [P, NT])
    w_in = st.sem("w_in")
    rooted = st.sem("rooted")
    d_ready = st.sem("d_ready")
    evacuated = st.sem("evacuated")
    projected = st.sem("projected")
    scaled = st.sem("scaled")
    added = st.sem("added")
    xg = core.x[:, :, :].rearrange("p (g q) f -> p g (q f)", q=4)

    with st.block() as block:
        @block.sync
        def _(sp):
            sp.dma_start(w[:, :], core.args["L0_gnn_W"]).then_inc(w_in, 16)

        @block.scalar
        def _(act):
            nc.scalar.activation(d_root[:, :], core.rowsum[:, :], ACT.Sqrt).then_inc(rooted, 1)

            def evacuate(k, b):
                act.wait_ge(projected, k + 1)
                nc.scalar.activation(evac[:, b, :], core.acc[:, bass.ds(k, 1), :].rearrange("p a f -> p (a f)"),
                                     ACT.Copy).then_inc(evacuated, 1)

            def scale(k, b):
                act.wait_ge(projected, k + 3)
                act.wait_ge(added, k + 1)
                for q in range(4):
                    ins = nc.scalar.activation(act_out[:, b, q * P:(q + 1) * P],
                                               core.acc[:, bass.ds(k, 1), q * P:(q + 1) * P].rearrange("p a f -> p (a f)"),
                                               ACT.Relu, scale=d[:, bass.ds(4 * k + q, 1)])
                ins.then_inc(scaled, 1)

            evacuate(0, 0)
            evacuate(1, 1)
            act.wait_ge(d_ready, 1)
            with act.Fori(0, NB // 2 - 1) as i:
                for b in range(2):
                    k = 2 * i + b
                    scale(k, b)
                    evacuate(k + 2, b)
            for b in range(2):
                scale(NB - 2 + b, b)

        @block.tensor
        def _(pe):
            pe.sem_inc(projected, 2)
            pe.wait_ge(w_in, 16)
            with pe.Fori(0, NB // 2) as i:
                for b in range(2):
                    k = 2 * i + b
                    pe.wait_ge(evacuated, k + 1)
                    for q in range(4):
                        last = nc.tensor.matmul(core.acc[:, bass.ds(k, 1), q * P:(q + 1) * P].rearrange("p a f -> p (a f)"),
                                                evac[:, b, q * P:(q + 1) * P], w[:, :], start=True, stop=True)
                    last.then_inc(projected, 1)

        @block.vector
        def _(dve):
            dve.sem_inc(added, 2)
            dve.wait_ge(rooted, 1)
            nc.vector.reciprocal(d[:, :], d_root[:, :]).then_inc(d_ready, 1)
            with dve.Fori(0, NB // 2) as i:
                for b in range(2):
                    k = 2 * i + b
                    dve.wait_ge(scaled, k + 1)
                    xk = xg[:, bass.ds(k, 1), :].rearrange("p a f -> p (a f)")
                    nc.vector.tensor_tensor(xk, xk, act_out[:, b, :], ALU.add).then_inc(added, 1)
                    dve.wait_ge(added, k + 3)
                    for q in range(4):
                        nc.vector.bn_stats(core.stats[:, bass.ds(4 * k + q, 1), :], core.x[:, bass.ds(4 * k + q, 1), :])


Q = 4


def slice_gather(core, st):
    nc = core.nc
    mean = st.sb("mean", [P, NT])
    var_eps = st.sb("var_eps", [P, NT])
    root = st.sb("root", [P, NT])
    rstd = st.sb("rstd", [P, NT])
    xn = st.sb("xn", [P, 4, 2, F + 2])
    xnT = st.sb("xnT", [P, 2, 2, P])
    e = st.sb("e", [P, 2, 2 * HG])
    sw = st.sb("sw", [P, 2, 2 * HG])
    neg_top = st.sb("neg_top", [P, 2, 2 * H])
    total = st.sb("total", [P, 2, 2 * H])
    inv = st.sb("inv", [P, 2, 2 * H])
    xnT_ps = st.ps("xnT_ps", [P, 2, 4, P])
    logits = st.ps("logits", [P, 2, 2, HG])
    gath = st.ps("gath", [P, 2, BANK])
    rooted = st.sem("rooted")
    normed = st.sem("normed")
    turned = st.sem("turned")
    xnT_ready = st.sem("xnT_ready")
    logits_done = st.sem("logits_done")
    top_ready = st.sem("top_ready")
    exped = st.sem("exped")
    sw_ready = st.sem("sw_ready")
    gathered_pair = st.sem("gathered_pair")
    sw_stored = [st.sem(f"sw_stored{k}") for k in range(2)]
    gath_done = st.sem("gath_done")
    x_stored = st.sem("x_stored")
    dve_own = st.sem("dve_own")
    pairs = NT // 2
    PH = 2 * H

    def region(g):
        return gath[:, g // 2, (g % 2) * 256:(g % 2) * 256 + F + 2]

    def heads(ap):
        return ap.rearrange("p (h g) -> p h g", g=G)

    def steps(eng, step, own=None, per=0):
        for k in range(2):
            step(k, k)
        with eng.Fori(0, (pairs - 4) // 4) as i:
            if own:
                own.enter(i, 4 * per)
            for b in range(4):
                step(4 * i + (b + 2), (b + 2) % 4, True)
            if own:
                own.leave((pairs - 4) // 4)
        for k in range(pairs - 2, pairs + 2):
            step(k, k % 4)

    with st.block() as block:
        @block.sync
        def _(sp):
            for b in range(2):
                sp.sem_inc(sw_stored[b], 16)
            sp.dma_start(natural(core.x_dram), core.x[:, :, :]).then_inc(x_stored, 16)
            core.mixer_weights.load(sp, core.args)
            with sp.Fori(0, pairs // 2) as i:
                for b in range(2):
                    u = 2 * i + b
                    sp.wait_ge(sw_ready, u + 3)
                    sp.dma_start(core.sw_dram[bass.ds(u, 1), :, :].rearrange("a p f -> p (a f)"), sw[:, b, :]).then_inc(sw_stored[b], 16)
            for b in range(2):
                sp.wait_ge(sw_stored[b], 16 * (pairs // 2 + 1))
            sp.wait_ge(x_stored, 16)

        @block.scalar
        def _(act):
            def copy_turned(u, b):
                act.wait_ge(turned, u + 1)
                nc.scalar.activation(xnT[:, b, :, :], xnT_ps[:, b, 0:2, :], ACT.Copy).then_inc(xnT_ready, 1)

            def exponentials(u, b):
                act.wait_ge(top_ready, u + 1)
                act.wait_ge(sw_ready, u + 1)
                for k in range(PH):
                    ins = nc.scalar.activation(e[:, b, k * G:(k + 1) * G], logits[:, b, k // H, (k % H) * G:(k % H + 1) * G],
                                               ACT.Exp, bias=neg_top[:, b, k:k + 1])
                ins.then_inc(exped, 1)

            def step(k, m, inside=False):
                if inside or k + 1 < pairs:
                    copy_turned(k + 1, (m + 1) % 2)
                if inside or k < pairs:
                    exponentials(k, m % 2)

            act.wait_ge(rooted, 1)
            nc.scalar.activation(root[:, :], var_eps[:, :], ACT.Sqrt).then_inc(rooted, 1)
            copy_turned(0, 0)
            steps(act, step)

        @block.vector
        def _(dve):
            own = Chain(dve, dve_own)

            def normalise(u, m):
                dve.wait_ge(gathered_pair, u + 1)
                for q in range(2):
                    t = 2 * u + q
                    ins = nc.vector.tensor_scalar(xn[:, m, q, 0:F], column(core.x, t), mean[:, bass.ds(t, 1)],
                                                  rstd[:, bass.ds(t, 1)], ALU.subtract, ALU.mult)
                ins.then_inc(normed, 1)

            def maximum(u, b):
                dve.wait_ge(logits_done, u + 1)
                own(nc.vector.tensor_reduce(neg_top[:, b, :], heads(logits[:, b, :, :].rearrange("p a f -> p (a f)")), AX.X, ALU.max))
                nc.vector.tensor_scalar(neg_top[:, b, :], neg_top[:, b, :], -1.0, None, ALU.mult).then_inc(top_ready, 1)

            def divide(u, b):
                dve.wait_ge(exped, u + 3)
                own(nc.vector.tensor_reduce(total[:, b, :], heads(e[:, b, :]), AX.X, ALU.add))
                own(nc.vector.reciprocal(inv[:, b, :], total[:, b, :]))
                dve.wait_ge(sw_stored[b], 8 * u + 16 - 8 * b)
                dve.wait_ge(gathered_pair, u + 3)
                nc.vector.tensor_tensor(heads(sw[:, b, :]), heads(e[:, b, :]), bcast_mid(inv[:, b, :], G), ALU.mult).then_inc(sw_ready, 1)

            def step(k, m, inside=False):
                if inside or k + 1 < pairs:
                    normalise(k + 1, (m + 1) % 4)
                if inside or k < pairs:
                    maximum(k, m % 2)
                if inside or 1 <= k <= pairs:
                    divide(k - 1, (m + 1) % 2)

            dve.sem_inc(sw_ready, 2)
            token_statistics(nc, dve, own, core.stats, mean, var_eps)
            dve.sem_inc(rooted, 1)
            dve.wait_ge(rooted, 2)
            own(nc.vector.reciprocal(rstd[:, :], root[:, :]))
            own(nc.vector.memset(xn[:, :, :, F:F + 2], 1.0))
            normalise(0, 0)
            steps(dve, step, own, 3)
            dve.wait_ge(gath_done, 1)
            for g in range(4):
                ins = nc.vector.tensor_copy(core.gathered[:, g, :], region(g)[:, 0:F + 1])
            own(ins)

        @block.tensor
        def _(pe):
            def turn(u, m):
                pe.wait_ge(normed, u + 1)
                for q in range(2):
                    ins = nc.tensor.transpose(xnT_ps[:, m % 2, q, :], xn[:, m, q, 0:F], core.ident[:, :])
                ins.then_inc(turned, 1)

            def products(u, b):
                pe.wait_ge(xnT_ready, u + 1)
                pe.wait_ge(exped, u + 1)
                for q in range(2):
                    nc.tensor.matmul(logits[:, b, q, :], xnT[:, b, q, :], core.wc[:, :], start=True, stop=False)
                    ins = nc.tensor.matmul(logits[:, b, q, :], core.ones_b[:, :], core.bias3[:, 0:HG], start=False, stop=True)
                ins.then_inc(logits_done, 1)

            def gather(u, m):
                pe.wait_ge(sw_ready, u + 3)
                for q in range(2):
                    for g in range(4):
                        at = q * HG + g * P
                        ins = nc.tensor.matmul(region(g), sw[:, m % 2, at:at + P], xn[:, m, q, :], start=False, stop=False)
                ins.then_inc(gathered_pair, 1)

            def step(k, m, inside=False):
                if inside or k < pairs:
                    products(k, m % 2)
                if inside or k + 1 < pairs:
                    turn(k + 1, (m + 1) % 4)
                if inside or k >= 2:
                    gather(k - 2, (m + 2) % 4)

            pe.sem_inc(gathered_pair, 4)
            pe.sem_inc(exped, 2)
            for k in range(2):
                nc.tensor.matmul(gath[:, k, :], core.zeros_b[:, 0:P], core.zeros_b[:, :], start=True, stop=False)
            turn(0, 0)
            steps(pe, step)
            for k in range(2):
                last = nc.tensor.matmul(gath[:, k, :], core.zeros_b[:, 0:P], core.zeros_b[:, :], start=False, stop=True)
            last.then_inc(gath_done, 1)


class MixerWeights:

    LOADS = 12

    def __init__(self, st):
        self.in_wT = st.sb("in_wT", [P, 4, NPROJ])
        self.w_fxT = st.sb("w_fxT", [P, DI])
        self.b_fx = st.sb("b_fx", [1, DI])
        self.conv_w = st.sb("conv_w", [P, CH, 3])
        self.conv_b = st.sb("conv_b", [P, CH])
        self.dt_bias = st.sb("dt_bias", [G, 2, H])
        self.a_neg = st.sb("a_neg", [G, H])
        self.d_skip = st.sb("d_skip", [G, H])
        self.fcdT = st.sb("fcdT", [P, 4, H])
        self.norm_w = st.sb("norm_w", [G, DI])
        self.out_wT = st.sb("out_wT", [P, 4, F])
        self.loaded = st.sem("mixer_loaded")

    def load(self, sp, a):
        loads = ((self.w_fxT[:, :], a["L0_ffn_W_fxT"]), (self.b_fx[:, :], a["L0_ffn_b_fx"].unsqueeze(0)),
                 (self.in_wT[:, :, :], a["L0_ffn_hy_in_wT"].rearrange("(k p) n -> p k n", p=P)),
                 (self.conv_w[:, :, :], a["conv_w"]), (self.conv_b[:, :], a["conv_b"]),
                 (self.dt_bias[:, 0, :], a["L0_ffn_hy_dt_bias"].partition_broadcast(G)),
                 (self.dt_bias[:, 1, :], a["L0_ffn_hy_dt_bias"].partition_broadcast(G)),
                 (self.a_neg[:, :], a["L0_ffn_hy_A_log"].partition_broadcast(G)),
                 (self.d_skip[:, :], a["L0_ffn_hy_D"].partition_broadcast(G)),
                 (self.fcdT[:, :, :], a["L0_ffn_hy_fcD_wT"]),
                 (self.norm_w[:, :], a["L0_ffn_hy_norm_w"].partition_broadcast(G)),
                 (self.out_wT[:, :, :], a["L0_ffn_out_wT"].rearrange("(k p) n -> p k n", p=P)))
        assert len(loads) == self.LOADS
        for dst, src in loads:
            sp.dma_start(dst, src).then_inc(self.loaded, 16)


def mixer(core, st):
    nc, a = core.nc, core.args
    w = core.mixer_weights
    in_wT, w_fxT, b_fx, conv_w, conv_b, dt_bias, a_neg, d_skip, fcdT, norm_w, out_wT = (
        w.in_wT, w.w_fxT, w.b_fx, w.conv_w, w.conv_b, w.dt_bias, w.a_neg, w.d_skip, w.fcdT, w.norm_w, w.out_wT)
    spare = core.x[:, :, :].rearrange("p t f -> p (t f)")
    hy_outT = spare[:, 0:4 * DI].rearrange("p (k n) -> p k n", k=4)
    mix = spare[0:G, 4 * DI:5 * DI].rearrange("p (h t) -> p h t", h=H)
    steps = spare[0:G, 5 * DI:7 * DI].rearrange("p (d h t) -> p d h t", d=2, h=H)
    y = spare[0:G, 7 * DI:8 * DI]
    gT = st.sb("gT", [P, 4, P])
    ratio_row = st.sb("ratio_row", [1, 4, P])
    inv = st.sb("inv", [P, 4])
    scaled = st.sb("scaled", [P, 4, F + 1])
    stT = st.sb("stT", [P, 4, G])
    xpad = st.sb("xpad", [P, CH, G + 2])
    tap = st.sb("tap", [P, CH, G])
    conv = st.sb("conv", [P, CH, G])
    act_e = tap
    xc = st.sb("xc", [P, CH, G])
    c_pad = st.sb("c_pad", [G, G + 2])
    x_nat = st.sb("x_nat", [G, DI])
    z = st.sb("z", [G, DI])
    z_e = st.sb("z_e", [G, DI])
    dt_raw = st.sb("dt_raw", [G, 2 * H])
    dt_u = st.sb("dt_u", [G, 2 * H])
    dt_l = st.sb("dt_l", [G, 2 * H])
    dt_p = st.sb("dt_p", [G, 2 * H])
    dt = st.sb("dt", [G, 2 * H])
    gt = st.sb("gt", [G, G])
    lt = st.sb("lt", [G, G])
    decay = st.sb("decay", [G, 2, H, G])
    cb = st.sb("cb", [G, 2, G])
    gate = st.sb("gate", [G, H])
    sq = st.sb("sq", [G, 2])
    ygT = st.sb("ygT", [P, 4, G])
    blocks = gT
    ps = [st.ps(f"ps{k}", [P, BANK]) for k in range(8)]
    loaded = st.sem("loaded")
    masks = st.sem("masks")
    to_pe = st.sem("to_pe")
    from_pe = st.sem("from_pe")
    to_act = st.sem("to_act")
    from_act = st.sem("from_act")
    dve_own = st.sem("dve_own")

    with st.block() as block:
        @block.sync
        def _(sp):
            sp.dma_start(hy_outT[:, :, :], a["L0_ffn_hy_out_wT"].rearrange("(k p) n -> p k n", p=P)).then_inc(loaded, 16)

        @block.gpsimd
        def _(pool):
            nc.gpsimd.memset(gt[:, :], 0.0)
            nc.gpsimd.memset(lt[:, :], 0.0).then_inc(masks, 1)
            pool.wait_ge(masks, 1)
            nc.gpsimd.affine_select(out=gt[:, :], in_=gt[:, :], compare_op=ALU.is_ge, fill=1.0,
                                    base=0, pattern=[[1, G]], channel_multiplier=-1)
            nc.gpsimd.affine_select(out=lt[:, :], in_=lt[:, :], compare_op=ALU.is_ge, fill=1.0,
                                    base=0, pattern=[[-1, G]], channel_multiplier=1).then_inc(masks, 1)

        @block.vector
        def _(dve):
            own = Chain(dve, dve_own)
            own(nc.vector.memset(xpad[:, :, :], 0.0))
            own(nc.vector.memset(c_pad[:, :], 0.0))
            own(nc.vector.memset(conv[:, :, :], 0.0))
            snorm = core.gathered[:, :, F]
            own(nc.vector.tensor_scalar(inv[:, :], snorm, EPS, None, ALU.add))
            own(nc.vector.reciprocal(inv[:, :], inv[:, :]))
            own(nc.vector.tensor_tensor(scaled[:, :, :], core.gathered[:, :, :], bcast_mid(inv[:, :], F + 1), ALU.mult))
            dve.sem_inc(to_pe, 1)
            dve.wait_ge(from_pe, 1)
            nc.vector.tensor_copy(gT[:, :, :], ps[0][:, :].rearrange("p (k g) -> p k g", k=4))
            own(nc.vector.tensor_copy(ratio_row[:, :, :], ps[1][0:1, :].rearrange("p (k g) -> p k g", k=4)))
            dve.sem_inc(to_pe, 1)
            dve.wait_ge(from_pe, 2)
            own(nc.vector.memset(blocks[:, :, :], 0.0))
            v = ps[2][:, :].rearrange("p (k g) -> p k g", k=4)
            nc.vector.tensor_copy(stT[0:G, :, :], v[0:G, :, 0:G])
            own(nc.vector.tensor_copy(stT[G:P, :, :], v[G:P, :, G:P]))
            dve.sem_inc(to_pe, 1)
            dve.wait_ge(w.loaded, 16 * w.LOADS)
            dve.wait_ge(from_pe, 3)
            nc.vector.tensor_copy(z[:, :], ps[3][0:G, :])
            nc.vector.tensor_tensor(dt_raw[:, :], ps[4][0:G, 0:2 * H], dt_bias[:, :, :].rearrange("p a h -> p (a h)"), ALU.add)
            pre = ps[5][:, 0:CH * G].rearrange("p (c t) -> p c t", c=CH)
            nc.vector.tensor_scalar(a_neg[:, :], a_neg[:, :], A_LOG_CAP, None, ALU.min)
            nc.vector.tensor_copy(xpad[:, 0:4, 2:G + 2], pre[:, 0:4, :])
            own(nc.vector.tensor_copy(xpad[0:G, 4:6, 2:G + 2], pre[0:G, 4:6, :]))
            own(nc.vector.tensor_scalar(dt_u[:, :], dt_raw[:, :], -1.0, None, ALU.mult))
            own(nc.vector.tensor_tensor(dt_u[:, :], dt_u[:, :], dt_raw[:, :], ALU.min))
            dve.sem_inc(to_act, 1)
            for k in range(3):
                own(nc.vector.tensor_tensor(tap[:, :, :], xpad[:, :, k:k + G], bcast_mid(conv_w[:, :, k], G), ALU.mult))
                own(nc.vector.tensor_tensor(conv[:, :, :], conv[:, :, :], tap[:, :, :], ALU.add))
            own(nc.vector.tensor_tensor(conv[:, :, :], conv[:, :, :], bcast_mid(conv_b[:, :], G), ALU.add))
            dve.sem_inc(to_act, 1)
            dve.wait_ge(from_act, 1)
            own(nc.vector.tensor_scalar(dt_p[:, :], dt_u[:, :], 1.0, None, ALU.add))
            dve.sem_inc(to_act, 1)
            dve.wait_ge(from_act, 2)
            own(nc.vector.tensor_scalar(act_e[:, :, :], act_e[:, :, :], 1.0, None, ALU.add))
            own(nc.vector.reciprocal(act_e[:, :, :], act_e[:, :, :]))
            own(nc.vector.tensor_tensor(xc[:, :, :], conv[:, :, :], act_e[:, :, :], ALU.mult))
            own(nc.vector.tensor_copy(c_pad[:, 1:G + 1], xc[0:G, 5, :]))
            dve.sem_inc(to_pe, 1)
            dve.wait_ge(from_act, 3)
            own(nc.vector.tensor_scalar(dt[:, :], dt_p[:, :], -1.0, 1e-30, ALU.add, ALU.max))
            own(nc.vector.reciprocal(dt[:, :], dt[:, :]))
            own(nc.vector.tensor_tensor(dt_l[:, :], dt_l[:, :], dt[:, :], ALU.mult))
            own(nc.vector.tensor_scalar(dt[:, :], dt_p[:, :], 1.0, None, ALU.is_equal))
            own(nc.vector.tensor_tensor(dt_l[:, :], dt_l[:, :], dt[:, :], ALU.add))
            own(nc.vector.tensor_tensor(dt_l[:, :], dt_l[:, :], dt_u[:, :], ALU.mult))
            own(nc.vector.scalar_tensor_tensor(out=dt[:, :], in0=dt_raw[:, :], scalar=0.0, in1=dt_l[:, :],
                                               op0=ALU.max, op1=ALU.add))
            dve.wait_ge(masks, 2)
            for d, m in ((0, lt), (1, gt)):
                own(nc.vector.tensor_tensor(steps[:, d, :, :], bcast_row(m[:, :], H),
                                            bcast_mid(dt[:, d * H:(d + 1) * H], G), ALU.mult))
            dve.sem_inc(to_pe, 1)
            dve.wait_ge(from_pe, 4)
            own(nc.vector.tensor_copy(x_nat[:, :], ps[6][0:G, :]))
            own(nc.vector.tensor_tensor(cb[:, 0, :], ps[7][0:G, 0:G], lt[:, :], ALU.mult))
            own(nc.vector.tensor_tensor(cb[:, 1, :], ps[7][0:G, G:2 * G], gt[:, :], ALU.mult))
            own(nc.vector.tensor_tensor(gate[:, :], ps[7][0:G, 2 * G:2 * G + H], d_skip[:, :], ALU.add))
            own(nc.vector.tensor_scalar(z_e[:, :], z_e[:, :], 1.0, None, ALU.add))
            own(nc.vector.reciprocal(z_e[:, :], z_e[:, :]))
            own(nc.vector.tensor_tensor(z[:, :], z[:, :], z_e[:, :], ALU.mult))
            dve.wait_ge(from_pe, 5)
            for d in range(2):
                own(nc.vector.tensor_tensor(decay[:, d, :, :], ps[d][0:G, :].rearrange("p (h t) -> p h t", h=H),
                                            bcast_mid(a_neg[:, :], G), ALU.mult))
            dve.sem_inc(to_act, 1)
            dve.wait_ge(from_act, 4)
            for d in range(2):
                own(nc.vector.tensor_tensor(decay[:, d, :, :], decay[:, d, :, :], bcast_row(cb[:, d, :], H), ALU.mult))
                own(nc.vector.tensor_tensor(decay[:, d, :, :], decay[:, d, :, :],
                                            bcast_mid(dt[:, d * H:(d + 1) * H], G), ALU.mult))
            own(nc.vector.tensor_tensor(mix[:, :, :], decay[:, 0, :, :], decay[:, 1, :, :], ALU.add))
            dve.sem_inc(to_pe, 1)
            own(nc.vector.tensor_tensor(y[:, :].rearrange("p (h c) -> p h c", h=H),
                                        x_nat[:, :].rearrange("p (h c) -> p h c", h=H), bcast_mid(gate[:, :], G), ALU.mult))
            dve.wait_ge(from_pe, 6)
            own(nc.vector.tensor_tensor(y[:, :], y[:, :], ps[2][0:G, :], ALU.add))
            own(nc.vector.tensor_tensor(y[:, :], y[:, :], z[:, :], ALU.mult))
            dve.sem_inc(to_act, 1)
            dve.wait_ge(from_act, 5)
            own(nc.vector.tensor_scalar(sq[:, 0:1], sq[:, 0:1], 1.0 / DI, EPS, ALU.mult, ALU.add))
            dve.sem_inc(to_act, 1)
            dve.wait_ge(from_act, 6)
            own(nc.vector.reciprocal(sq[:, 0:1], sq[:, 1:2]))
            own(nc.vector.scalar_tensor_tensor(out=y[:, :], in0=y[:, :], scalar=sq[:, 0:1], in1=norm_w[:, :],
                                               op0=ALU.mult, op1=ALU.mult))
            dve.sem_inc(to_pe, 1)
            dve.wait_ge(from_pe, 7)
            own(nc.vector.tensor_copy(ygT[:, :, :], ps[3][:, 0:4 * G].rearrange("p (k t) -> p k t", k=4)))
            dve.sem_inc(to_pe, 1)
            dve.wait_ge(from_pe, 8)
            v = ps[4][:, 0:4 * G].rearrange("p (k t) -> p k t", k=4)
            nc.vector.tensor_copy(blocks[0:G, :, 0:G], v[0:G, :, :])
            own(nc.vector.tensor_copy(blocks[G:P, :, G:P], v[G:P, :, :]))
            dve.sem_inc(to_pe, 1)
            dve.wait_ge(from_pe, 9)
            own(nc.vector.tensor_copy(core.way_back[:, :, :], ps[5][:, :].rearrange("p (k f) -> p k f", k=4)))

        @block.scalar
        def _(act):
            act.wait_ge(to_act, 1)
            nc.scalar.activation(a_neg[:, :], a_neg[:, :], ACT.Exp)
            nc.scalar.activation(z_e[:, :], z[:, :], ACT.Exp, scale=-1.0)
            nc.scalar.activation(dt_u[:, :], dt_u[:, :], ACT.Exp).then_inc(from_act, 1)
            act.wait_ge(from_act, 1)
            nc.scalar.mul(a_neg[:, :], a_neg[:, :], -1.0)
            act.wait_ge(to_act, 2)
            nc.scalar.activation(act_e[:, :, :], conv[:, :, :], ACT.Exp, scale=-1.0).then_inc(from_act, 1)
            act.wait_ge(to_act, 3)
            nc.scalar.activation(dt_l[:, :], dt_p[:, :], ACT.Ln).then_inc(from_act, 1)
            act.wait_ge(to_act, 4)
            nc.scalar.activation(decay[:, :, :, :], decay[:, :, :, :], ACT.Exp).then_inc(from_act, 1)
            act.wait_ge(to_act, 5)
            nc.scalar.activation(z_e[:, :], y[:, :], ACT.Square, accum_out=sq[:, 0:1]).then_inc(from_act, 1)
            act.wait_ge(to_act, 6)
            nc.scalar.activation(sq[:, 1:2], sq[:, 0:1], ACT.Sqrt).then_inc(from_act, 1)

        @block.tensor
        def _(pe):
            mm, tr = nc.tensor.matmul, nc.tensor.transpose
            pe.wait_ge(to_pe, 1)
            for k in range(4):
                tr(ps[0][:, k * P:(k + 1) * P], scaled[:, k, 0:F], core.ident[:, :])
                last = tr(ps[1][0:1, k * P:(k + 1) * P], scaled[:, k, F:F + 1], core.ident[:, :])
            last.then_inc(from_pe, 1)
            pe.wait_ge(w.loaded, 16 * w.LOADS)
            pe.wait_ge(to_pe, 2)
            for k in range(4):
                mm(ps[2][:, k * P:(k + 1) * P], w_fxT[:, k * P:(k + 1) * P], gT[:, k, :], start=True, stop=False)
                last = mm(ps[2][:, k * P:(k + 1) * P], b_fx[:, k * P:(k + 1) * P], ratio_row[:, k, :], start=False, stop=True)
            last.then_inc(from_pe, 1)
            pe.wait_ge(to_pe, 3)
            for k in range(4):
                mm(ps[3][0:G, :], stT[:, k, :], in_wT[:, k, 0:DI], start=k == 0, stop=k == 3)
            for k in range(4):
                mm(ps[4][0:G, 0:2 * H], stT[:, k, :], in_wT[:, k, 2 * DI + 2 * NS:NPROJ], start=k == 0, stop=k == 3)
            for c in range(CH):
                lo = DI + c * P if c < 4 else 2 * DI + (c - 4) * NS
                m = P if c < 4 else NS
                for k in range(4):
                    last = mm(ps[5][0:m, c * G:(c + 1) * G], in_wT[:, k, lo:lo + m], stT[:, k, :], start=k == 0, stop=k == 3)
            last.then_inc(from_pe, 1)
            pe.wait_ge(to_pe, 4)
            for k in range(4):
                tr(ps[6][0:G, k * P:(k + 1) * P], xc[:, k, :], core.ident[:, :])
            for d in range(2):
                mm(ps[7][0:G, d * G:(d + 1) * G], xc[0:G, 4, :], c_pad[:, 2 * d:2 * d + G], start=True, stop=True)
            for k in range(4):
                last = mm(ps[7][0:G, 2 * G:2 * G + H], xc[:, k, :], fcdT[:, k, :], start=k == 0, stop=k == 3)
            last.then_inc(from_pe, 1)
            pe.wait_ge(to_pe, 5)
            for d, m in ((0, gt), (1, lt)):
                last = mm(ps[d][0:G, :], m[:, :], steps[:, d, :, :].rearrange("p h t -> p (h t)"), start=True, stop=True)
            last.then_inc(from_pe, 1)
            pe.wait_ge(to_pe, 6)
            for h in range(H):
                last = mm(ps[2][0:G, h * G:(h + 1) * G], mix[:, h, :], x_nat[:, h * G:(h + 1) * G], start=True, stop=True)
            last.then_inc(from_pe, 1)
            pe.wait_ge(to_pe, 7)
            for k in range(4):
                last = tr(ps[3][:, k * G:(k + 1) * G], y[:, k * P:(k + 1) * P], core.ident[0:G, 0:G])
            last.then_inc(from_pe, 1)
            pe.wait_ge(to_pe, 8)
            pe.wait_ge(loaded, 16)
            for m in range(4):
                for k in range(4):
                    last = mm(ps[4][:, m * G:(m + 1) * G], hy_outT[:, k, m * P:(m + 1) * P], ygT[:, k, :], start=k == 0, stop=k == 3)
            last.then_inc(from_pe, 1)
            pe.wait_ge(to_pe, 9)
            for k in range(4):
                last = mm(ps[5][:, k * P:(k + 1) * P], blocks[:, k, :], out_wT[:, k, :], start=True, stop=True)
            last.then_inc(from_pe, 1)


def slice_scatter(core, st):
    nc = core.nc
    sw = st.sb("sw", [P, 2, Q, HG])
    swT = st.sb("swT", [P, Q, 4, P])
    swT_ps = st.ps("swT_ps", [P, Q, 4, P])
    out_ps = st.ps("out_ps", [P, 2, Q, P])
    sw_in = [st.sem(f"sw_in{k}") for k in range(2)]
    turned = st.sem("turned")
    swT_ready = st.sem("swT_ready")
    scattered = st.sem("scattered")
    added = st.sem("added")
    x_back = st.sem("x_back")
    counted = st.sem("counted")
    x_groups = core.x_dram.rearrange("(g q p) f -> g p q f", p=P, q=Q)
    turns = NT // Q // 2
    xg = core.x[:, :, :].rearrange("p (g q) f -> p g (q f)", q=Q)

    with st.block() as block:
        @block.sync
        def _(sp):
            with sp.Fori(0, turns) as i:
                for b in range(2):
                    g = 2 * i + b
                    sp.wait_ge(turned, 2 * g + 2)
                    for c in range(2):
                        sp.dma_start(sw[:, b, 2 * c:2 * c + 2, :].rearrange("p a f -> p (a f)"),
                                     core.sw_dram[bass.ds(2 * g + c, 1), :, :].rearrange("a p f -> p (a f)")).then_inc(sw_in[b], 16)

        @block.tensor
        def _(pe):
            pe.sem_inc(turned, 4)
            pe.sem_inc(scattered, 1)
            with pe.Fori(0, turns) as i:
                for b in range(2):
                    g = 2 * i + b
                    pe.wait_ge(sw_in[b], 32 * (i + 1))
                    for c in range(2):
                        pe.wait_ge(swT_ready, 2 * g + c + 1)
                        for q in (2 * c, 2 * c + 1):
                            for k in range(4):
                                last = nc.tensor.transpose(swT_ps[:, q, k, :], sw[:, b, q, k * P:(k + 1) * P], core.ident[:, :])
                        last.then_inc(turned, 1)
                    pe.wait_ge(added, g + 1)
                    for c in range(2):
                        pe.wait_ge(swT_ready, 2 * g + c + 3)
                        for q in (2 * c, 2 * c + 1):
                            for k in range(4):
                                nc.tensor.matmul(out_ps[:, b, q, :], swT[:, q, k, :], core.way_back[:, k, :], start=k == 0, stop=False)
                            last = nc.tensor.matmul(out_ps[:, b, q, :], core.ones_b[:, :], core.bias3[:, HG:HG + F], start=False, stop=True)
                    last.then_inc(scattered, 1)

        @block.scalar
        def _(act):
            act.sem_inc(swT_ready, 2)
            with act.Fori(0, turns) as i:
                for b in range(2):
                    g = 2 * i + b
                    act.wait_ge(scattered, g + 1)
                    for c in range(2):
                        act.wait_ge(turned, 2 * g + c + 5)
                        nc.scalar.activation(swT[:, 2 * c:2 * c + 2, :, :], swT_ps[:, 2 * c:2 * c + 2, :, :], ACT.Copy).then_inc(swT_ready, 1)

        @block.vector
        def _(dve):
            dve.sem_inc(added, 2)
            dve.wait_ge(x_back, 16)
            with dve.Fori(0, turns) as i:
                for b in range(2):
                    g = 2 * i + b
                    dve.wait_ge(scattered, g + 2)
                    nc.vector.tensor_tensor(column(xg, g), out_ps[:, b, :, :].rearrange("p q f -> p (q f)"), column(xg, g),
                                            ALU.add).then_inc(added, 1)
                    dve.wait_ge(added, g + 3)
                    for q in range(Q):
                        ins = nc.vector.bn_stats(core.stats[:, bass.ds(Q * g + q, 1), :], core.x[:, bass.ds(Q * g + q, 1), :])
                    ins.then_inc(counted, 1)
            dve.wait_ge(counted, 2 * turns)

        @block.gpsimd
        def _(pool):
            pool.wait_ge(sw_in[0], 32)
            pool.dma_start(core.x[:, :, :], natural(core.x_dram)).then_inc(x_back, 16)
            pool.wait_ge(x_back, 16)
            with pool.Fori(0, turns) as i:
                for b in range(2):
                    g = 2 * i + b
                    pool.wait_ge(added, g + 3)
                    pool.dma_start(x_groups[g], core.x[:, bass.ds(Q * g, Q), :]).then_inc(core.x_saved, 16)


def slice_attention(core):
    with core.stage("slice") as st:
        core.gathered = st.sb("gathered", [P, 4, F + 1])
        core.way_back = st.sb("way_back", [P, 4, F])
        core.mixer_weights = MixerWeights(st)
        with core.stage("slig") as s:
            slice_gather(core, s)
        with core.stage("mix") as s:
            mixer(core, s)
        with core.stage("slis") as s:
            slice_scatter(core, s)


def attention_factors(core, st):
    nc, a = core.nc, core.args
    mean = st.sb("mean", [P, NT])
    var_eps = st.sb("var_eps", [P, NT])
    root = st.sb("root", [P, NT])
    rstd = st.sb("rstd", [P, NT])
    a_cols = st.sb("a_cols", [F, 2])
    a_wide = st.sb("a_wide", [F, P])
    xn = st.sb("xn", [P, 2, 4, F])
    xnT = st.sb("xnT", [P, 2, BANK])
    feats = st.sb("feats", [P, 2, NT])
    top = st.sb("top", [P, 1])
    top_all = st.sb("top_all", [P, 1])
    expo = st.sb("expo", [P, 3, NT])
    fours = st.sb("fours", [P, 4, NT])
    parts = st.sb("parts", [P, 3, 4, NT], BF16)
    rest = st.sb("rest", [P, 4, NT])
    xnT_ps = st.ps("xnT_ps", [P, 2, BANK])
    rows_ps = st.ps("rows_ps", [P, 2, BANK])
    feats_ps = st.ps("feats_ps", [P, BANK])
    loaded = st.sem("loaded")
    rooted = st.sem("rooted")
    stats_done = st.sem("stats_done")
    a_ready = st.sem("a_ready")
    normed = st.sem("normed")
    written_back = st.sem("written_back")
    turned = st.sem("turned")
    xnT_ready = st.sem("xnT_ready")
    rows_done = st.sem("rows_done")
    rows_copied = st.sem("rows_copied")
    feats_done = st.sem("feats_done")
    top_ready = st.sem("top_ready")
    expo_ready = st.sem("expo_ready")
    exped = st.sem("exped")
    dve_own = st.sem("dve_own")

    with st.block() as block:
        @block.sync
        def _(sp):
            sp.dma_start(a_cols[:, :], a["L1_gnn_a"]).then_inc(loaded, 16)
            sp.dma_start(core.coef[:, :], a["L1_gnn_temp"].partition_broadcast(P)).then_inc(loaded, 16)

        @block.gpsimd
        def _(pool):
            pool.wait_ge(top_ready, 1)
            nc.gpsimd.partition_all_reduce(top_all[:, :], top[:, :], P, RMAX).then_inc(top_ready, 1)

        @block.scalar
        def _(act):
            act.wait_ge(stats_done, 1)
            nc.scalar.activation(root[:, :], var_eps[:, :], ACT.Sqrt).then_inc(rooted, 1)
            act.wait_ge(core.x_saved, 16 * NB)
            with act.Fori(0, NB // 2) as i:
                for b in range(2):
                    act.wait_ge(turned, 2 * i + b + 1)
                    nc.scalar.activation(xnT[:, b, :], xnT_ps[:, b, :], ACT.Copy).then_inc(xnT_ready, 1)
                    nc.scalar.activation(core.x[:, bass.ds(8 * i + 4 * b, 4), :], xn[:, b, :, :], ACT.Copy).then_inc(written_back, 1)
            act.wait_ge(expo_ready, 1)
            nc.scalar.activation(expo[:, 0:3, :], expo[:, 0:3, :], ACT.Exp).then_inc(exped, 1)
            nc.scalar.activation(core.coef[:, :], core.coef[:, :], ACT.Exp, scale=-1.0).then_inc(exped, 1)
            act.wait_ge(expo_ready, 2)
            nc.scalar.activation(core.r_rows[:, :], core.r_rows[:, :], ACT.Exp, scale=SLOPE - 1.0).then_inc(exped, 1)
            act.wait_ge(exped, 3)

        @block.vector
        def _(dve):
            own = Chain(dve, dve_own)
            dve.sem_inc(written_back, 2)
            token_statistics(nc, dve, own, core.stats, mean, var_eps)
            dve.sem_inc(stats_done, 1)
            dve.wait_ge(loaded, 32)
            nc.vector.tensor_copy(a_wide[:, :], a_cols[:, 0:1].to_broadcast([F, P])).then_inc(a_ready, 1)
            dve.wait_ge(rooted, 1)
            own(nc.vector.reciprocal(rstd[:, :], root[:, :]))
            def normalise(g, b):
                dve.wait_ge(written_back, g + 1)
                for q in range(4):
                    t = 4 * g + q
                    ins = nc.vector.tensor_scalar(xn[:, b, q, :], column(core.x, t), mean[:, bass.ds(t, 1)],
                                                  rstd[:, bass.ds(t, 1)], ALU.subtract, ALU.mult)
                ins.then_inc(normed, 1)

            def copy_rows(g, b):
                dve.wait_ge(rows_done, g + 1)
                nc.vector.tensor_copy(core.r_rows[:, bass.ds(g * BANK, BANK)], rows_ps[:, b, :]).then_inc(rows_copied, 1)

            for g in range(2):
                normalise(g, g)
            with dve.Fori(0, NB // 2 - 1) as i:
                for b in range(2):
                    normalise(2 * i + (b + 2), b)
                    copy_rows(2 * i + b, b)
            for b in range(2):
                copy_rows(NB - 2 + b, b)
            dve.wait_ge(feats_done, 1)
            dve.wait_ge(written_back, NB + 2)
            own(nc.vector.tensor_copy(feats[:, :, :].rearrange("p k t -> p t k"),
                                      feats_ps[:, 0:2 * NT].rearrange("p (t k) -> p t k", k=2)))
            own(nc.vector.tensor_reduce(top[:, :], feats[:, 1, :], AX.X, ALU.max))
            dve.sem_inc(top_ready, 1)
            dve.wait_ge(top_ready, 2)
            nc.vector.tensor_scalar(expo[:, 0, :], feats[:, 1, :], top_all[:, :], None, ALU.subtract)
            own(nc.vector.tensor_scalar(expo[:, 2, :], feats[:, 0, :], top_all[:, :], 0.0, ALU.add, ALU.max))
            nc.vector.tensor_scalar(expo[:, 1, :], expo[:, 0, :], SLOPE, None, ALU.mult)
            own(nc.vector.tensor_scalar(expo[:, 2, :], expo[:, 2, :], SLOPE - 1.0, None, ALU.mult))
            dve.sem_inc(expo_ready, 1)
            dve.wait_ge(rows_copied, NB + 2)
            own(nc.vector.tensor_scalar(core.r_rows[:, :], core.r_rows[:, :], top_all[:, :], 0.0, ALU.add, ALU.max))
            dve.sem_inc(expo_ready, 1)
            dve.wait_ge(exped, 2)
            high, low, r = (expo[:, k, :] for k in range(3))
            nc.vector.tensor_copy(core.r[:, :], r)
            nc.vector.tensor_copy(core.token[:, :, HIGH], high)
            nc.vector.tensor_copy(core.token[:, :, LOW], low)
            nc.vector.tensor_scalar(core.token[:, :, NEG_HIGH], high, -1.0, None, ALU.mult)
            own(nc.vector.tensor_scalar(core.coef[:, :], core.coef[:, :], 1.0, None, ALU.add))
            own(nc.vector.reciprocal(core.coef[:, :], core.coef[:, :]))
            nc.vector.tensor_scalar(core.coef_rest[:, :], core.coef[:, :], -1.0, 1.0, ALU.mult, ALU.add)
            nc.vector.tensor_copy(fours[:, 0, :], high)
            nc.vector.tensor_tensor(fours[:, 1, :], high, high, ALU.mult)
            nc.vector.tensor_copy(fours[:, 2, :], low)
            nc.vector.tensor_tensor(fours[:, 3, :], low, low, ALU.mult)
            own(nc.vector.memset(core.weigh[:, :, :], 0.0))
            split3(nc, own, [parts[:, k, :, :] for k in range(3)], fours[:, :, :], rest[:, :, :])
            for k in range(3):
                nc.vector.tensor_copy(core.weigh[:, :, k:6:3].rearrange("p t q -> p q t"), parts[:, k, 0:2, :])
                nc.vector.tensor_scalar(core.weigh[:, :, WK + k:WK + 6:3].rearrange("p t q -> p q t"), parts[:, k, 0:2, :], -1.0, None, ALU.mult)
                ins = nc.vector.tensor_copy(core.weigh[:, :, WK + 6 + k:WK + 12:3].rearrange("p t q -> p q t"), parts[:, k, 2:4, :])
            own(ins)

        @block.tensor
        def _(pe):
            pe.sem_inc(rows_copied, 2)
            pe.wait_ge(loaded, 32)
            pe.wait_ge(a_ready, 1)

            def turn(g, b):
                pe.wait_ge(normed, g + 1)
                for q in range(4):
                    ins = nc.tensor.transpose(xnT_ps[:, b, q * P:(q + 1) * P], xn[:, b, q, :], core.ident[:, :])
                ins.then_inc(turned, 1)

            def products(g, b):
                pe.wait_ge(xnT_ready, g + 1)
                pe.wait_ge(rows_copied, g + 1)
                nc.tensor.matmul(rows_ps[:, b, :], a_wide[:, :], xnT[:, b, :], start=True, stop=True).then_inc(rows_done, 1)
                for q in range(4):
                    nc.tensor.matmul(feats_ps[:, bass.ds(8 * g + 2 * q, 2)], xnT[:, b, q * P:(q + 1) * P], a_cols[:, :], start=True, stop=True)

            turn(0, 0)
            with pe.Fori(0, NB // 2 - 1) as i:
                for b in range(2):
                    turn(2 * i + (b + 1), 1 - b)
                    products(2 * i + b, b)
            turn(NB - 1, 1)
            products(NB - 2, 0)
            products(NB - 1, 1)
            nc.tensor.matmul(feats_ps[:, P:2 * P], core.zeros_b[:, 0:P], core.zeros_b[:, 0:P], start=True, stop=True).then_inc(feats_done, 1)


WK = 12
CHUNK = 1024
HIGH, LOW, NEG_HIGH = range(3)


def propagate_first(core, st, half):
    nc = core.nc
    above = st.sb("above", [P, 2, CHUNK])
    mask_b = st.sb("mask_b", [P, 2, CHUNK], BF16)
    z = st.sb("z", [P, 2, CHUNK])
    lower = st.sb("lower", [P, 2, CHUNK], BF16)
    tokj = st.sb("tokj", [P, 2, 3])
    xj = st.sb("xj", [P, 2, F])
    wj = st.sb("wj", [P, 2, 2 * WK], BF16)
    above_ready = st.sem("above_ready")
    sign_ready = st.sem("sign_ready")
    mask_ready = st.sem("mask_ready")
    z_ready = st.sem("z_ready")
    lower_ready = st.sem("lower_ready")
    used = st.sem("used")
    picked = st.sem("picked")
    ended = st.sem("ended")
    kept = st.sem("kept")
    acc, sums = core.acc, core.sums
    base = half * HALF

    with st.block() as block:
        @block.gpsimd
        def _(pool):
            with pool.Fori(0, NT // 2) as i:
                for b in range(2):
                    j = 2 * i + b
                    pool.wait_ge(used, 2 * j + 2)
                    nc.gpsimd.tensor_copy(xj[:, b, :], column(core.x, j))
                    nc.gpsimd.tensor_copy(tokj[:, b, :], column(core.token, j))
                    nc.gpsimd.tensor_copy(wj[:, b, :], column(core.weigh, j)).then_inc(picked, 1)

        @block.scalar
        def _(act):
            with act.Fori(0, NT // 2) as i:
                for b in range(2):
                    j = 2 * i + b
                    act.wait_ge(picked, j + 1)
                    for c in range(2):
                        n = 2 * j + c
                        lo = base + c * CHUNK
                        act.wait_ge(z_ready, n + 1)
                        nc.scalar.activation(above[:, c, :], core.r_rows[:, lo:lo + CHUNK], ACT.Relu,
                                             scale=tokj[:, b, LOW:LOW + 1], bias=tokj[:, b, NEG_HIGH:NEG_HIGH + 1]).then_inc(above_ready, 1)
                        act.wait_ge(above_ready, n + 1)
                        act.wait_ge(used, n + 3)
                        nc.scalar.activation(lower[:, c, :], above[:, c, :], ACT.Sign).then_inc(sign_ready, 1)
            if half == 0:
                act.wait_ge(ended, 1)
                nc.scalar.activation(core.acc_kept[:, :], acc[:, :, :].rearrange("p k c -> p (k c)"), ACT.Copy).then_inc(kept, 1)
                act.wait_ge(kept, 2)

        @block.vector
        def _(dve):
            dve.sem_inc(z_ready, 2)
            dve.sem_inc(lower_ready, 2)
            with dve.Fori(0, NT // 2) as i:
                for b in range(2):
                    j = 2 * i + b
                    for c in range(2):
                        n = 2 * j + c
                        lo = base + c * CHUNK
                        dve.wait_ge(used, n + 3)
                        nc.vector.tensor_copy(mask_b[:, c, :], column(core.mask[:, :, lo:lo + CHUNK], j)).then_inc(mask_ready, 1)
                        dve.wait_ge(above_ready, n + 1)
                        nc.vector.scalar_tensor_tensor(out=z[:, c, :], in0=above[:, c, :], scalar=tokj[:, b, HIGH:HIGH + 1],
                                                       in1=column(core.mask[:, :, lo:lo + CHUNK], j), op0=ALU.add, op1=ALU.mult).then_inc(z_ready, 1)
                        dve.wait_ge(sign_ready, n + 1)
                        dve.wait_ge(mask_ready, n + 1)
                        nc.vector.tensor_tensor(lower[:, c, :], lower[:, c, :], mask_b[:, c, :], ALU.mult).then_inc(lower_ready, 1)
            if half == 0:
                dve.wait_ge(ended, 1)
                nc.vector.tensor_copy(core.sums_kept[:, :, :], sums[:, :, :]).then_inc(kept, 1)
                dve.wait_ge(kept, 2)

        @block.tensor
        def _(pe):
            pe.sem_inc(used, 4)
            for k in range(4):
                nc.tensor.matmul(acc[:, k, :], core.zeros_b[:, 0:P], core.zeros_b[:, :], start=True, stop=False)
            for c in range(2):
                nc.tensor.matmul(sums[:, c, :], core.zeros_b[:, 0:P], core.zeros_b[:, :], start=True, stop=False)
            if half == 1:
                turn_sums(core, core.sums_kept, 0)
            with pe.Fori(0, NT // 2) as i:
                for b in range(2):
                    j = 2 * i + b
                    pe.wait_ge(picked, j + 1)
                    for c in range(2):
                        n = 2 * j + c
                        pe.wait_ge(z_ready, n + 3)
                        for k in range(2):
                            nc.tensor.matmul(acc[:, 2 * c + k, :], xj[:, b, :], z[:, c, k * BANK:(k + 1) * BANK],
                                             start=False, stop=False)
                        pe.wait_ge(lower_ready, n + 3)
                        for k in range(2):
                            for m, moving in enumerate((mask_b, lower)):
                                at = 32 * (2 * k + m)
                                last = nc.tensor.matmul(sums[at:at + WK, c, :], wj[:, b, m * WK:(m + 1) * WK],
                                                        moving[:, c, k * BANK:(k + 1) * BANK], start=False, stop=False)
                        last.then_inc(used, 1)
            for k in range(4):
                nc.tensor.matmul(acc[:, k, :], core.zeros_b[:, 0:P], core.zeros_b[:, :], start=False, stop=True)
            for c in range(2):
                last = nc.tensor.matmul(sums[:, c, :], core.zeros_b[:, 0:P], core.zeros_b[:, :], start=False, stop=True)
            last.then_inc(ended, 1)
            pe.wait_ge(ended, 1)


def turn_sums(core, kept, half):
    nc = core.nc
    for u in range(NT // 2):
        t = NT // 2 * half + u
        ins = nc.tensor.matmul(core.psum[:, NB - 1, 4 * t:4 * t + 4], kept[:, u // 8, (u % 4) * P:(u % 4 + 1) * P],
                               core.select[:, (u // 4) % 2, :], start=True, stop=True)
    return ins


def features(core, st):
    nc = core.nc
    acc, sums = core.acc, core.sums
    turned_ps = core.psum
    acc_kept = [core.acc_kept, st.sb("acc_kept", [P, HALF])]
    sums_kept = st.sb("sums_kept", [P, 2, BANK])
    four = st.sb("four", [P, NT, 4])
    tok = st.sb("tok", [P, 3, NT])
    clamped = st.sb("clamped", [P, HALF])
    acc_copied = st.sem("acc_copied")
    sums_copied = st.sem("sums_copied")
    four_done = st.sem("four_done")
    four_copied = st.sem("four_copied")
    turned = st.sem("turned")
    share_ready = st.sem("share_ready")
    x_scaled = st.sem("x_scaled")
    dve_own = st.sem("dve_own")
    four_ps = turned_ps[:, NB - 1, 0:4 * NT]

    with st.block() as block:
        @block.tensor
        def _(pe):
            pe.wait_ge(sums_copied, 1)
            turn_sums(core, sums_kept, 1).then_inc(four_done, 1)
            for g in range(NB):
                if g == NB // 2 - 1:
                    pe.wait_ge(four_copied, 1)
                if g == NB // 2:
                    pe.wait_ge(acc_copied, 1)
                for q in range(4):
                    t = 4 * g + q
                    last = nc.tensor.transpose(turned_ps[:, (g + NB // 2) % NB, q * P:(q + 1) * P],
                                               acc_kept[g // 4][:, (t % 16) * P:(t % 16 + 1) * P], core.ident[:, :])
                last.then_inc(turned, 1)

        @block.scalar
        def _(act):
            nc.scalar.activation(acc_kept[1][:, :], acc[:, :, :].rearrange("p k c -> p (k c)"), ACT.Copy).then_inc(acc_copied, 1)
            act.wait_ge(share_ready, 1)
            with act.Fori(0, NB) as g:
                for q in range(4):
                    t = 4 * g + q
                    last = nc.scalar.activation(column(core.x, t), column(core.x, t), ACT.Copy, scale=tok[:, 2, bass.ds(t, 1)])
                last.then_inc(x_scaled, 1)

        @block.vector
        def _(dve):
            own = Chain(dve, dve_own)
            r, inv, rowsum = core.r[:, :], core.inv_z[:, :], core.half_u2[:, :]
            nc.vector.tensor_copy(sums_kept[:, :, :], sums[:, :, :]).then_inc(sums_copied, 1)
            dve.wait_ge(four_done, 1)
            own(nc.vector.tensor_copy(four[:, :, :].rearrange("p t k -> p (t k)"), four_ps))
            dve.sem_inc(four_copied, 1)
            nc.vector.tensor_tensor(tok[:, 0, :], four[:, :, 2], r, ALU.mult)
            own(nc.vector.tensor_tensor(tok[:, 1, :], four[:, :, 3], r, ALU.mult))
            nc.vector.tensor_tensor(tok[:, 0, :], tok[:, 0, :], four[:, :, 0], ALU.add)
            own(nc.vector.tensor_tensor(tok[:, 1, :], tok[:, 1, :], r, ALU.mult))
            nc.vector.reciprocal(inv, tok[:, 0, :])
            own(nc.vector.tensor_tensor(tok[:, 1, :], tok[:, 1, :], four[:, :, 1], ALU.add))
            own(nc.vector.tensor_tensor(tok[:, 1, :], tok[:, 1, :], inv, ALU.mult))
            own(nc.vector.scalar_tensor_tensor(out=rowsum, in0=tok[:, 1, :], scalar=0.5, in1=inv, op0=ALU.mult, op1=ALU.mult))
            own(nc.vector.tensor_scalar(tok[:, 2, :], rowsum, -1.0, core.coef_rest[:, 2:3], ALU.mult, ALU.add))
            dve.sem_inc(share_ready, 1)
            for half in range(2):
                with dve.Fori(0, NB // 4) as i:
                    own.enter(i, 1)
                    for b in range(2):
                        g = NB // 2 * half + 2 * i + b
                        bank = 2 * i + (b + NB // 2 * (1 - half))
                        dve.wait_ge(turned, g + 1)
                        dve.wait_ge(x_scaled, g + 1)
                        for q in range(4):
                            t = 4 * g + q
                            ins = nc.vector.scalar_tensor_tensor(
                                out=column(core.x, t), in0=turned_ps[:, bass.ds(bank, 1), q * P:(q + 1) * P].rearrange("p a f -> p (a f)"),
                                scalar=inv[:, bass.ds(t, 1)], in1=column(core.x, t), op0=ALU.mult, op1=ALU.add)
                    own(ins)
                    own.leave(NB // 4)
                v = core.x[:, half * (NT // 2):(half + 1) * (NT // 2), :].rearrange("p q f -> p (q f)")
                own(nc.vector.tensor_scalar(clamped[:, :], v, THRESH, -THRESH, ALU.min, ALU.max))
                own(nc.vector.tensor_tensor(v, v, clamped[:, :], ALU.subtract))


def propagate_second(core, st):
    nc = core.nc
    h0_tiles = core.args["L1_gnn_h0"].rearrange("(t p) f -> t p f", p=P)
    coef, rest_of = core.coef, core.coef_rest
    above = st.sb("above", [P, 2, CHUNK])
    z = st.sb("z", [P, 2, CHUNK])
    fj = st.sb("fj", [P, 2, F])
    tokj = st.sb("tokj", [P, 2, 3])
    h0 = st.sb("h0", [P, 2, F])
    k0 = st.sb("k0", [P, 2])
    gamma = st.sb("gamma", [P, NT])
    x_in = st.sem("x_in")
    h0_in = [st.sem(f"h0_in{b}") for b in range(2)]
    h0_used = st.sem("h0_used")
    dve_own = st.sem("dve_own")
    above_ready = st.sem("above_ready")
    weighed = st.sem("weighed")
    used = st.sem("used")
    picked = st.sem("picked")
    ended = st.sem("ended")
    acc = core.acc2
    NC = N // CHUNK

    with st.block() as block:
        @block.sync
        def _(sp):
            sp.dma_start(core.rest[:, :, :], natural(core.x_dram)).then_inc(x_in, 16)
            with sp.Fori(0, NT // 2) as i:
                for b in range(2):
                    j = 2 * i + b
                    sp.wait_ge(h0_used, j + 1)
                    sp.dma_start(h0[:, b, :], h0_tiles[j]).then_inc(h0_in[b], 16)

        @block.gpsimd
        def _(pool):
            with pool.Fori(0, NT // 2) as i:
                for b in range(2):
                    j = 2 * i + b
                    pool.wait_ge(used, NC * j + 1)
                    nc.gpsimd.tensor_copy(fj[:, b, :], column(core.x, j))
                    nc.gpsimd.tensor_copy(tokj[:, b, :], column(core.token, j)).then_inc(picked, 1)

        @block.scalar
        def _(act):
            with act.Fori(0, NT // 2) as i:
                for b in range(2):
                    j = 2 * i + b
                    act.wait_ge(picked, j + 1)
                    for c in range(NC):
                        act.wait_ge(weighed, NC * j + c + 1)
                        nc.scalar.activation(above[:, c % 2, :], core.r_rows[:, c * CHUNK:(c + 1) * CHUNK], ACT.Relu,
                                             scale=tokj[:, b, LOW:LOW + 1], bias=tokj[:, b, NEG_HIGH:NEG_HIGH + 1]).then_inc(above_ready, 1)

        @block.vector
        def _(dve):
            dve.sem_inc(weighed, 2)
            dve.sem_inc(h0_used, 2)
            own = Chain(dve, dve_own)
            nc.vector.tensor_tensor(k0[:, 0:1], rest_of[:, 1:2], coef[:, 0:1], ALU.mult)
            own(nc.vector.tensor_tensor(k0[:, 1:2], rest_of[:, 1:2], rest_of[:, 0:1], ALU.mult))
            own(nc.vector.tensor_scalar(gamma[:, :], core.half_u2[:, :], coef[:, 1:2], k0[:, 0:1], ALU.mult, ALU.add))
            own(nc.vector.tensor_scalar(core.mu[:, :], gamma[:, :], coef[:, 3:4], None, ALU.mult))
            own(nc.vector.tensor_scalar(core.mu[:, :], core.mu[:, :], -1.0, coef[:, 1:2], ALU.mult, ALU.add))
            own(nc.vector.tensor_tensor(core.mu[:, :], core.mu[:, :], core.inv_z[:, :], ALU.mult))
            dve.wait_ge(x_in, 16)
            with dve.Fori(0, NT // 2) as i:
                own.enter(i, 2)
                for b in range(2):
                    j = 2 * i + b
                    for c in range(NC):
                        n = NC * j + c
                        dve.wait_ge(above_ready, n + 1)
                        dve.wait_ge(used, n + 4)
                        nc.vector.scalar_tensor_tensor(out=z[:, c % 2, :], in0=above[:, c % 2, :], scalar=tokj[:, b, HIGH:HIGH + 1],
                                                       in1=column(core.mask[:, :, c * CHUNK:(c + 1) * CHUNK], j),
                                                       op0=ALU.add, op1=ALU.mult).then_inc(weighed, 1)
                        rest = column(core.rest, j)
                        if c == 0:
                            dve.wait_ge(h0_in[b], 16 * (i + 1))
                            nc.vector.scalar_tensor_tensor(out=rest, in0=h0[:, b, :], scalar=k0[:, 1:2], in1=rest,
                                                           op0=ALU.mult, op1=ALU.add).then_inc(h0_used, 1)
                        if c == 2:
                            dve.wait_ge(h0_used, j + 3)
                            ins = nc.vector.scalar_tensor_tensor(out=rest, in0=column(core.x, j), scalar=gamma[:, bass.ds(j, 1)],
                                                                 in1=rest, op0=ALU.mult, op1=ALU.add)
                    own(ins)
                own.leave(NT // 2)

        @block.tensor
        def _(pe):
            pe.sem_inc(used, 5)
            for k in range(NB):
                nc.tensor.matmul(acc[:, k, :], core.zeros_b[:, 0:P], core.zeros_b[:, :], start=True, stop=False)
            with pe.Fori(0, NT // 2) as i:
                for b in range(2):
                    j = 2 * i + b
                    pe.wait_ge(picked, j + 1)
                    for c in range(NC):
                        pe.wait_ge(weighed, NC * j + c + 3)
                        for k in range(2):
                            last = nc.tensor.matmul(acc[:, 2 * c + k, :], fj[:, b, :], z[:, c % 2, k * BANK:(k + 1) * BANK],
                                                    start=False, stop=False)
                        last.then_inc(used, 1)
            for k in range(NB):
                last = nc.tensor.matmul(acc[:, k, :], core.zeros_b[:, 0:P], core.zeros_b[:, :], start=False, stop=True)
            last.then_inc(ended, 1)
            pe.wait_ge(ended, 1)


def attention_finish(core, st):
    nc = core.nc
    evac = st.sb("evac", [P, 2, BANK])
    evacuated = st.sem("evacuated")
    turned = st.sem("turned")
    dve_own = st.sem("dve_own")
    acc = core.acc2

    with st.block() as block:
        @block.sync
        def _(sp):
            load_expert_weights(core, sp)

        @block.scalar
        def _(act):
            with act.Fori(0, NB // 2) as i:
                for b in range(2):
                    g = 2 * i + b
                    act.wait_ge(turned, g + 1)
                    nc.scalar.activation(evac[:, b, :], column(acc, g), ACT.Copy).then_inc(evacuated, 1)

        @block.tensor
        def _(pe):
            pe.sem_inc(turned, 2)
            for g in range(NB):
                pe.wait_ge(evacuated, g + 1)
                for q in range(4):
                    last = nc.tensor.transpose(acc[:, g, q * P:(q + 1) * P], evac[:, g % 2, q * P:(q + 1) * P], core.ident[:, :])
                last.then_inc(turned, 1)

        @block.vector
        def _(dve):
            own = Chain(dve, dve_own)
            with dve.Fori(0, NB // 2) as i:
                own.enter(i, 1)
                for b in range(2):
                    g = 2 * i + b
                    dve.wait_ge(turned, g + 3)
                    for q in range(4):
                        t = 4 * g + q
                        ins = nc.vector.scalar_tensor_tensor(
                            out=column(core.x, t), in0=acc[:, bass.ds(g, 1), q * P:(q + 1) * P].rearrange("p a f -> p (a f)"),
                            scalar=core.mu[:, bass.ds(t, 1)], in1=column(core.rest, t), op0=ALU.mult, op1=ALU.add)
                own(ins)
                for q in range(8):
                    nc.vector.bn_stats(core.stats[:, bass.ds(8 * i + q, 1), :], core.x[:, bass.ds(8 * i + q, 1), :])
                own.leave(NB // 2)


def graph_attention(core):
    with core.stage("attn") as st:
        core.r_rows = st.sb("r_rows", [P, N])
        core.weigh = st.sb("weigh", [P, NT, 2 * WK], BF16)
        core.token = st.sb("token", [P, NT, 3])
        core.r = st.sb("r", [P, NT])
        with core.stage("attf") as s:
            attention_factors(core, s)
        with core.stage("att1") as outer:
            core.acc_kept = outer.sb("acc_kept", [P, HALF])
            core.sums_kept = outer.sb("sums_kept", [P, 2, BANK])
            core.psum = outer.ps("psum", [P, NB, BANK])
            core.acc, core.sums = core.psum[:, 0:4, :], core.psum[:, 4:6, :]
            for half in range(2):
                with core.stage(f"att1p{half}") as s:
                    propagate_first(core, s, half)
            with core.stage("att1f") as s:
                features(core, s)
        with core.stage("att2") as outer:
            core.rest = outer.sb("rest", [P, NT, F])
            core.acc2 = outer.ps("acc2", [P, NB, BANK])
            with core.stage("att2p") as s:
                propagate_second(core, s)
            expert_weights(core)
            with core.stage("attd") as s:
                attention_finish(core, s)


def from_stage_two(core, upto):
    core.x_saved = core.late.sem("x_saved")
    slice_attention(core)
    if upto > 3:
        core.route = core.late.sb("route", [1, N // TOK], I32)
        core.small_in = core.late.sem("small_in")
        core.weights_in = [core.late.sem(f"weights_in{l}") for l in range(2)]
        graph_attention(core)


TOK = N // 64
U = 4
WARM = 12


def expert_weights(core):
    words = core.mask[:, 0:24, :].rearrange("p t n -> p (t n)").bitcast(F32)
    size = KH * NE * (HID + 1)
    core.w_routed = words[:, 0:2 * size].rearrange("p (l k e h) -> p l k e h", l=2, k=KH, e=NE)
    at = 2 * size
    core.w_shared = words[:, at:at + 2 * KH * (HID + 1)].rearrange("p (l k h) -> p l k h", l=2, k=KH)
    at += 2 * KH * (HID + 1)
    core.w_in = words[:, at:at + HID]
    at += HID
    core.w_out = words[:, at:at + KH * F].rearrange("p (k f) -> p k f", k=KH)
    at += KH * F
    core.b_in = words[:, at:at + KH]


def load_expert_weights(core, sp):
    a = core.args
    for dst, src in ((core.w_in, a["L1_ffn_WiT"]), (core.b_in, a["L1_ffn_bi"]),
                     (core.w_out, a["L1_ffn_WoT"].rearrange("(k p) f -> p k f", p=P)),
                     (core.route[:, :], a["L1_ffn_route_id"].unsqueeze(0)),
                     (core.w_shared, a["L1_ffn_WsT"])):
        sp.dma_start(dst, src).then_inc(core.small_in, 16)
    for l in range(2):
        sp.dma_start(core.w_routed[:, l].rearrange("p k e h -> p (k e h)"), a["L1_ffn_WrT"][:, l]).then_inc(core.weights_in[l], 16)


def routed_mlp(core, st):
    nc = core.nc
    mean = st.sb("mean", [P, NT])
    var_eps = st.sb("var_eps", [P, NT])
    root = st.sb("root", [P, NT])
    rstd = st.sb("rstd", [P, NT])
    w_sum = st.sb("w_sum", [P, 2, U, 2, KH, HID + 1])
    xn = st.sb("xn", [P, U, F])
    xnT = st.sb("xnT", [P, U, P])
    hT = [st.sb(f"hT{l}", [P, U, KH, P]) for l in range(3)]
    res = st.sb("res", [P, U, F])
    turn_ps = st.ps("turn_ps", [P, U, P])
    first_ps = st.ps("first_ps", [P, U, KH, P])
    layer_ps = st.ps("layer_ps", [P, U, BANK // P, P])
    out_ps = st.ps("out_ps", [P, U, F])
    stats_done = st.sem("stats_done")
    rooted = st.sem("rooted")
    w_shared_ready = st.sem("w_shared_ready")
    normed = st.sem("normed")
    turned = st.sem("turned")
    xnT_ready = st.sem("xnT_ready")
    w_ready = [st.sem(f"w_ready{l}") for l in range(2)]
    h_done = [st.sem(f"h_done{l}") for l in range(3)]
    h_ready = [st.sem(f"h_ready{l}") for l in range(3)]
    out_done = st.sem("out_done")
    res_ready = st.sem("res_ready")
    stored = st.sem("stored")
    dve_own = st.sem("dve_own")
    groups = NT // U
    PAIRS = U // 2
    SMALL = 16 * 5
    x_out = core.out.rearrange("(i q p) f -> i p q f", p=P, q=U)
    xg = core.x[:, :, :].rearrange("p (g q) f -> p g (q f)", q=U)

    def sum_weights(eng, g, l, ahead):
        expert = [eng.value_load(core.route[0:1, bass.ds(2 * U * g + u, 1)], min_val=0, max_val=NE - 1) for u in range(2 * U)]
        if not ahead:
            eng.wait_ge(core.weights_in[l], 16)
        for q in range(U):
            if ahead:
                eng.wait_ge(h_ready[l + 1], U * g - U + q + 1)
            for s in range(2):
                picked = core.w_routed[:, l, :, bass.ds(expert[2 * q + s], 1), :].rearrange("p k a h -> p k (a h)")
                ins = eng.tensor_tensor(w_sum[:, l, q, s, :, :], picked, core.w_shared[:, l, :, :], ALU.add)
            ins.then_inc(w_ready[l], 1)

    with st.block() as block:
        @block.gpsimd
        def _(pool):
            pool.wait_ge(w_shared_ready, 1)
            sum_weights(pool, 0, 1, False)
            with pool.Fori(0, groups - 1) as i:
                sum_weights(pool, i + 1, 1, True)

        @block.sync
        def _(sp):
            sp.sem_inc(stored, 16)
            with sp.Fori(0, groups) as i:
                sp.wait_ge(res_ready, i + 2)
                sp.dma_start(x_out[i], res[:, :, :]).then_inc(stored, 16)
            sp.wait_ge(stored, 16 * (groups + 1))

        @block.scalar
        def _(act):
            def copy_turned(g):
                act.wait_ge(turned, g + 2)
                nc.scalar.activation(xnT[:, :, :], turn_ps[:, :, :], ACT.Copy).then_inc(xnT_ready, 1)

            def first(g):
                for c in range(PAIRS):
                    act.wait_ge(h_done[0], PAIRS * g + c + 1)
                    for k in range(KH):
                        ins = nc.scalar.activation(hT[0][:, 2 * c:2 * c + 2, k, :], first_ps[:, 2 * c:2 * c + 2, k, :], ACT.Relu,
                                                   bias=core.b_in[:, k:k + 1])
                    ins.then_inc(h_ready[0], 1)

            def layer(g, l):
                for q in range(U):
                    act.wait_ge(h_done[l + 1], U * g + q + 1)
                    for s in range(2):
                        for k in range(KH):
                            part = slice(s * TOK, (s + 1) * TOK)
                            ins = nc.scalar.activation(hT[l + 1][:, q, k, part], layer_ps[:, q, k, part], ACT.Relu,
                                                       bias=w_sum[:, l, q, s, k, HID:HID + 1])
                    ins.then_inc(h_ready[l + 1], 1)

            act.wait_ge(stats_done, 1)
            nc.scalar.activation(root[:, :], var_eps[:, :], ACT.Sqrt).then_inc(rooted, 1)
            act.wait_ge(core.small_in, SMALL)
            copy_turned(0)
            first(0)
            with act.Fori(0, groups - 1) as i:
                layer(i, 0)
                copy_turned(i + 1)
                layer(i, 1)
                first(i + 1)
            layer(groups - 1, 0)
            layer(groups - 1, 1)

        @block.vector
        def _(dve):
            own = Chain(dve, dve_own)

            def normalise(g):
                dve.wait_ge(turned, g + 1)
                for q in range(U):
                    t = U * g + q
                    ins = nc.vector.tensor_scalar(xn[:, q, :], column(core.x, t), mean[:, bass.ds(t, 1)], rstd[:, bass.ds(t, 1)],
                                                  ALU.subtract, ALU.mult)
                ins.then_inc(normed, 1)

            def finish(g):
                dve.wait_ge(out_done, g + 1)
                dve.wait_ge(stored, 16 * (g + 1))
                nc.vector.tensor_tensor(res[:, :, :].rearrange("p q f -> p (q f)"), out_ps[:, :, :].rearrange("p q f -> p (q f)"),
                                        column(xg, g), ALU.add).then_inc(res_ready, 1)

            token_statistics(nc, dve, own, core.stats, mean, var_eps)
            dve.sem_inc(stats_done, 1)
            dve.sem_inc(res_ready, 1)
            dve.wait_ge(core.small_in, SMALL)
            for l in range(2):
                for k in range(KH):
                    part = core.w_shared[:, l, k, k * P:(k + 1) * P]
                    ins = nc.vector.tensor_tensor(part, part, core.ident[:, :], ALU.add)
            own(ins)
            dve.wait_ge(rooted, 1)
            own(nc.vector.reciprocal(rstd[:, :], root[:, :]))
            normalise(0)
            dve.sem_inc(w_shared_ready, 1)
            sum_weights(dve, 0, 0, False)
            with dve.Fori(0, groups - 1) as i:
                normalise(i + 1)
                sum_weights(dve, i + 1, 0, True)
                finish(i)
            finish(groups - 1)

        @block.tensor
        def _(pe):
            mm, tr = nc.tensor.matmul, nc.tensor.transpose

            def turn(g):
                pe.wait_ge(normed, g + 1)
                for q in range(U):
                    ins = tr(turn_ps[:, q, :], xn[:, q, :], core.ident[:, :])
                ins.then_inc(turned, 1)

            def first(g):
                pe.wait_ge(xnT_ready, g + 1)
                for q in range(U):
                    for k in range(KH):
                        ins = mm(first_ps[:, q, k, :], core.w_in[:, k * P:(k + 1) * P], xnT[:, q, :], start=True, stop=True)
                    if q % 2:
                        ins.then_inc(h_done[0], 1)

            def layer(g, l):
                for q in range(U):
                    pe.wait_ge(w_ready[l], U * g + q + 1)
                    pe.wait_ge(h_ready[l], U * g + q + 1 if l else PAIRS * g + q // 2 + 1)
                    for s in range(2):
                        part = slice(s * TOK, (s + 1) * TOK)
                        for m in range(KH):
                            for k in range(KH):
                                ins = mm(layer_ps[:, q, m, part], w_sum[:, l, q, s, k, m * P:(m + 1) * P], hT[l][:, q, k, part],
                                         start=k == 0, stop=k == KH - 1)
                    ins.then_inc(h_done[l + 1], 1)

            def output(g):
                pe.wait_ge(res_ready, g + 1)
                for q in range(U):
                    pe.wait_ge(h_ready[2], U * g + q + 1)
                    for k in range(KH):
                        mm(out_ps[:, q, :], hT[2][:, q, k, :], core.w_out[:, k, :], start=k == 0, stop=False)
                    ins = mm(out_ps[:, q, :], core.ones_b[:, :], core.bias3[:, HG + F:HG + 2 * F], start=False, stop=True)
                ins.then_inc(out_done, 1)

            pe.sem_inc(turned, 1)
            for k in range(WARM):
                mm(first_ps[:, 0:2, :, :].rearrange("p q k c -> p (q k c)"), core.zeros_b[:, 0:P], core.zeros_b[:, :], start=True, stop=True)
            pe.wait_ge(core.small_in, SMALL)
            turn(0)
            first(0)
            with pe.Fori(0, groups - 1) as i:
                layer(i, 0)
                turn(i + 1)
                layer(i, 1)
                first(i + 1)
                output(i)
            layer(groups - 1, 0)
            layer(groups - 1, 1)
            output(groups - 1)


def program(nc, args, out, upto=99):
    core = Core(nc, args, out)
    core.ctx = ExitStack()
    with core.ctx, core.stage("keep") as keep:
        core.ident = keep.sb("ident", [P, P])
        core.ones_b = keep.sb("ones_b", [P, P], BF16)
        core.zeros_b = keep.sb("zeros_b", [P, BANK], BF16)
        core.x = keep.sb("x", [P, NT, F])
        core.bias3 = keep.sb("bias3", [P, HG + 2 * F], BF16)
        core.wc = keep.sb("wc", [P, HG])
        core.sw_dram = nc.dram_tensor("sw_scratch", (NT // 2, P, 2 * HG), F32, kind="Internal").ap()
        core.x_dram = nc.dram_tensor("x_scratch", (N, F), F32, kind="Internal").ap()
        core.rowsum = keep.sb("rowsum", [P, NT])
        core.select = keep.sb("select", [P, 2, 4])
        core.coef = keep.sb("coef", [P, 5])
        core.coef_rest = keep.sb("coef_rest", [P, 5])
        core.inv_z = keep.sb("inv_z", [P, NT])
        core.half_u2 = keep.sb("half_u2", [P, NT])
        core.mu = keep.sb("mu", [P, NT])
        core.stats = keep.sb("stats", [P, NT, 6])
        with core.stage("masked") as masked:
            core.mask = masked.sb("mask", [P, NT, N], U8)
            with core.stage("gcn") as st:
                core.acc = st.ps("acc", [P, NB, BANK])
                with core.stage("gcnp") as sp:
                    gcn_propagate(core, sp)
                with core.stage("gcnf") as sf:
                    gcn_finish(core, sf)
            with core.stage("late") as core.late:
                if upto > 1:
                    from_stage_two(core, upto)
                if upto > 8:
                    with core.stage("mlp") as st:
                        routed_mlp(core, st)
        if upto < 9:
            dump(core)


def dump(core):
    nc = core.nc
    with core.stage("dump") as st:
        stored = st.sem("stored")
        with st.block() as block:
            @block.sync
            def _(sp):
                sp.dma_start(natural(core.out), core.x[:, :, :]).then_inc(stored, 16)
                sp.wait_ge(stored, 16)


def channel_chunks(w):
    x, b, c = w[:DI], w[DI:DI + NS], w[DI + NS:]
    return np.concatenate([x.reshape(4, P, -1).transpose(1, 0, 2), np.concatenate([b, b])[:, None],
                           np.concatenate([c, c])[:, None]], axis=1)


def with_bias(w, b):
    wT = w.reshape(w.shape[:3] + (KH, P)).transpose(4, 0, 3, 1, 2)
    bT = b.reshape(b.shape[:2] + (KH, P)).transpose(3, 0, 2, 1)
    return np.concatenate([wT, bT[..., None]], axis=-1)


def layouts(inputs):
    a = {k: np.asarray(v) for k, v in inputs.items()}
    return {
        "x": a["x"],
        "adj": a["adj"],
        "adjT": np.ascontiguousarray(a["adj"].T),
        "L0_gnn_W": a["L0_gnn_W"],
        "L0_ffn_W_x": a["L0_ffn_W_x"],
        "L0_ffn_W_sliceT": a["L0_ffn_W_slice"].T,
        "L0_ffn_b_xT": a["L0_ffn_b_x"].reshape(H, G).T,
        "L0_ffn_b_slice": a["L0_ffn_b_slice"],
        "L0_ffn_temperature": a["L0_ffn_temperature"].reshape(H),
        "L0_ffn_out_b": a["L0_ffn_out_b"],
        "L0_ffn_W_fxT": a["L0_ffn_W_fx"].T,
        "L0_ffn_b_fx": a["L0_ffn_b_fx"],
        "L0_ffn_hy_in_wT": a["L0_ffn_hy_in_w"].T,
        "conv_w": channel_chunks(a["L0_ffn_hy_conv_w"]),
        "conv_b": channel_chunks(a["L0_ffn_hy_conv_b"][:, None])[:, :, 0],
        "L0_ffn_hy_dt_bias": a["L0_ffn_hy_dt_bias"],
        "L0_ffn_hy_A_log": a["L0_ffn_hy_A_log"],
        "L0_ffn_hy_D": a["L0_ffn_hy_D"],
        "L0_ffn_hy_fcD_wT": a["L0_ffn_hy_fcD_w"].reshape(H, 4, P).transpose(2, 1, 0),
        "L0_ffn_hy_norm_w": a["L0_ffn_hy_norm_w"],
        "L0_ffn_hy_out_wT": a["L0_ffn_hy_out_w"].T,
        "L0_ffn_out_wT": a["L0_ffn_out_w"].T,
        "L1_gnn_a": a["L1_gnn_a"].reshape(2, F).T,
        "L1_gnn_temp": a["L1_gnn_temp"],
        "L1_gnn_h0": a["L1_gnn_h0"],
        "L1_ffn_bo": a["L1_ffn_bo"],
        "L1_ffn_route_id": a["L1_ffn_route_id"],
        "L1_ffn_WiT": a["L1_ffn_Wi"].T,
        "L1_ffn_bi": a["L1_ffn_bi"].reshape(KH, P).T,
        "L1_ffn_WrT": with_bias(a["L1_ffn_Wr"], a["L1_ffn_br"]).reshape(P, 2, KH * NE * (HID + 1)),
        "L1_ffn_WsT": with_bias(a["L1_ffn_Ws"], a["L1_ffn_bs"])[:, :, :, 0, :],
        "L1_ffn_WoT": a["L1_ffn_Wo"].T,
    }


def kernel(**inputs):
    import concourse.bacc as _bacc
    from concourse import mybir as _mybir
    from concourse.bass_utils import run_bass_kernel_spmd as _run

    nc = _bacc.Bacc("TRN2", target_bir_lowering=False, num_devices=1)
    arrays, args = {}, {}
    for name, a in layouts(inputs).items():
        a = np.ascontiguousarray(a)
        arrays[f"in_{name}"] = a
        args[name] = nc.dram_tensor(f"in_{name}", a.shape, _mybir.dt.from_np(a.dtype), kind="ExternalInput").ap()
    out = nc.dram_tensor("out", (N, F), _mybir.dt.float32, kind="ExternalOutput").ap()
    program(nc, args, out)
    r = _run(nc, [arrays], core_ids=[0])
    return r.results[0]["out"]
```
